# Optimizing a Trainium2 kernel written in Bass

```python
import numpy as np
import jax
import jax.numpy as jnp

def _softmax(x, axis=-1):
    return jax.nn.softmax(x, axis=axis)

def _gelu(x):
    return jax.nn.gelu(x, approximate=True)

def _silu(x):
    return jax.nn.silu(x)

def _sigmoid(x):
    return jax.nn.sigmoid(x)

def _layernorm(x, axis=-1, eps=1e-05):
    m = jnp.mean(x, axis=axis, keepdims=True)
    v = jnp.var(x, axis=axis, keepdims=True)
    return (x - m) / jnp.sqrt(v + eps)

def _scatter_add(tgt, idx, src, axis=0):
    return tgt.at[idx].add(src)

def _segment_sum(src, seg, n):
    return jax.ops.segment_sum(src, seg, n)
kernel_name = 'mk_cond_resid_d4_seqx_r4_f61d52'

def setup_inputs(seed: int=0):
    np.random.seed(seed)
    _w = jnp.asarray

    def _rec_inputs():
        import jax
        import jax.numpy as jnp
        _rk = jax.random.key(seed)
        x = 7.22e-05 + 1 * jax.random.normal(jax.random.fold_in(_rk, 1), (8, 256, 512), jnp.float32)
        _lenS = 256 - jax.random.randint(jax.random.fold_in(_rk, 7), (8,), 0, max(1, 256 // 4) + 1, jnp.int32)
        _lenS2 = 256 - jax.random.randint(jax.random.fold_in(_rk, 8), (8,), 0, max(1, 256 // 4) + 1, jnp.int32)
        cond_2048 = jax.random.bernoulli(jax.random.fold_in(_rk, 11), 0.8975, (8, 512)).astype(jnp.float32)
        return (x, cond_2048)
    x, cond_2048 = _rec_inputs()

    def _L0_cond_setup():
        import jax, jax.numpy as jnp
        import numpy as np
        import math
        D_MODEL = 256
        NUM_HEAD = 16
        NEG_INF = -1e+30
        key = jax.random.key(seed)
        k_x, k_m, k_q, k_k, k_v = jax.random.split(key, 5)
        B, C, T = (4, D_MODEL, 512)
        x = jax.random.normal(k_x, (B, C, T), dtype=jnp.float32)
        mask = (jax.random.uniform(k_m, (B, T)) < 0.9).astype(jnp.float32)
        limit = math.sqrt(6.0 / (C + C))
        Wq = jax.random.uniform(k_q, (C, C), minval=-limit, maxval=limit, dtype=jnp.float32)
        Wk = jax.random.uniform(k_k, (C, C), minval=-limit, maxval=limit, dtype=jnp.float32)
        Wv = jax.random.uniform(k_v, (C, C), minval=-limit, maxval=limit, dtype=jnp.float32)
        b = jnp.zeros((1,), dtype=jnp.float32)
        return {'x': x, 'mask': mask, 'Wq': Wq, 'Wk': Wk, 'Wv': Wv, 'b': b}
    _L0_cond_all = _L0_cond_setup()
    _L0_cond_in = {k: v for k, v in _L0_cond_all.items() if k in ('Wq', 'Wk', 'Wv', 'b')}
    del _L0_cond_all

    def _L1_cond_setup():
        import jax, jax.numpy as jnp
        import numpy as np
        HEADS = 16
        EPS = 1e-06

        def _rms_norm(x, g):
            xf = x.astype(jnp.float32)
            y = xf * jax.lax.rsqrt(jnp.mean(xf * xf, axis=-1, keepdims=True) + EPS)
            return y.astype(x.dtype) * g
        key = jax.random.key(seed)
        ks = jax.random.split(key, 6)
        b, n, dim, emb_dim = (4, 512, 512, 512)
        d_head = dim // HEADS
        return {'x': jax.random.normal(ks[0], (b, n, dim), jnp.float32), 'emb': jax.random.normal(ks[1], (b, 1, emb_dim), jnp.float32), 'W_emb': jax.random.normal(ks[2], (emb_dim, 2 * dim), jnp.float32) * emb_dim ** (-0.5), 'b_emb': jnp.zeros((2 * dim,), jnp.float32), 'g_norm': jnp.ones((dim,), jnp.float32), 'W_qkv': jax.random.normal(ks[3], (dim, 3 * dim), jnp.float32) * dim ** (-0.5), 'g_q': jnp.ones((d_head,), jnp.float32), 'g_k': jnp.ones((d_head,), jnp.float32), 'W_out': jax.random.normal(ks[4], (dim, dim), jnp.float32) * dim ** (-0.5)}
    _L1_cond_all = _L1_cond_setup()
    _L1_cond_in = {k: v for k, v in _L1_cond_all.items() if k in ('W_emb', 'b_emb', 'g_norm', 'W_qkv', 'g_q', 'g_k', 'W_out')}
    del _L1_cond_all

    def _L2_cond_setup():
        import jax, jax.numpy as jnp
        import numpy as np
        B, T, D = (16, 128, 512)
        key = jax.random.key(seed)
        k0, k1, k2, k3 = jax.random.split(key, 4)
        scale = 1.0 / np.sqrt(D)
        return {'initial_state': jax.random.normal(k0, (B, D), jnp.float32), 'inputs': jax.random.normal(k1, (B, T, D), jnp.float32), 'W_ih': jax.random.normal(k2, (D, 3 * D), jnp.float32) * scale, 'W_hh': jax.random.normal(k3, (D, 3 * D), jnp.float32) * scale, 'b_ih': jnp.zeros((3 * D,), jnp.float32), 'b_hh': jnp.zeros((3 * D,), jnp.float32)}
    _L2_cond_all = _L2_cond_setup()
    _L2_cond_in = {k: v for k, v in _L2_cond_all.items() if k in ('W_ih', 'W_hh', 'b_ih', 'b_hh')}
    del _L2_cond_all

    def _L3_cond_setup():
        import jax, jax.numpy as jnp
        import numpy as np
        NUM_BLOCKS = 8
        NUM_LAYERS = 4
        EPS = 1e-06
        key = jax.random.key(seed)
        ks = jax.random.split(key, 6)
        B, S, H = (4, 1024, 512)
        inputs = jax.random.normal(ks[0], (B, S, H), dtype=jnp.float32)
        query_vectors = jax.random.normal(ks[1], (NUM_LAYERS, H), dtype=jnp.float32) * 0.01
        lim = float(np.sqrt(6.0 / (H + H)))
        Wk = jax.random.uniform(ks[2], (H, H), minval=-lim, maxval=lim, dtype=jnp.float32)
        Wo = jax.random.uniform(ks[3], (H, H), minval=-lim, maxval=lim, dtype=jnp.float32)
        rms_weight = jnp.ones((H,), dtype=jnp.float32)
        ln_gamma = jnp.ones((H,), dtype=jnp.float32)
        ln_beta = jnp.zeros((H,), dtype=jnp.float32)
        return {'inputs': inputs, 'layer_idx': 1, 'rms_weight': rms_weight, 'query_vectors': query_vectors, 'Wk': Wk, 'Wo': Wo, 'ln_gamma': ln_gamma, 'ln_beta': ln_beta}
    _L3_cond_all = _L3_cond_setup()
    _L3_cond_in = {k: v for k, v in _L3_cond_all.items() if k in ('rms_weight', 'Wk', 'Wo', 'ln_gamma', 'ln_beta')}
    del _L3_cond_all
    return {'x': x, 'cond_2048': cond_2048, 'L0_cond_Wq': _L0_cond_in['Wq'], 'L0_cond_Wk': _L0_cond_in['Wk'], 'L0_cond_Wv': _L0_cond_in['Wv'], 'L0_cond_b': _L0_cond_in['b'], 'L1_cond_W_emb': _L1_cond_in['W_emb'], 'L1_cond_b_emb': _L1_cond_in['b_emb'], 'L1_cond_g_norm': _L1_cond_in['g_norm'], 'L1_cond_W_qkv': _L1_cond_in['W_qkv'], 'L1_cond_g_q': _L1_cond_in['g_q'], 'L1_cond_g_k': _L1_cond_in['g_k'], 'L1_cond_W_out': _L1_cond_in['W_out'], 'L2_cond_W_ih': _L2_cond_in['W_ih'], 'L2_cond_W_hh': _L2_cond_in['W_hh'], 'L2_cond_b_ih': _L2_cond_in['b_ih'], 'L2_cond_b_hh': _L2_cond_in['b_hh'], 'L3_cond_rms_weight': _L3_cond_in['rms_weight'], 'L3_cond_Wk': _L3_cond_in['Wk'], 'L3_cond_Wo': _L3_cond_in['Wo'], 'L3_cond_ln_gamma': _L3_cond_in['ln_gamma'], 'L3_cond_ln_beta': _L3_cond_in['ln_beta']}

def reference(x, cond_2048, L0_cond_Wq, L0_cond_Wk, L0_cond_Wv, L0_cond_b, L1_cond_W_emb, L1_cond_b_emb, L1_cond_g_norm, L1_cond_W_qkv, L1_cond_g_q, L1_cond_g_k, L1_cond_W_out, L2_cond_W_ih, L2_cond_W_hh, L2_cond_b_ih, L2_cond_b_hh, L3_cond_rms_weight, L3_cond_Wk, L3_cond_Wo, L3_cond_ln_gamma, L3_cond_ln_beta):
    import jax
    import jax.numpy as jnp

    def _L0_cond_ref(x, mask, Wq, Wk, Wv, b):
        import jax, jax.numpy as jnp
        import numpy as np
        import math
        D_MODEL = 256
        NUM_HEAD = 16
        NEG_INF = -1e+30
        B, C, T = x.shape
        H = NUM_HEAD
        Dh = C // H

        def proj(W):
            y = jnp.einsum('oc,bct->bto', W, x)
            return y.reshape(B, T, H, Dh).transpose(0, 2, 1, 3)
        Q, K, V = (proj(Wq), proj(Wk), proj(Wv))
        att = jnp.einsum('bhqd,bhkd->bhqk', Q, K) * (1.0 / math.sqrt(Dh))
        att = att + b[0]
        m = mask[:, None, None, :]
        att = att * m + (1.0 - m) * NEG_INF
        att = jax.nn.softmax(att, axis=-1)
        y = jnp.einsum('bhqk,bhkd->bhqd', att, V)
        y = y.transpose(0, 2, 1, 3).reshape(B, T, C)
        return y.transpose(0, 2, 1)

    def _L1_cond_ref(x, emb, W_emb, b_emb, g_norm, W_qkv, g_q, g_k, W_out):
        import jax, jax.numpy as jnp
        import numpy as np
        HEADS = 16
        EPS = 1e-06

        def _rms_norm(x, g):
            xf = x.astype(jnp.float32)
            y = xf * jax.lax.rsqrt(jnp.mean(xf * xf, axis=-1, keepdims=True) + EPS)
            return y.astype(x.dtype) * g
        b, n, dim = x.shape
        h = HEADS
        d = dim // h
        scale_shift = emb @ W_emb + b_emb
        scale, shift = jnp.split(scale_shift, 2, axis=-1)
        xn = _rms_norm(x, g_norm) * (1.0 + scale) + shift
        qkv = xn @ W_qkv
        qkv = qkv.reshape(b, n, 3, h, d)
        q, k, v = jnp.moveaxis(qkv, 2, 0)
        q = jnp.swapaxes(q, 1, 2)
        k = jnp.swapaxes(k, 1, 2)
        v = jnp.swapaxes(v, 1, 2)
        q = _rms_norm(q, g_q)
        k = _rms_norm(k, g_k)
        logits = jnp.einsum('bhqd,bhkd->bhqk', q, k) * d ** (-0.5)
        attn = jax.nn.softmax(logits, axis=-1)
        o = jnp.einsum('bhqk,bhkd->bhqd', attn, v)
        o = jnp.swapaxes(o, 1, 2).reshape(b, n, dim)
        return o + o @ W_out

    def _L2_cond_ref(initial_state, inputs, W_ih, W_hh, b_ih, b_hh):
        import jax, jax.numpy as jnp
        import numpy as np
        B, T, D = (16, 128, 512)
        "ScanOverTime(GRU cell): sequential per-timestep module call with\n            dict-state passing; merge_dict_trees stacks the per-step\n            'state_predicted' tensors along axis=1 -> [B, T, D]."

        def cell(h, x):
            gi = x @ W_ih + b_ih
            gh = h @ W_hh + b_hh
            i_r, i_z, i_n = jnp.split(gi, 3, axis=-1)
            h_r, h_z, h_n = jnp.split(gh, 3, axis=-1)
            r = jax.nn.sigmoid(i_r + h_r)
            z = jax.nn.sigmoid(i_z + h_z)
            n = jnp.tanh(i_n + r * h_n)
            h_new = (1.0 - z) * n + z * h
            return (h_new, h_new)
        xs = jnp.swapaxes(inputs, 0, 1)
        _, hs = jax.lax.scan(cell, initial_state, xs)
        return jnp.swapaxes(hs, 0, 1)

    def _L3_cond_ref(inputs, layer_idx, rms_weight, query_vectors, Wk, Wo, ln_gamma, ln_beta):
        import jax, jax.numpy as jnp
        import numpy as np
        NUM_BLOCKS = 8
        NUM_LAYERS = 4
        EPS = 1e-06
        B, S, H = inputs.shape
        block_size = max(1, S // NUM_BLOCKS)
        n_blocks = S // block_size
        block_repr = inputs.reshape(B, n_blocks, block_size, H).sum(axis=2)
        keys = jnp.einsum('bnh,kh->bnk', block_repr, Wk)
        rms = jnp.sqrt(jnp.mean(keys * keys, axis=-1, keepdims=True) + EPS)
        keys = keys / rms * rms_weight
        q = query_vectors[layer_idx]
        scores = jnp.einsum('bnh,h->bn', keys, q)
        attn = jax.nn.softmax(scores, axis=-1)
        attended = jnp.einsum('bn,bnh->bh', attn, block_repr)
        attended = jnp.broadcast_to(attended[:, None, :], (B, S, H))
        proj = jnp.einsum('bsh,kh->bsk', attended, Wo)
        x = inputs + proj
        mu = jnp.mean(x, axis=-1, keepdims=True)
        var = jnp.mean((x - mu) ** 2, axis=-1, keepdims=True)
        out = (x - mu) / jnp.sqrt(var + EPS) * ln_gamma + ln_beta
        return out
    x = x + _L0_cond_ref(x, cond_2048, L0_cond_Wq, L0_cond_Wk, L0_cond_Wv, L0_cond_b)
    x = x + _L1_cond_ref(x, cond_2048[:, None, :], L1_cond_W_emb, L1_cond_b_emb, L1_cond_g_norm, L1_cond_W_qkv, L1_cond_g_q, L1_cond_g_k, L1_cond_W_out)
    x = x + _L2_cond_ref(cond_2048, x, L2_cond_W_ih, L2_cond_W_hh, L2_cond_b_ih, L2_cond_b_hh)
    x = x + _L3_cond_ref(x, 1, L3_cond_rms_weight, cond_2048, L3_cond_Wk, L3_cond_Wo, L3_cond_ln_gamma, L3_cond_ln_beta)
    return x

_drawn_inputs = setup_inputs


def setup_inputs(seed=0):
    import zlib

    import numpy as np

    out = dict(_drawn_inputs(seed))
    spreads = {'L1_cond_b_emb': (0.0, 0.1),
     'L1_cond_g_norm': (1.0, 0.2),
     'L1_cond_g_q': (1.0, 0.6),
     'L1_cond_g_k': (1.0, 0.6),
     'L2_cond_b_ih': (0.0, 0.1),
     'L2_cond_b_hh': (0.0, 0.422),
     'L3_cond_rms_weight': (1.0, 0.6),
     'L3_cond_ln_gamma': (1.0, 0.2),
     'L3_cond_ln_beta': (0.0, 0.1)}
    factors = {}
    for name, (base, spread) in spreads.items():
        noise = np.random.default_rng([zlib.crc32(name.encode()), seed]).standard_normal(out[name].shape)
        drawn = base * np.exp(spread * noise) if base else spread * noise
        out[name] = jnp.asarray(drawn.astype(out[name].dtype))
    for name, factor in factors.items():
        out[name] = (out[name] * factor).astype(out[name].dtype)
    return out
```

```python
from contextlib import ExitStack

import concourse.bass as bass
from concourse import mybir

F32 = mybir.dt.float32
F16 = mybir.dt.float16
ALU = mybir.AluOpType
ACT = mybir.ActivationFunctionType
AX = mybir.AxisListType

P = 128
B, N, D = 8, 256, 512
H = 16
DH0 = N // H
DH1 = D // H
NC, DC = N // P, D // P
G = H // 4
MC = 3 * DC
TB = 64
EPS = 1e-6

QS = 32.0
LOGIT0 = 1.0 / (QS * QS * DH0 ** 0.5)
LOGIT1 = 1.0 / (QS * QS * DH1 ** 0.5)
ROW = 4096.0
MASKED = 60000.0
HS = 2.0 ** 11
WS = 2.0 ** 10
GS = HS * WS


def build(nc, x, cond, Wq0, Wk0, Wv0, b0, W_emb, b_emb, g_norm, W_qkv, g_q, g_k, W_out,
          W_ih, W_hh, b_ih, b_hh, rms_w, Wk3, Wo3, gamma, beta, out):
    top = ExitStack()
    with top:
        def sem(name):
            return top.enter_context(nc.semaphore(name))

        def sb(ctx, name, shape, dt=F32):
            return ctx.enter_context(nc.sbuf_tensor(name, shape, dt))

        def scratch(name, shape, dt):
            return nc.dram_tensor(name, shape, dt, kind="Internal").ap()

        mask_rows = scratch("mask_rows", (B, 3, D), F16)
        parts0 = scratch("parts0", (4, H, DH0, D), F16)
        parts1 = scratch("parts1", (4, H, DH1, N), F16)
        score_col = scratch("score_col", (B, B), F32)

        pA, pB, pC, pD = [top.enter_context(nc.psum_tensor(f"bank_pair_{n}", [P, 2, 512], F32)) for n in "ABCD"]

        xT = sb(top, "xT", [P, DC, B, N])
        ident = sb(top, "ident", [P, P])
        condT = sb(top, "condT", [P, DC, B])

        attention(nc, sem, sb, x, cond, Wq0, Wk0, Wv0, b0, W_emb, b_emb, g_norm, W_qkv, g_q, g_k, W_out,
                  mask_rows, parts0, parts1, pA, pB, pC, pD, xT, ident, condT)
        recurrence(nc, sem, sb, W_ih, W_hh, b_ih, b_hh, pA, pB, pC, pD, xT, ident, condT)
        block_attention(nc, sem, sb, cond, rms_w, Wk3, Wo3, gamma, beta, score_col, out,
                        pA, pB, pC, pD, xT, ident)


def attention(nc, sem, sb, x, cond, Wq0, Wk0, Wv0, b0, W_emb, b_emb, g_norm, W_qkv, g_q, g_k, W_out,
              mask_rows, parts0, parts1, pA, pB, pC, pD, xT, ident, condT):
    with ExitStack() as ctx:
        def t(name, shape, dt=F32):
            return sb(ctx, name, shape, dt)

        W0T = t("W0T", [P, 3, NC, N])
        wqkv = t("wqkv", [P, DC, 3 * D])
        wout = t("wout", [P, DC, D])
        film_scale = t("film_scale", [P, DC, B])
        film_shift = t("film_shift", [P, DC, B])
        head_ones = t("head_ones", [P, P])
        ones32 = t("ones32", [P, 32])
        row_const = t("row_const", [P, P], F16)
        gq = t("gq", [P, 1])
        gk = t("gk", [P, 1])
        xs = t("xs", [P, NC, D])
        mask_bc = t("mask_bc", [P, D])
        parts = t("parts", [P, 4, NC, D], F16)
        part = [parts[:, n, :, :] for n in range(4)]
        q_hi, q_lo, k_hi, k_lo = part
        kf = t("kf", [P, NC, D])
        q_rep = t("q_rep", [P, H, D], F16)
        k_rep = t("k_rep", [P, H, D], F16)
        v_aug = t("v_aug", [P, DC, H, 32])
        probs = [t(f"probs{n}", [P, 4, D]) for n in range(2)]
        head_max = t("head_max", [P, H * DC])
        max_row = t("max_row", [H * DC, P], F16)
        sums = t("sums", [P, D])
        y_pad = [t(f"y_pad{n}", [P, D]) for n in range(2)]
        y = t("y", [P, NC, D])
        x1 = t("x1", [P, NC, D])
        sq_sum = t("sq_sum", [P, NC])
        rstd = t("rstd", [P, NC])
        xn = kf
        xnT = t("xnT", [P, DC, N])
        sq = [t(f"sq{n}", [P, N]) for n in range(2)]
        head_rstd = [t(f"head_rstd{n}", [P, N]) for n in range(2)]
        qn = [t(f"qn{n}", [P, N]) for n in range(2)]
        hi1 = parts[:, 0:2, :, :].rearrange("p a c (e n) -> p a (c e) n", e=2)
        lo1 = parts[:, 2:4, :, :].rearrange("p a c (e n) -> p a (c e) n", e=2)
        q1_rep = t("q1_rep", [P, H, N], F16)
        k1_rep = t("k1_rep", [P, H, N], F16)
        max1_rows = t("max1_rows", [P, H, N], F16)
        v1 = t("v1", [P, NC, D])
        head_max1 = t("head_max1", [P, H * NC])
        max1_row = t("max1_row", [H * NC, P], F16)
        inv_sum = t("inv_sum", [P, N])
        tick = t("tick", [P, 1])
        eps_d = t("eps_d", [P, 1])
        eps_h = t("eps_h", [P, 1])
        oT = t("oT", [P, DC, N])

        with ExitStack() as prep:
            w0 = [w[:, :].rearrange("p (c n) -> p c n", c=NC) for w in (y_pad[0], y_pad[1], sums)]
            cond_sb = mask_bc[0:B, :]
            rows = y[0:B, :, :].rearrange("p a b -> p (a b)").bitcast(F16)[:, 0:3 * D].rearrange("p (r d) -> p r d", r=3)
            wemb = [p[:, :, :] for p in probs]
            bemb_c = sb(prep, "bemb_c", [P, 2 * DC])
            gn_c = sb(prep, "gn_c", [P, DC])
            bcol = sb(prep, "bcol", [P, 1])
            bcol16 = sb(prep, "bcol16", [P, 1], F16)
            low_sel = sb(prep, "low_sel", [P, 1])
            brow = sb(prep, "brow", [P, 1])
            film = sb(prep, "film", [P, 2 * DC, B])

            c_cond, c_w0, c_emb, c_bias, c_vec, c_big = (sem(n) for n in ("c_cond", "c_w0", "c_emb", "c_bias", "c_vec", "c_big"))
            c_zero, c_fill, c_diag, c_rows, c_rows_out, c_gains = (sem(n) for n in ("c_zero", "c_fill", "c_diag", "c_rows", "c_rows_out", "c_gains"))
            c_w0t, c_w0t_out, c_condt, c_condt_out, c_film, c_film_out, c_b = (
                sem(n) for n in ("c_w0t", "c_w0t_out", "c_condt", "c_condt_out", "c_film", "c_film_out", "c_b"))
            block = prep.enter_context(nc.Block())

            @block.sync
            def _(sp):
                sp.dma_start(cond_sb, cond).then_inc(c_cond, 16)
                for n, w in enumerate((Wq0, Wk0, Wv0)):
                    sp.dma_start(w0[n], w.rearrange("(c p) n -> p c n", p=P)).then_inc(c_w0, 16)
                we = W_emb.rearrange("(c p) n -> p c n", p=P)
                for n in range(2):
                    sp.dma_start(wemb[n].rearrange("p a b -> p (a b)").rearrange("p (c n) -> p c n", c=2),
                                 we[:, 2 * n:2 * n + 2, :]).then_inc(c_emb, 16)
                sp.dma_start(wqkv[:, :, :], W_qkv.rearrange("(c p) n -> p c n", p=P)).then_inc(c_big, 16)
                sp.dma_start(wout[:, :, :], W_out.rearrange("(c p) n -> p c n", p=P)).then_inc(c_big, 16)
                sp.wait_ge(c_rows, 2)
                sp.dma_start(mask_rows, rows[:, :, :]).then_inc(c_rows_out, 16)
                sp.wait_ge(c_rows_out, 16)
                sp.wait_ge(c_big, 32)

            @block.scalar
            def _(act):
                nc.scalar.preload_act_table_set("natural_log_exp_and_others")

            @block.gpsimd
            def _(pool):
                pool.dma_start(bcol[65:66, :], b0.rearrange("(a n) -> a n", a=1)).then_inc(c_bias, 16)
                pool.dma_start(bcol[66:67, :], b0.rearrange("(a n) -> a n", a=1)).then_inc(c_bias, 16)
                pool.dma_start(bemb_c[:, :], b_emb.rearrange("(c p) -> p c", p=P), allow_slow_non_contiguous=True).then_inc(c_vec, 16)
                pool.dma_start(gn_c[:, :], g_norm.rearrange("(c p) -> p c", p=P), allow_slow_non_contiguous=True).then_inc(c_vec, 16)
                for j in range(4):
                    pool.dma_start(gq[32 * j:32 * j + 32, :], g_q.rearrange("(p a) -> p a", a=1)).then_inc(c_vec, 16)
                    pool.dma_start(gk[32 * j:32 * j + 32, :], g_k.rearrange("(p a) -> p a", a=1)).then_inc(c_vec, 16)
                pool.wait_ge(c_zero, 4)
                pool.affine_select(out=ident[:, :], in_=ident[:, :], compare_op=ALU.not_equal, fill=1.0,
                                   base=0, pattern=[[-1, P]], channel_multiplier=1).then_inc(c_diag, 1)
                pool.affine_select(out=low_sel[:, :], in_=low_sel[:, :], compare_op=ALU.not_equal, fill=1.0,
                                   base=-66, pattern=[[0, 1]], channel_multiplier=1).then_inc(c_diag, 1)
                pool.wait_ge(c_vec, 160)

            @block.vector
            def _(dve):
                for tile in (ident, head_ones, row_const, low_sel):
                    nc.vector.memset(tile[:, :], 0.0).then_inc(c_zero, 1)
                nc.vector.memset(q_rep[:, :, :].bitcast(F32), 0.0).then_inc(c_b, 1)
                nc.vector.memset(k_rep[:, :, :].bitcast(F32), 0.0).then_inc(c_b, 1)
                nc.vector.memset(max1_rows[:, :, :].bitcast(F32), 0.0).then_inc(c_fill, 1)
                nc.vector.memset(ones32[:, :], 1.0).then_inc(c_fill, 1)
                nc.vector.memset(eps_d[:, :], D * EPS).then_inc(c_fill, 1)
                nc.vector.memset(eps_h[:, :], DH1 * EPS).then_inc(c_fill, 1)
                nc.vector.memset(v_aug[:, :, :, :], 1.0).then_inc(c_fill, 1)
                dve.wait_ge(c_zero, 4)
                nc.vector.memset(row_const[0:1, :], ROW).then_inc(c_fill, 1)
                for j in range(4):
                    nc.vector.memset(head_ones[32 * j:32 * j + 32, 32 * j:32 * j + 32], 1.0).then_inc(c_fill, 1)
                dve.wait_ge(c_cond, 16)
                nc.vector.tensor_scalar(rows[:, 0, :], cond_sb[:, :], MASKED, -MASKED, ALU.mult, ALU.add).then_inc(c_rows, 1)
                nc.vector.tensor_copy(rows[:, 1:3, :], cond_sb[:, :].unsqueeze(1).broadcast_to([B, 2, D])).then_inc(c_rows, 1)
                dve.wait_ge(c_vec, 160)
                nc.vector.tensor_scalar(gq[:, :], gq[:, :], QS * DH1 ** 0.5, None, ALU.mult).then_inc(c_gains, 1)
                nc.vector.tensor_scalar(gk[:, :], gk[:, :], QS * DH1 ** 0.5, None, ALU.mult).then_inc(c_gains, 1)
                dve.wait_ge(c_b, 2)
                nc.vector.memset(k_rep[96:97, :, :], ROW).then_inc(c_b, 1)
                nc.vector.memset(bcol[64:65, :], ROW).then_inc(c_b, 1)
                dve.wait_ge(c_bias, 32)
                dve.wait_ge(c_b, 4)
                dve.wait_ge(c_diag, 2)
                nc.vector.tensor_copy(bcol16[64:67, :], bcol[64:67, :]).then_inc(c_b, 1)
                dve.wait_ge(c_b, 5)
                nc.vector.tensor_tensor(brow[64:67, :], bcol16[64:67, :], low_sel[64:67, :], ALU.mult).then_inc(c_b, 1)
                dve.wait_ge(c_b, 6)
                nc.vector.tensor_tensor(brow[64:67, :], bcol[64:67, :], brow[64:67, :], ALU.subtract).then_inc(c_b, 1)
                dve.wait_ge(c_b, 7)
                nc.vector.tensor_scalar(q_rep[64:67, :, :], q_rep[64:67, :, :], brow[64:67, 0:1], None, ALU.add).then_inc(c_b, 1)
                dve.wait_ge(c_w0t, 1)
                for n in range(3):
                    src = (pA, pA, pB)[n][:, n % 2, :].rearrange("p (c o) -> p c o", c=NC)
                    last = nc.vector.tensor_copy(W0T[:, n, :, :], src)
                last.then_inc(c_w0t_out, 1)
                dve.wait_ge(c_condt, 1)
                nc.vector.tensor_copy(condT[:, :, :], pC[:, 0, 0:DC * B].rearrange("p (c b) -> p c b", c=DC)).then_inc(c_condt_out, 1)
                dve.wait_ge(c_film, 1)
                nc.vector.tensor_tensor(film[:, :, :], pD[:, 0, 0:2 * DC * B].rearrange("p (c b) -> p c b", c=2 * DC),
                                        bemb_c[:, :].unsqueeze(2).broadcast_to([P, 2 * DC, B]), ALU.add).then_inc(c_film_out, 1)
                dve.wait_ge(c_film_out, 1)
                nc.vector.tensor_scalar(film_scale[:, :, :], film[:, 0:DC, :], 1.0, None, ALU.add).then_inc(c_film_out, 1)
                nc.vector.tensor_copy(film_shift[:, :, :], film[:, DC:, :]).then_inc(c_film_out, 1)
                dve.wait_ge(c_film_out, 3)
                nc.vector.tensor_tensor(film_scale[:, :, :], film_scale[:, :, :],
                                        gn_c[:, :].unsqueeze(2).broadcast_to([P, DC, B]), ALU.mult).then_inc(c_film_out, 1)

            @block.tensor
            def _(pe):
                pe.wait_ge(c_diag, 1)
                pe.wait_ge(c_w0, 48)
                for n in range(3):
                    for oc in range(NC):
                        for cc in range(NC):
                            last = nc.tensor.transpose((pA, pA, pB)[n][:, n % 2, cc * N + oc * P:cc * N + oc * P + P],
                                                       w0[n][:, oc, cc * P:cc * P + P], ident[:, :])
                last.then_inc(c_w0t, 1)
                pe.wait_ge(c_cond, 16)
                for c in range(DC):
                    last = nc.tensor.transpose(pC[:, 0, c * B:c * B + B], cond_sb[:, c * P:c * P + P], ident[0:B, 0:B])
                last.then_inc(c_condt, 1)
                pe.wait_ge(c_condt_out, 1)
                pe.wait_ge(c_emb, 32)
                for m in range(2 * DC):
                    for k in range(DC):
                        w = wemb[k // 2].rearrange("p a b -> p (a b)").rearrange("p (c n) -> p c n", c=2)
                        last = nc.tensor.matmul(pD[:, 0, m * B:m * B + B], w[:, k % 2, m * P:m * P + P], condT[:, k, :],
                                                start=(m == 0 and k == 0), stop=(k == DC - 1), skip_group_check=True)
                last.then_inc(c_film, 1)

        ld_x, ld_mask, ld_rows, st_parts, ld_rep, ld_max = (
            sem(n) for n in ("ld_x", "ld_mask", "ld_rows", "st_parts", "ld_rep", "ld_max"))
        ld_y = [sem(f"ld_y{n}") for n in range(2)]
        q_ps, k_ps, v_ps, q_hi_ok, q_lo_ok, kf_ok, k_hi_ok, k_lo_ok, v_ok = (
            sem(n) for n in ("q_ps", "k_ps", "v_ps", "q_hi_ok", "q_lo_ok", "kf_ok", "k_hi_ok", "k_lo_ok", "v_ok"))
        s_ps, s_max, neg_max, max_ps, max_ok, st_ps, exp_ok, pv_ps, sums_ok, y_ok, x1_ok = (
            sem(n) for n in ("s_ps", "s_max", "neg_max", "max_ps", "max_ok", "st_ps", "exp_ok", "pv_ps", "sums_ok", "y_ok", "x1_ok"))
        ss_ok, sse_ok, log_ok, hln_ok, rstd_ok, xn_ok, xnT_ps, xnT_ok, qk_ps, sq_ok, hss_ps, hrs_ok, qn_ok, hi_ok, lo_ok, v1_ps, v1_ok = (
            sem(n) for n in ("ss_ok", "sse_ok", "log_ok", "hln_ok", "rstd_ok", "xn_ok", "xnT_ps", "xnT_ok", "qk_ps", "sq_ok", "hss_ps", "hrs_ok", "qn_ok",
                             "hi_ok", "lo_ok", "v1_ps", "v1_ok"))
        st_parts1, ld_rep1, s1_ps, s1_max, neg_max1, max1_ps, max1_ok, ld_max1, st1_ps, exp1_ok, pv1_ps, inv_ok, inv1_ok, log1_ok, oT_ok, res_ps, xT_ok = (
            sem(n) for n in ("st_parts1", "ld_rep1", "s1_ps", "s1_max", "neg_max1", "max1_ps", "max1_ok", "ld_max1", "st1_ps",
                             "exp1_ok", "pv1_ps", "inv_ok", "inv1_ok", "log1_ok", "oT_ok", "res_ps", "xT_ok"))
        ticked = sem("ticked")
        block = ctx.enter_context(nc.Block())
        pair = [pA, pB]
        U0 = 2 * H
        U1 = H // 2

        @block.sync
        def _(sp):
            with sp.Fori(0, B) as i:
                sp.wait_ge(x1_ok, i)
                sp.dma_start(xs[:, :, :], x[bass.ds(i, 1), :, :].rearrange("o (c p) d -> p (o c) d", p=P)).then_inc(ld_x, 16)
                sp.wait_ge(kf_ok, i)
                sp.dma_start(mask_bc[:, :], cond[bass.ds(i, 1), :].broadcast_to([P, D])).then_inc(ld_mask, 16)
                sp.wait_ge(st_ps, U0 * i)
                sp.dma_start(k_rep[64:67, :, :], mask_rows[bass.ds(i, 1), :, :].rearrange("o r t -> (o r) t").unsqueeze(1)
                             .broadcast_to([3, H, D])).then_inc(ld_rows, 16)
                for n, ready in enumerate((q_hi_ok, q_lo_ok, k_hi_ok, k_lo_ok)):
                    sp.wait_ge(ready, i + 1)
                    sp.dma_start(parts0[n].rearrange("(c h) d t -> (h d) c t", c=2), part[n][:, :, :]).then_inc(st_parts, 16)
                sp.wait_ge(st_parts, 64 * i + 64)
                for n, row in ((0, 0), (0, 32), (1, 16), (1, 48)):
                    sp.dma_start(q_rep[row:row + DH0, :, :], parts0[n].rearrange("h d t -> d h t")).then_inc(ld_rep, 16)
                for n, row in ((2, 0), (2, 16), (3, 32), (3, 48)):
                    sp.dma_start(k_rep[row:row + DH0, :, :], parts0[n].rearrange("h d t -> d h t")).then_inc(ld_rep, 16)
                sp.wait_ge(max_ok, i + 1)
                sp.dma_start(q_rep[96:97, :, :].rearrange("o h (c t) -> o (h c) t", c=DC), max_row[:, :]).then_inc(ld_max, 16)
                for g in range(G):
                    sp.wait_ge(y_ok, G * i + g + 1)
                    for j in range(4):
                        r = (4 * g + j) * DH0
                        sp.dma_start(y[r % P:r % P + DH0, r // P, :], y_pad[g % 2][32 * j:32 * j + DH0, :]).then_inc(ld_y[g % 2], 16)
                sp.wait_ge(hi_ok, 8 * i + 8)
                sp.wait_ge(lo_ok, 8 * i + 8)
                for n in range(2):
                    for m, tile in enumerate((hi1, lo1)):
                        sp.dma_start(parts1[2 * n + m].rearrange("(c h) d t -> (h d) c t", c=DC), tile[:, n, :, :]).then_inc(st_parts1, 16)
                sp.wait_ge(st_parts1, 64 * i + 64)
                for n, row in ((0, 0), (0, 64), (1, 32), (1, 96)):
                    sp.dma_start(q1_rep[row:row + DH1, :, :], parts1[n].rearrange("h d t -> d h t")).then_inc(ld_rep1, 16)
                for n, row in ((2, 0), (2, 32), (3, 64), (3, 96)):
                    sp.dma_start(k1_rep[row:row + DH1, :, :], parts1[n].rearrange("h d t -> d h t")).then_inc(ld_rep1, 16)
                sp.wait_ge(max1_ok, i + 1)
                sp.dma_start(max1_rows[0:1, :, :].rearrange("o h (c t) -> o (h c) t", c=NC), max1_row[:, :]).then_inc(ld_max1, 16)

        @block.tensor
        def _(pe):
            with pe.Fori(0, B) as i:
                pe.wait_ge(ld_x, 16 * i + 16)
                pe.wait_ge(xT_ok, i)
                for n, (bank, done) in enumerate(((pA, q_ps), (pB, k_ps))):
                    for oc in range(NC):
                        for c in range(NC):
                            last = nc.tensor.matmul(bank[:, oc, :], W0T[:, n, c, oc * P:oc * P + P], xs[:, c, :],
                                                    start=(c == 0), stop=(c == NC - 1))
                    last.then_inc(done, 1)
                for tc in range(DC):
                    for c in range(NC):
                        last = nc.tensor.matmul(pC[:, tc // 2, (tc % 2) * N:(tc % 2) * N + N], xs[:, c, tc * P:tc * P + P],
                                                W0T[:, 2, c, :], start=(tc % 2 == 0 and c == 0), stop=(c == NC - 1),
                                                skip_group_check=True)
                last.then_inc(v_ps, 1)
                pe.wait_ge(ld_rep, 128 * i + 128)
                pe.wait_ge(ld_rows, 16 * i + 16)
                pe.wait_ge(q_lo_ok, i + 1)
                pe.wait_ge(kf_ok, i + 1)
                for u in range(U0):
                    if u >= 2:
                        pe.wait_ge(s_max, U0 * i + u - 1)
                    for qc in range(2):
                        t0 = (2 * (u % 2) + qc) * P
                        last = nc.tensor.matmul(pair[u % 2][:, qc, :], q_rep[0:96, u // 2, t0:t0 + P], k_rep[0:96, u // 2, :],
                                                start=True, stop=True)
                    last.then_inc(s_ps, 1)
                pe.wait_ge(neg_max, i + 1)
                nc.tensor.matmul(pD[0:H * DC, 0, 0:P], head_max[:, :], ident[:, :], start=True, stop=True).then_inc(max_ps, 1)
                pe.wait_ge(ld_max, 16 * i + 16)
                pe.wait_ge(v_ok, i + 1)

                def weigh(n):
                    g, kc = n // DC, n % DC
                    pe.wait_ge(exp_ok, U0 * i + 2 * n + 2)
                    if kc == 0 and g >= 2:
                        pe.wait_ge(y_ok, G * i + g - 1)
                    for j in range(4):
                        last = nc.tensor.matmul(pC[32 * j:32 * j + 32, g % 2, :], v_aug[:, kc, 4 * g + j, :], probs[n % 2][:, j, :],
                                                start=(kc == 0), stop=(kc == DC - 1), skip_group_check=True)
                    last.then_inc(pv_ps, 1)

                for n in range(G * DC):
                    g, kc = n // DC, n % DC
                    for hf in range(2):
                        u = 2 * n + hf
                        if u >= 2:
                            pe.wait_ge(exp_ok, U0 * i + u - 1)
                        for j in range(2):
                            h = 4 * g + 2 * hf + j
                            last = nc.tensor.matmul(pair[u % 2][:, j, :], k_rep[:, h, kc * P:kc * P + P], q_rep[:, h, :],
                                                    start=True, stop=True)
                        last.then_inc(st_ps, 1)
                    if n >= 1:
                        weigh(n - 1)
                weigh(G * DC - 1)
                pe.wait_ge(xn_ok, 2 * i + 2)
                for c in range(DC):
                    for tc in range(NC):
                        last = nc.tensor.transpose(pA[:, c // 2, (c % 2) * N + tc * P:(c % 2) * N + tc * P + P],
                                                   xn[:, tc, c * P:c * P + P], ident[:, :])
                last.then_inc(xnT_ps, 1)
                pe.wait_ge(xnT_ok, DC * i + DC)

                def head_sums(m):
                    pe.wait_ge(sq_ok, 8 * i + m + 1)
                    if m >= 2:
                        pe.wait_ge(hrs_ok, 8 * i + m - 1)
                    nc.tensor.matmul(pD[:, m % 2, 0:N], head_ones[:, :], sq[m % 2][:, :], start=True, stop=True).then_inc(hss_ps, 1)

                pe.wait_ge(y_ok, G * i + G)
                pe.wait_ge(exp_ok, U0 * i + U0)
                for m in range(2 * DC):
                    if m >= 4:
                        pe.wait_ge(qn_ok, 8 * i + m - 3)
                    for c in range(DC):
                        last = nc.tensor.matmul((pB, pC)[(m % 4) // 2][:, m % 2, 0:N], wqkv[:, c, m * P:m * P + P], xnT[:, c, :],
                                                start=(c == 0), stop=(c == DC - 1))
                    last.then_inc(qk_ps, 1)
                    if m >= 1:
                        head_sums(m - 1)
                head_sums(2 * DC - 1)
                for tc in range(NC):
                    for c in range(DC):
                        last = nc.tensor.matmul(pA[:, tc, :], xnT[:, c, tc * P:tc * P + P], wqkv[:, c, 2 * D:3 * D],
                                                start=(c == 0), stop=(c == DC - 1))
                last.then_inc(v1_ps, 1)
                pe.wait_ge(ld_rep1, 128 * i + 128)
                pe.wait_ge(v1_ok, i + 1)
                pe.wait_ge(qn_ok, 8 * i + 8)
                for u in range(U1):
                    if u >= 2:
                        pe.wait_ge(s1_max, U1 * i + u - 1)
                    for j in range(2):
                        for qc in range(NC):
                            last = nc.tensor.matmul(pair[u % 2][:, j, qc * N:qc * N + N], q1_rep[:, 2 * u + j, qc * P:qc * P + P],
                                                    k1_rep[:, 2 * u + j, :], start=(qc == 0), stop=(qc == NC - 1),
                                                    skip_group_check=True)
                    last.then_inc(s1_ps, 1)
                pe.wait_ge(neg_max1, i + 1)
                pe.wait_ge(hrs_ok, 8 * i + 8)
                nc.tensor.matmul(pD[0:H * NC, 0, 0:P], head_max1[:, :], ident[:, :], start=True, stop=True).then_inc(max1_ps, 1)
                pe.wait_ge(ld_max1, 16 * i + 16)
                pe.wait_ge(max1_ok, i + 1)

                def weigh1(g):
                    pe.wait_ge(exp1_ok, U1 * i + 2 * g + 2)
                    if g >= 2:
                        pe.wait_ge(oT_ok, G * i + g - 1)
                    for bank, ones in ((pC, False), (pD, True)):
                        for kc in range(NC):
                            for j in range(4):
                                h = 4 * g + j
                                v = ones32[:, :] if ones else v1[:, kc, h * DH1:h * DH1 + DH1]
                                last = nc.tensor.matmul(bank[32 * j:32 * j + 32, g % 2, 0:N], v, probs[g % 2][:, j, kc * N:kc * N + N],
                                                        start=(kc == 0), stop=(kc == NC - 1), skip_group_check=True)
                    last.then_inc(pv1_ps, 1)

                for u in range(U1):
                    if u >= 2:
                        pe.wait_ge(exp1_ok, U1 * i + u - 1)
                    else:
                        pe.wait_ge(s1_max, U1 * i + U1)
                    for j in range(2):
                        for kc in range(NC):
                            o = pair[u % 2][:, j, kc * N:kc * N + N]
                            nc.tensor.matmul(o, k1_rep[:, 2 * u + j, kc * P:kc * P + P], q1_rep[:, 2 * u + j, :],
                                             start=(kc == 0), stop=False, skip_group_check=True)
                            last = nc.tensor.matmul(o, row_const[:, :], max1_rows[:, 2 * u + j, :], start=False, stop=True,
                                                    skip_group_check=True)
                    last.then_inc(st1_ps, 1)
                    if u % 2 == 1 and u >= 3:
                        weigh1(u // 2 - 1)
                weigh1(G - 1)
                pe.wait_ge(exp1_ok, U1 * i + U1)
                pe.wait_ge(oT_ok, G * i + G)
                for oc in range(DC):
                    o = pA[:, oc // 2, (oc % 2) * N:(oc % 2) * N + N]
                    for tc in range(NC):
                        nc.tensor.matmul(o[:, tc * P:tc * P + P], x1[:, tc, oc * P:oc * P + P], ident[:, :],
                                         start=(oc % 2 == 0 and tc == 0), stop=False, skip_group_check=True)
                    for c in range(DC):
                        last = nc.tensor.matmul(o, wout[:, c, oc * P:oc * P + P], oT[:, c, :], start=False, stop=(c == DC - 1),
                                                skip_group_check=True)
                last.then_inc(res_ps, 1)

        @block.scalar
        def _(act):
            with act.Fori(0, B) as i:
                act.wait_ge(st_parts1, 64 * i)
                act.wait_ge(q_ps, i + 1)
                nc.scalar.activation(q_hi[:, :, :], pA[:, :, :], ACT.Copy, scale=QS).then_inc(q_hi_ok, 1)
                act.wait_ge(v_ps, i + 1)
                nc.scalar.activation(v_aug[:, :, :, 0:DH0], pC[:, :, :].rearrange("p a (b h d) -> p (a b) h d", b=2, d=DH0),
                                     ACT.Copy).then_inc(v_ok, 1)
                act.wait_ge(kf_ok, i + 1)
                nc.scalar.activation(k_hi[:, :, :], kf[:, :, :], ACT.Copy).then_inc(k_hi_ok, 1)
                act.wait_ge(max_ps, i + 1)
                nc.scalar.activation(max_row[:, :], pD[0:H * DC, 0, 0:P], ACT.Copy).then_inc(max_ok, 1)
                def inverse(g):
                    act.wait_ge(sums_ok, G * i + g + 1)
                    nc.scalar.activation(sums[:, :], sums[:, :], ACT.Ln).then_inc(log_ok, 1)
                    act.wait_ge(log_ok, G * i + g + 1)
                    nc.scalar.activation(sums[:, :], sums[:, :], ACT.Exp, scale=-1.0).then_inc(inv_ok, 1)

                for n in range(G * DC):
                    for hf in range(2):
                        u = 2 * n + hf
                        act.wait_ge(st_ps, U0 * i + u + 1)
                        if n >= 2 and hf == 0:
                            act.wait_ge(pv_ps, G * DC * i + n - 1)
                        nc.scalar.activation(probs[n % 2][:, 2 * hf:2 * hf + 2, :], pair[u % 2][:, :, :], ACT.Exp,
                                             scale=LOGIT0).then_inc(exp_ok, 1)
                    if n % DC == 1 and n >= DC:
                        inverse(n // DC - 1)
                inverse(G - 1)
                act.wait_ge(x1_ok, i + 1)
                act.wait_ge(rstd_ok, i)
                act.wait_ge(xn_ok, 2 * i)
                for c in range(NC):
                    nc.scalar.activation(xn[:, c, :], x1[:, c, :], ACT.Square, accum_out=sq_sum[:, c:c + 1]).then_inc(ss_ok, 1)
                act.wait_ge(ss_ok, 2 * i + 2)
                nc.scalar.activation(rstd[:, :], sq_sum[:, :], ACT.Ln, bias=eps_d[:, 0:1]).then_inc(sse_ok, 1)
                act.wait_ge(sse_ok, i + 1)
                nc.scalar.activation(rstd[:, :], rstd[:, :], ACT.Exp, scale=-0.5).then_inc(rstd_ok, 1)
                act.wait_ge(st_parts, 64 * i + 64)

                def head_rms(m):
                    act.wait_ge(hss_ps, 8 * i + m + 1)
                    if m >= 2:
                        act.wait_ge(qn_ok, 8 * i + m - 1)
                    nc.scalar.activation(head_rstd[m % 2][:, :], pD[:, m % 2, 0:N], ACT.Ln, bias=eps_h[:, 0:1]).then_inc(hln_ok, 1)
                    act.wait_ge(hln_ok, 8 * i + m + 1)
                    nc.scalar.activation(head_rstd[m % 2][:, :], head_rstd[m % 2][:, :], ACT.Exp, scale=-0.5).then_inc(hrs_ok, 1)

                def hi_part(m):
                    act.wait_ge(qn_ok, 8 * i + m + 1)
                    nc.scalar.activation(hi1[:, m // DC, m % DC, :], qn[m % 2][:, :], ACT.Copy).then_inc(hi_ok, 1)

                for m in range(2 * DC):
                    act.wait_ge(qk_ps, 8 * i + m + 1)
                    if m >= 2:
                        act.wait_ge(hss_ps, 8 * i + m - 1)
                    nc.scalar.activation(sq[m % 2][:, :], (pB, pC)[(m % 4) // 2][:, m % 2, 0:N], ACT.Square).then_inc(sq_ok, 1)
                    if m >= 1:
                        head_rms(m - 1)
                    if m >= 2:
                        hi_part(m - 2)
                head_rms(2 * DC - 1)
                hi_part(2 * DC - 2)
                hi_part(2 * DC - 1)
                act.wait_ge(v1_ps, i + 1)
                nc.scalar.activation(v1[:, :, :], pA[:, :, :], ACT.Copy).then_inc(v1_ok, 1)
                act.wait_ge(max1_ps, i + 1)
                nc.scalar.activation(max1_row[:, :], pD[0:H * NC, 0, 0:P], ACT.Copy).then_inc(max1_ok, 1)
                act.wait_ge(pv_ps, G * DC * i + G * DC)

                def inverse1(g):
                    act.wait_ge(pv1_ps, G * i + g + 1)
                    act.wait_ge(oT_ok, G * i + g)
                    nc.scalar.activation(inv_sum[:, :], pD[:, g % 2, 0:N], ACT.Ln).then_inc(log1_ok, 1)
                    act.wait_ge(log1_ok, G * i + g + 1)
                    nc.scalar.activation(inv_sum[:, :], inv_sum[:, :], ACT.Exp, scale=-1.0).then_inc(inv1_ok, 1)

                for u in range(U1):
                    act.wait_ge(st1_ps, U1 * i + u + 1)
                    if u >= 4 and u % 2 == 0:
                        act.wait_ge(pv1_ps, G * i + u // 2 - 1)
                    nc.scalar.activation(probs[(u // 2) % 2][:, 2 * (u % 2):2 * (u % 2) + 2, :], pair[u % 2][:, :, :], ACT.Exp,
                                         scale=LOGIT1).then_inc(exp1_ok, 1)
                    if u % 2 and u >= 3:
                        inverse1(u // 2 - 1)
                inverse1(G - 1)

        @block.vector
        def _(dve):
            with dve.Fori(0, B) as i:
                dve.wait_ge(ld_mask, 16 * i + 16)
                dve.wait_ge(k_ps, i + 1)
                dve.wait_ge(ss_ok, 2 * i)
                for c in range(NC):
                    last = nc.vector.scalar_tensor_tensor(out=kf[:, c, :], in0=pB[:, c, :], scalar=QS, in1=mask_bc[:, :],
                                                          op0=ALU.mult, op1=ALU.mult)
                last.then_inc(kf_ok, 1)
                dve.wait_ge(st_parts1, 64 * i)
                dve.wait_ge(q_hi_ok, i + 1)
                nc.vector.scalar_tensor_tensor(out=q_lo[:, :, :], in0=pA[:, :, :], scalar=QS, in1=q_hi[:, :, :],
                                               op0=ALU.mult, op1=ALU.subtract).then_inc(q_lo_ok, 1)
                dve.wait_ge(kf_ok, i + 1)
                dve.wait_ge(k_hi_ok, i + 1)
                nc.vector.tensor_tensor(k_lo[:, :, :], kf[:, :, :], k_hi[:, :, :], ALU.subtract).then_inc(k_lo_ok, 1)
                dve.wait_ge(max_ps, i)
                for u in range(U0):
                    dve.wait_ge(s_ps, U0 * i + u + 1)
                    nc.vector.tensor_reduce(head_max[:, 2 * u:2 * u + 2], pair[u % 2][:, :, :], AX.X, ALU.max).then_inc(s_max, 1)
                dve.wait_ge(s_max, U0 * i + U0)
                nc.vector.tensor_scalar(head_max[:, :], head_max[:, :], -1.0 / ROW, None, ALU.mult).then_inc(neg_max, 1)
                for g in range(G):
                    dve.wait_ge(pv_ps, G * DC * i + DC * (g + 1))
                    if g >= 1:
                        dve.wait_ge(y_ok, G * i + g)
                    nc.vector.memset(tick[:, :], 0.0).then_inc(ticked, 1)
                    nc.vector.stream_shuffle(sums[:, :], pC[:, g % 2, :], [16 + n % 16 for n in range(32)]).then_inc(sums_ok, 1)
                    dve.wait_ge(inv_ok, G * i + g + 1)
                    if g >= 2:
                        dve.wait_ge(ld_y[g % 2], 128 * i + 64)
                    nc.vector.tensor_tensor(y_pad[g % 2][:, :], pC[:, g % 2, :], sums[:, :], ALU.mult).then_inc(y_ok, 1)
                dve.wait_ge(rstd_ok, i + 1)
                for c in range(NC):
                    nc.vector.tensor_scalar(xn[:, c, :], x1[:, c, :], rstd[:, c:c + 1], D ** 0.5, ALU.mult, ALU.mult).then_inc(xn_ok, 1)
                dve.wait_ge(xnT_ps, i + 1)
                for c in range(DC):
                    nc.vector.tensor_scalar(xnT[:, c, :], pA[:, c // 2, (c % 2) * N:(c % 2) * N + N],
                                            film_scale[:, c, bass.ds(i, 1)], film_shift[:, c, bass.ds(i, 1)],
                                            ALU.mult, ALU.add).then_inc(xnT_ok, 1)
                dve.wait_ge(st_parts, 64 * i + 64)

                def lo_part(m):
                    dve.wait_ge(hi_ok, 8 * i + m + 1)
                    nc.vector.tensor_tensor(lo1[:, m // DC, m % DC, :], qn[m % 2][:, :], hi1[:, m // DC, m % DC, :],
                                            ALU.subtract).then_inc(lo_ok, 1)

                for m in range(2 * DC):
                    dve.wait_ge(hrs_ok, 8 * i + m + 1)
                    if m >= 2:
                        dve.wait_ge(lo_ok, 8 * i + m - 1)
                    nc.vector.scalar_tensor_tensor(out=qn[m % 2][:, :], in0=(pB, pC)[(m % 4) // 2][:, m % 2, 0:N],
                                                   scalar=(gq if m < DC else gk)[:, 0:1], in1=head_rstd[m % 2][:, :],
                                                   op0=ALU.mult, op1=ALU.mult).then_inc(qn_ok, 1)
                    if m >= 1:
                        lo_part(m - 1)
                lo_part(2 * DC - 1)
                dve.wait_ge(max1_ps, i)
                for u in range(U1):
                    dve.wait_ge(s1_ps, U1 * i + u + 1)
                    nc.vector.tensor_reduce(head_max1[:, 4 * u:4 * u + 4], pair[u % 2][:, :, :].rearrange("p j (q k) -> p (j q) k", q=NC),
                                            AX.X, ALU.max).then_inc(s1_max, 1)
                dve.wait_ge(s1_max, U1 * i + U1)
                nc.vector.tensor_scalar(head_max1[:, :], head_max1[:, :], -1.0 / ROW, None, ALU.mult).then_inc(neg_max1, 1)
                for g in range(G):
                    dve.wait_ge(inv1_ok, G * i + g + 1)
                    nc.vector.tensor_tensor(oT[:, g, :], pC[:, g % 2, 0:N], inv_sum[:, :], ALU.mult).then_inc(oT_ok, 1)
                dve.wait_ge(res_ps, i + 1)
                dve.wait_ge(oT_ok, G * i + G)
                nc.vector.tensor_tensor(xT[:, :, bass.ds(i, 1), :].rearrange("p c o t -> p c (o t)"),
                                        pA[:, :, :].rearrange("p a (b t) -> p (a b) t", b=2), oT[:, :, :], ALU.add).then_inc(xT_ok, 1)

        @block.gpsimd
        def _(pool):
            with pool.Fori(0, B) as i:
                for n in range(2):
                    pool.wait_ge(ld_y[n], 128 * i + 128)
                pool.wait_ge(ld_x, 16 * i + 16)
                pool.wait_ge(res_ps, i)
                nc.gpsimd.tensor_tensor(x1[:, :, :], xs[:, :, :], y[:, :, :], ALU.add).then_inc(x1_ok, 1)


def recurrence(nc, sem, sb, W_ih, W_hh, b_ih, b_hh, pA, pB, pC, pD, xT, ident, condT):
    with ExitStack() as ctx:
        def t(name, shape, dt=F32):
            return sb(ctx, name, shape, dt)

        wih = t("wih", [P, DC, 3 * D])
        w_part = [t(f"whh_{n}", [P, DC, 3 * D], F16) for n in ("hi", "lo")]
        gi = t("gi", [P, TB, MC, B])
        bias_in = t("bias_in", [P, MC])
        bias_hn = t("bias_hn", [P, DC, B])
        state = [t(f"state{n}", [P, DC, B]) for n in range(2)]
        moving = t("moving", [P, DC, 2, B], F16)
        r_pre = t("r_pre", [P, DC, B])
        r_gate = t("r_gate", [P, DC, B])
        z_pre = t("z_pre", [P, DC, B])
        z_gate = t("z_gate", [P, DC, B])
        n_terms = t("n_terms", [P, DC, 3, B])
        n_pre = t("n_pre", [P, DC, B])
        cand = t("cand", [P, DC, B])
        diff = t("diff", [P, DC, B])
        z_diff = t("z_diff", [P, DC, B])
        unscaled = t("unscaled", [P, DC, B])
        unit = t("unit", [P, DC, B])
        whh = t("whh", [P, DC, 3 * D])
        bih_c = t("bih_c", [P, MC])
        bhh_c = t("bhh_c", [P, MC])

        w_ld, w_ld2, b_ld, w_hi, w_lo, b_ok, h_ok = (sem(n) for n in ("w_ld", "w_ld2", "b_ld", "w_hi", "w_lo", "b_ok", "h_ok"))
        gi_ps, gi_ok, unit_ok = sem("gi_ps"), sem("gi_ok"), sem("unit_ok")
        inj, r_ps, n_ps, z_ps, r_sum, z_sum, r_ok, z_ok, n_mul, n_in, n_sum, n_ok, d_ok, zd_ok, st_ok, hi_done, lo_done, h_un, x_add = (
            sem("gru_" + n) for n in ("inj", "r_ps", "n_ps", "z_ps", "r_sum", "z_sum", "r_ok", "z_ok", "n_mul", "n_in", "n_sum", "n_ok",
                                    "d_ok", "zd_ok", "st_ok", "hi_done", "lo_done", "h_un", "x_add"))
        block = ctx.enter_context(nc.Block())
        pR, pN, pZ = pA[:, 0, 0:64], pB[:, 0, 0:64], pC[:, 0, 0:64]
        pG = [pA[:, 1, :], pB[:, 1, :]]

        def gate(ps):
            return ps.rearrange("p (c s b) -> p c s b", c=DC, s=2)

        STEPS = TB // 2

        @block.sync
        def _(sp):
            sp.dma_start(wih[:, :, :], W_ih.rearrange("(c p) n -> p c n", p=P)).then_inc(w_ld, 16)
            sp.dma_start(whh[:, :, :], W_hh.rearrange("(c p) n -> p c n", p=P)).then_inc(w_ld2, 16)
            sp.dma_start(bih_c[:, :], b_ih.rearrange("(c p) -> p c", p=P), allow_slow_non_contiguous=True).then_inc(b_ld, 16)
            sp.dma_start(bhh_c[:, :], b_hh.rearrange("(c p) -> p c", p=P), allow_slow_non_contiguous=True).then_inc(b_ld, 16)

        @block.tensor
        def _(pe):
            pe.wait_ge(w_ld, 16)
            pe.wait_ge(w_lo, 1)
            with pe.Fori(0, N // TB) as blk:
                for m in range(MC):
                    if m >= 2:
                        pe.wait_ge(gi_ok, MC * blk + m - 1)
                    else:
                        pe.wait_ge(gi_ok, MC * blk)
                    for k in range(DC):
                        last = nc.tensor.matmul(pG[m % 2], wih[:, k, m * P:m * P + P], xT[:, k, :, bass.ts(blk, TB)],
                                                start=(k == 0), stop=(k == DC - 1))
                    last.then_inc(gi_ps, 1)
                with pe.Fori(0, STEPS) as s:
                    for par in range(2):
                        step = blk * TB + s * 2 + par
                        pe.wait_ge(b_ok, 5)
                        pe.wait_ge(gi_ok, MC * blk + MC)
                        pe.wait_ge(r_sum, step)
                        nc.tensor.matmul(gate(pR)[:, :, 0, :], ident[:, :], gi[:, bass.ds(s * 2 + par, 1), 0:DC, :].rearrange("p o c b -> p (o c) b"),
                                         start=True, stop=False, skip_group_check=True)
                        pe.wait_ge(n_mul, step)
                        nc.tensor.matmul(gate(pN)[:, :, 0, :], ident[:, :], bias_hn[:, :, :], start=True, stop=False, skip_group_check=True)
                        pe.wait_ge(z_sum, step)
                        nc.tensor.matmul(gate(pZ)[:, :, 0, :], ident[:, :],
                                         gi[:, bass.ds(s * 2 + par, 1), DC:2 * DC, :].rearrange("p o c b -> p (o c) b"),
                                         start=True, stop=False, skip_group_check=True)
                        pe.wait_ge(lo_done, step + 1)
                        for ps, first, done in ((pR, 0, r_ps), (pN, 2 * DC, n_ps), (pZ, DC, z_ps)):
                            for c in range(DC):
                                for k in range(DC):
                                    for w in w_part:
                                        last = nc.tensor.matmul(ps[:, c * 16:c * 16 + 16], w[:, k, (first + c) * P:(first + c) * P + P],
                                                                moving[:, k, :, :].rearrange("p s b -> p (s b)"), start=False,
                                                                stop=(k == DC - 1), skip_group_check=True)
                            last.then_inc(done, 1)

        @block.scalar
        def _(act):
            act.wait_ge(w_ld2, 16)
            nc.scalar.activation(w_part[0][:, :, :], whh[:, :, :], ACT.Copy, scale=WS).then_inc(w_hi, 1)
            act.wait_ge(b_ok, 5)
            with act.Fori(0, N // TB) as blk:
                act.wait_ge(n_sum, TB * blk)
                act.wait_ge(z_ps, TB * blk)
                for m in range(MC):
                    act.wait_ge(gi_ps, MC * blk + m + 1)
                    nc.scalar.activation(gi[:, :, m, :].rearrange("p t b -> p b t"), pG[m % 2].rearrange("p (b t) -> p b t", b=B),
                                         ACT.Identity, bias=bias_in[:, m:m + 1], scale=GS).then_inc(gi_ok, 1)
                with act.Fori(0, STEPS) as s:
                    for par in range(2):
                        step = blk * TB + s * 2 + par
                        act.wait_ge(r_sum, step + 1)
                        nc.scalar.activation(r_gate[:, :, :], r_pre[:, :, :], ACT.Sigmoid, scale=1.0 / GS).then_inc(r_ok, 1)
                        act.wait_ge(n_sum, step + 1)
                        nc.scalar.activation(cand[:, :, :], n_pre[:, :, :], ACT.Tanh, scale=1.0 / GS).then_inc(n_ok, 1)
                        act.wait_ge(z_sum, step + 1)
                        nc.scalar.activation(z_gate[:, :, :], z_pre[:, :, :], ACT.Sigmoid, scale=1.0 / GS).then_inc(z_ok, 1)

        @block.vector
        def _(dve):
            dve.wait_ge(w_hi, 1)
            for k in range(DC):
                last = nc.vector.scalar_tensor_tensor(out=w_part[1][:, k, :], in0=whh[:, k, :], scalar=WS, in1=w_part[0][:, k, :],
                                                      op0=ALU.mult, op1=ALU.subtract)
            last.then_inc(w_lo, 1)
            dve.wait_ge(b_ld, 32)
            nc.vector.tensor_tensor(bias_in[:, 0:2 * DC], bih_c[:, 0:2 * DC], bhh_c[:, 0:2 * DC], ALU.add).then_inc(b_ok, 1)
            nc.vector.tensor_copy(bias_in[:, 2 * DC:], bih_c[:, 2 * DC:]).then_inc(b_ok, 1)
            nc.vector.tensor_copy(bias_hn[:, :, :], bhh_c[:, 2 * DC:].unsqueeze(2).broadcast_to([P, DC, B])).then_inc(b_ok, 1)
            dve.wait_ge(b_ok, 3)
            nc.vector.tensor_scalar(bias_in[:, :], bias_in[:, :], GS, None, ALU.mult).then_inc(b_ok, 1)
            nc.vector.tensor_scalar(bias_hn[:, :, :], bias_hn[:, :, :], GS, None, ALU.mult).then_inc(b_ok, 1)
            nc.vector.tensor_scalar(state[1][:, :, :], condT[:, :, :], HS, None, ALU.mult).then_inc(h_ok, 1)
            nc.vector.tensor_scalar(moving[:, :, 0, :], condT[:, :, :], HS, None, ALU.mult).then_inc(hi_done, 1)
            dve.wait_ge(h_ok, 1)
            dve.wait_ge(hi_done, 1)
            nc.vector.tensor_tensor(moving[:, :, 1, :], state[1][:, :, :], moving[:, :, 0, :], ALU.subtract).then_inc(lo_done, 1)
            with dve.Fori(0, N // TB) as blk:
                with dve.Fori(0, STEPS) as s:
                    for par in range(2):
                        step = blk * TB + s * 2 + par
                        old, new = state[1 - par], state[par]
                        dve.wait_ge(r_ps, step + 1)
                        nc.vector.tensor_reduce(r_pre[:, :, :], gate(pR).rearrange("p c s b -> p c b s"), AX.X, ALU.add).then_inc(r_sum, 1)
                        dve.wait_ge(n_ps, step + 1)
                        dve.wait_ge(r_ok, step + 1)
                        nc.vector.tensor_tensor(n_terms[:, :, 0:2, :], gate(pN), r_gate[:, :, :].unsqueeze(2).broadcast_to([P, DC, 2, B]),
                                                ALU.mult).then_inc(n_mul, 1)
                        dve.wait_ge(n_mul, step + 1)
                        dve.wait_ge(n_in, step + 1)
                        nc.vector.tensor_reduce(n_pre[:, :, :], n_terms[:, :, :, :].rearrange("p c s b -> p c b s"), AX.X,
                                                ALU.add).then_inc(n_sum, 1)
                        dve.wait_ge(z_ps, step + 1)
                        nc.vector.tensor_reduce(z_pre[:, :, :], gate(pZ).rearrange("p c s b -> p c b s"), AX.X, ALU.add).then_inc(z_sum, 1)
                        dve.wait_ge(n_ok, step + 1)
                        nc.vector.scalar_tensor_tensor(out=diff[:, :, :], in0=cand[:, :, :], scalar=-HS, in1=old[:, :, :],
                                                       op0=ALU.mult, op1=ALU.add).then_inc(d_ok, 1)
                        dve.wait_ge(d_ok, step + 1)
                        dve.wait_ge(z_ok, step + 1)
                        nc.vector.tensor_tensor(z_diff[:, :, :], z_gate[:, :, :], diff[:, :, :], ALU.mult).then_inc(zd_ok, 1)
                        dve.wait_ge(zd_ok, step + 1)
                        nc.vector.scalar_tensor_tensor(out=moving[:, :, 0, :], in0=cand[:, :, :], scalar=HS, in1=z_diff[:, :, :],
                                                       op0=ALU.mult, op1=ALU.add).then_inc(hi_done, 1)
                        nc.vector.scalar_tensor_tensor(out=new[:, :, :], in0=cand[:, :, :], scalar=HS, in1=z_diff[:, :, :],
                                                       op0=ALU.mult, op1=ALU.add).then_inc(st_ok, 1)
                        dve.wait_ge(st_ok, step + 1)
                        dve.wait_ge(hi_done, step + 2)
                        dve.wait_ge(h_un, step)
                        nc.vector.tensor_tensor(moving[:, :, 1, :], new[:, :, :], moving[:, :, 0, :], ALU.subtract).then_inc(lo_done, 1)

        @block.gpsimd
        def _(pool):
            nc.gpsimd.memset(unit[:, :, :], 1.0 / HS).then_inc(unit_ok, 1)
            with pool.Fori(0, N // TB) as blk:
                with pool.Fori(0, STEPS) as s:
                    for par in range(2):
                        step = blk * TB + s * 2 + par
                        pool.wait_ge(unit_ok, 1)
                        pool.wait_ge(gi_ok, MC * blk + MC)
                        pool.wait_ge(n_sum, step)
                        nc.gpsimd.tensor_copy(n_terms[:, :, 2, :], gi[:, bass.ds(s * 2 + par, 1), 2 * DC:, :].rearrange("p o c b -> p (o c) b")).then_inc(n_in, 1)
                        pool.wait_ge(st_ok, step + 1)
                        pool.wait_ge(x_add, step)
                        nc.gpsimd.tensor_tensor(unscaled[:, :, :], state[par][:, :, :], unit[:, :, :], ALU.mult).then_inc(h_un, 1)
                        pool.wait_ge(h_un, step + 1)
                        xt = xT[:, :, :, bass.ds(step, 1)].rearrange("p c b o -> p c (b o)")
                        nc.gpsimd.tensor_tensor(xt, xt, unscaled[:, :, :], ALU.add).then_inc(x_add, 1)


def block_attention(nc, sem, sb, cond, rms_w, Wk3, Wo3, gamma, beta, score_col, out, pA, pB, pC, pD, xT, ident):
    NB = 8
    R = B * NB
    with ExitStack() as ctx:
        def t(name, shape, dt=F32):
            return sb(ctx, name, shape, dt)

        wk = t("wk", [P, DC, D])
        tick = t("tick3", [P, 1])
        wo = t("wo", [P, DC, D])
        wkT = t("wkT", [P, DC, D])
        woT = t("woT", [P, DC, D])
        gamma_bc = t("gamma_bc", [P, D])
        beta_bc = t("beta_bc", [P, D])
        query = t("query", [R, D])
        rms_bc = t("rms_bc", [R, D])
        ones_row = t("ones_row", [1, P])
        eps_d = t("eps_d3", [P, 1])
        eps_1 = t("eps_1", [P, 1])
        sumsT = t("sumsT", [P, DC, R])
        key_sq = t("key_sq", [R, D])
        key_q = t("key_q", [R, D])
        key_ss = t("key_ss", [R, 1])
        key_rstd = t("key_rstd", [R, 1])
        key_dot = t("key_dot", [R, 1])
        score = t("score", [R, 1])
        srow = t("srow", [1, B, NB])
        smax = t("smax", [1, B])
        sden = t("sden", [1, B])
        weighted = t("weighted", [P, DC, B, NB])
        attT = t("attT", [P, DC, B])
        projT = t("projT", [P, DC, B])
        xp = t("xp", [P, DC, B, N])
        stats = [t(f"stats{n}", [P, 6]) for n in range(2)]
        mv = [t(f"mv{n}", [P, 2]) for n in range(2)]
        ln_rstd = [t(f"ln_rstd{n}", [P, 1]) for n in range(2)]
        ln_shift = [t(f"ln_shift{n}", [P, 1]) for n in range(2)]
        ln = [t(f"ln{n}", [P, D]) for n in range(2)]
        ln_g = [t(f"ln_g{n}", [P, D]) for n in range(2)]
        ln_x = [t(f"ln_x{n}", [P, D]) for n in range(2)]
        res = [t(f"res{n}", [P, D]) for n in range(2)]

        ld, ones_ok, wT_ps, wT_ok, sums_ok, qw_ok, key_ps, sq_ok, dot_ok, rs_ok, sc_ok, sc_ps, sm, at_ps, wt_ok, att_ok, pj_ps, pj_ok, xp_ok = (
            sem("blk_" + n) for n in ("ld", "ones", "wT_ps", "wT_ok", "sums", "qw", "key_ps", "sq", "dot", "rs", "sc", "sc_ps", "sm", "at_ps",
                                    "wt", "att", "pj_ps", "pj", "xp"))
        y_ps, st_ok, mv_ok, rstd_ok, shift_ok, ln_ok, g_ok, x_ok, res_ok, stored = (
            sem("norm_" + n) for n in ("y_ps", "st", "mv", "rstd", "shift", "ln", "g", "x", "res", "stored"))
        ticked = sem("ticked3")
        block = ctx.enter_context(nc.Block())
        TILES = B * NC

        @block.sync
        def _(sp):
            sp.dma_start(wk[:, :, :], Wk3.rearrange("(c p) n -> p c n", p=P)).then_inc(ld, 16)
            sp.dma_start(wo[:, :, :], Wo3.rearrange("(c p) n -> p c n", p=P)).then_inc(ld, 16)
            sp.dma_start(query[:, :], cond[1:2, :].broadcast_to([R, D])).then_inc(ld, 16)
            sp.dma_start(rms_bc[:, :], rms_w.rearrange("(a n) -> a n", a=1).broadcast_to([R, D])).then_inc(ld, 16)
            sp.dma_start(gamma_bc[:, :], gamma.rearrange("(a n) -> a n", a=1).broadcast_to([P, D])).then_inc(ld, 16)
            sp.dma_start(beta_bc[:, :], beta.rearrange("(a n) -> a n", a=1).broadcast_to([P, D])).then_inc(ld, 16)
            with sp.Fori(0, B) as b:
                for c in range(NC):
                    sp.wait_ge(res_ok, NC * b + c + 1)
                    sp.dma_start(out[bass.ds(b, 1), c * P:c * P + P, :].rearrange("o p d -> (o p) d"), res[c][:, :]).then_inc(stored, 16)
            sp.wait_ge(stored, 16 * TILES)

        @block.tensor
        def _(pe):
            pe.wait_ge(ld, 96)
            for n, w in enumerate((wk, wo)):
                for kc in range(DC):
                    if n or kc >= 2:
                        pe.wait_ge(wT_ok, DC * n + kc - 1)
                    for hc in range(DC):
                        last = nc.tensor.transpose(pA[:, kc % 2, hc * P:hc * P + P], w[:, kc, hc * P:hc * P + P], ident[:, :])
                    last.then_inc(wT_ps, 1)
            pe.wait_ge(wT_ok, 2 * DC)
            pe.wait_ge(sums_ok, DC)
            for c in range(DC):
                last = nc.tensor.matmul(pB[0:R, 0, :], sumsT[:, c, :], wkT[:, c, :], start=(c == 0), stop=(c == DC - 1))
            last.then_inc(key_ps, 1)
            pe.wait_ge(sc_ok, 1)
            nc.tensor.transpose(pC[0:1, 0, 0:R], score[:, :], ident[0:R, 0:R]).then_inc(sc_ps, 1)
            pe.wait_ge(sm, 6)
            pe.wait_ge(ones_ok, 3)
            nc.tensor.matmul(pD[:, 0, 0:R], ones_row[:, :], srow[:, :, :].rearrange("o b n -> o (b n)"), start=True, stop=True).then_inc(at_ps, 1)
            pe.wait_ge(att_ok, 1)
            for kc in range(DC):
                for c in range(DC):
                    last = nc.tensor.matmul(pC[:, 1, kc * B:kc * B + B], woT[:, c, kc * P:kc * P + P], attT[:, c, :],
                                            start=(kc == 0 and c == 0), stop=(c == DC - 1), skip_group_check=True)
            last.then_inc(pj_ps, 1)
            pe.wait_ge(xp_ok, B * DC)
            for b in range(B):
                for tc in range(NC):
                    if b >= 1:
                        pe.wait_ge(x_ok, NC * (b - 1) + tc + 1)
                    for bank, src in ((pA, xp), (pB, xT)):
                        for c in range(DC):
                            last = nc.tensor.matmul(bank[:, tc, c * P:c * P + P], src[:, c, b, tc * P:tc * P + P], ident[:, :],
                                                    start=(c == 0), stop=(c == DC - 1), skip_group_check=True)
                    last.then_inc(y_ps, 1)

        @block.scalar
        def _(act):
            act.wait_ge(key_ps, 1)
            nc.scalar.activation(key_sq[:, :], pB[0:R, 0, :], ACT.Square, accum_out=key_ss[:, :]).then_inc(sq_ok, 1)
            act.wait_ge(sq_ok, 1)
            act.wait_ge(ones_ok, 3)
            nc.scalar.activation(key_rstd[:, :], key_ss[:, :], ACT.Ln, bias=eps_d[0:R, 0:1]).then_inc(rs_ok, 1)
            act.wait_ge(rs_ok, 1)
            nc.scalar.activation(key_rstd[:, :], key_rstd[:, :], ACT.Exp, scale=-0.5).then_inc(rs_ok, 1)
            act.wait_ge(sm, 2)
            nc.scalar.activation(srow[:, :, :], srow[:, :, :], ACT.Exp).then_inc(sm, 1)
            with act.Fori(0, B) as b:
                for tc in range(NC):
                    act.wait_ge(mv_ok, NC * b + tc + 1)
                    nc.scalar.activation(ln_rstd[tc][:, :], mv[tc][:, 1:2], ACT.Ln, bias=eps_1[:, 0:1]).then_inc(rstd_ok, 1)
                    act.wait_ge(rstd_ok, 2 * (NC * b + tc) + 1)
                    nc.scalar.activation(ln_rstd[tc][:, :], ln_rstd[tc][:, :], ACT.Exp, scale=-0.5).then_inc(rstd_ok, 1)
                    act.wait_ge(shift_ok, NC * b + tc + 1)
                    act.wait_ge(g_ok, NC * b)
                    nc.scalar.activation(ln[tc][:, :], pA[:, tc, :], ACT.Identity, bias=ln_shift[tc][:, 0:1],
                                         scale=ln_rstd[tc][:, 0:1]).then_inc(ln_ok, 1)

        @block.vector
        def _(dve):
            nc.vector.memset(ones_row[:, :], 1.0).then_inc(ones_ok, 1)
            nc.vector.memset(eps_d[:, :], D * EPS).then_inc(ones_ok, 1)
            nc.vector.memset(eps_1[:, :], EPS).then_inc(ones_ok, 1)
            for c in range(DC):
                nc.vector.tensor_reduce(sumsT[:, c, :].rearrange("p (b n) -> p b n", b=B),
                                        xT[:, c, :, :].rearrange("p b (n t) -> p b n t", n=NB), AX.X, ALU.add).then_inc(sums_ok, 1)
            dve.wait_ge(ld, 96)
            nc.vector.tensor_tensor(query[:, :], query[:, :], rms_bc[:, :], ALU.mult).then_inc(qw_ok, 1)
            for n, w in enumerate((wkT, woT)):
                for kc in range(DC):
                    dve.wait_ge(wT_ps, DC * n + kc + 1)
                    nc.vector.tensor_copy(w[:, :, kc * P:kc * P + P], pA[:, kc % 2, :].rearrange("p (h k) -> p h k", h=DC)).then_inc(wT_ok, 1)
            dve.wait_ge(sq_ok, 1)
            dve.wait_ge(qw_ok, 1)
            nc.vector.tensor_tensor(key_q[:, :], pB[0:R, 0, :], query[:, :], ALU.mult).then_inc(dot_ok, 1)
            dve.wait_ge(dot_ok, 1)
            nc.vector.tensor_reduce(key_dot[:, :], key_q[:, :], AX.X, ALU.add).then_inc(dot_ok, 1)
            dve.wait_ge(dot_ok, 2)
            dve.wait_ge(rs_ok, 2)
            nc.vector.tensor_scalar(score[:, :], key_dot[:, :], key_rstd[:, 0:1], D ** 0.5, ALU.mult, ALU.mult).then_inc(sc_ok, 1)
            dve.wait_ge(sc_ps, 1)
            nc.vector.tensor_reduce(smax[:, :], pC[0:1, 0, 0:R].rearrange("o (b n) -> o b n", b=B), AX.X, ALU.max).then_inc(sm, 1)
            dve.wait_ge(sm, 1)
            nc.vector.tensor_tensor(srow[:, :, :], pC[0:1, 0, 0:R].rearrange("o (b n) -> o b n", b=B),
                                    smax[:, :].unsqueeze(2).broadcast_to([1, B, NB]), ALU.subtract).then_inc(sm, 1)
            dve.wait_ge(sm, 3)
            nc.vector.tensor_reduce(sden[:, :], srow[:, :, :], AX.X, ALU.add).then_inc(sm, 1)
            dve.wait_ge(sm, 4)
            nc.vector.reciprocal(sden[:, :], sden[:, :]).then_inc(sm, 1)
            dve.wait_ge(sm, 5)
            nc.vector.tensor_tensor(srow[:, :, :], srow[:, :, :], sden[:, :].unsqueeze(2).broadcast_to([1, B, NB]), ALU.mult).then_inc(sm, 1)
            dve.wait_ge(at_ps, 1)
            dve.wait_ge(sums_ok, DC)
            for c in range(DC):
                nc.vector.tensor_tensor(weighted[:, c, :, :].rearrange("p b n -> p (b n)"), sumsT[:, c, :], pD[:, 0, 0:R], ALU.mult).then_inc(wt_ok, 1)
            dve.wait_ge(wt_ok, DC)
            nc.vector.tensor_reduce(attT[:, :, :], weighted[:, :, :, :], AX.X, ALU.add).then_inc(att_ok, 1)
            dve.wait_ge(pj_ps, 1)
            nc.vector.tensor_copy(projT[:, :, :], pC[:, 1, 0:DC * B].rearrange("p (c b) -> p c b", c=DC)).then_inc(pj_ok, 1)
            dve.wait_ge(pj_ok, 1)
            for c in range(DC):
                for b in range(B):
                    nc.vector.tensor_scalar(xp[:, c, b, :], xT[:, c, b, :], projT[:, c, b:b + 1], None, ALU.add).then_inc(xp_ok, 1)
            with dve.Fori(0, B) as b:
                for tc in range(NC):
                    n = NC * b + tc
                    dve.wait_ge(y_ps, n + 1)
                    nc.vector.bn_stats(stats[tc][:, :], pA[:, tc, :]).then_inc(st_ok, 1)
                    dve.wait_ge(st_ok, n + 1)
                    nc.vector.memset(tick[:, :], 0.0).then_inc(ticked, 1)
                    nc.vector.bn_aggr(mv[tc][:, :], stats[tc][:, :]).then_inc(mv_ok, 1)
                    dve.wait_ge(rstd_ok, 2 * n + 2)
                    nc.vector.scalar_tensor_tensor(out=ln_shift[tc][:, :], in0=mv[tc][:, 0:1], scalar=-1.0, in1=ln_rstd[tc][:, :],
                                                   op0=ALU.mult, op1=ALU.mult).then_inc(shift_ok, 1)
                    dve.wait_ge(g_ok, n + 1)
                    dve.wait_ge(res_ok, NC * b)
                    nc.vector.tensor_tensor(ln_x[tc][:, :], pB[:, tc, :], ln_g[tc][:, :], ALU.add).then_inc(x_ok, 1)

        @block.gpsimd
        def _(pool):
            with pool.Fori(0, B) as b:
                for tc in range(NC):
                    n = NC * b + tc
                    pool.wait_ge(ln_ok, n + 1)
                    pool.wait_ge(x_ok, NC * b)
                    pool.wait_ge(ld, 96)
                    nc.gpsimd.tensor_tensor(ln_g[tc][:, :], ln[tc][:, :], gamma_bc[:, :], ALU.mult).then_inc(g_ok, 1)
                    pool.wait_ge(x_ok, n + 1)
                    pool.wait_ge(stored, 16 * NC * b)
                    nc.gpsimd.tensor_tensor(res[tc][:, :], ln_x[tc][:, :], beta_bc[:, :], ALU.add).then_inc(res_ok, 1)


_INS = ['x', 'cond_2048', 'L0_cond_Wq', 'L0_cond_Wk', 'L0_cond_Wv', 'L0_cond_b', 'L1_cond_W_emb', 'L1_cond_b_emb', 'L1_cond_g_norm',
        'L1_cond_W_qkv', 'L1_cond_g_q', 'L1_cond_g_k', 'L1_cond_W_out', 'L2_cond_W_ih', 'L2_cond_W_hh', 'L2_cond_b_ih', 'L2_cond_b_hh',
        'L3_cond_rms_weight', 'L3_cond_Wk', 'L3_cond_Wo', 'L3_cond_ln_gamma', 'L3_cond_ln_beta']


def kernel(**inputs):
    import numpy as _np
    import concourse.bacc as _bacc
    from concourse import mybir as _mybir
    from concourse.bass_utils import run_bass_kernel_spmd as _run

    nc = _bacc.Bacc("TRN2", target_bir_lowering=False, num_devices=1)
    arrays, args = {}, []
    for name in _INS:
        a = _np.ascontiguousarray(inputs[name])
        arrays[f"in_{name}_dram"] = a
        args.append(nc.dram_tensor(f"in_{name}_dram", a.shape, _mybir.dt.from_np(a.dtype), kind="ExternalInput").ap())
    args.append(nc.dram_tensor("out_0_dram", (B, N, D), F32, kind="ExternalOutput").ap())
    build(nc, *args)
    r = _run(nc, [arrays], core_ids=[0])
    return r.results[0]["out_0_dram"]
```

```python
from contextlib import ExitStack

import concourse.bass as bass
from concourse import mybir

F32 = mybir.dt.float32
F16 = mybir.dt.float16
ALU = mybir.AluOpType
ACT = mybir.ActivationFunctionType
AX = mybir.AxisListType

P = 128
B, N, D = 8, 256, 512
H = 16
DH0 = N // H
DH1 = D // H
NC, DC = N // P, D // P
G = H // 4
MC = 3 * DC
TB = 64
EPS = 1e-6

QS = 32.0
LOGIT0 = 1.0 / (QS * QS * DH0 ** 0.5)
LOGIT1 = 1.0 / (QS * QS * DH1 ** 0.5)
ROW = 4096.0
MASKED = 60000.0
HS = 2.0 ** 11
WS = 2.0 ** 10
GS = HS * WS
IS = 2.0 ** 6


def build(nc, x, cond, Wq0, Wk0, Wv0, b0, W_emb, b_emb, g_norm, W_qkv, g_q, g_k, W_out,
          W_ih, W_hh, b_ih, b_hh, rms_w, Wk3, Wo3, gamma, beta, out):
    top = ExitStack()
    with top:
        def sem(name):
            return top.enter_context(nc.semaphore(name))

        def sb(ctx, name, shape, dt=F32):
            return ctx.enter_context(nc.sbuf_tensor(name, shape, dt))

        def scratch(name, shape, dt):
            return nc.dram_tensor(name, shape, dt, kind="Internal").ap()

        mask_rows = scratch("mask_rows", (B, 3, D), F16)
        parts0 = scratch("parts0", (4, H, DH0, D), F16)
        parts1 = scratch("parts1", (4, H, DH1, N), F16)
        score_col = scratch("score_col", (B, B), F32)

        pA, pB, pC, pD = [top.enter_context(nc.psum_tensor(f"bank_pair_{n}", [P, 2, 512], F32)) for n in "ABCD"]

        xT = sb(top, "xT", [P, DC, B, N])
        ident = sb(top, "ident", [P, P])
        condT = sb(top, "condT", [P, DC, B])

        attention(nc, sem, sb, x, cond, Wq0, Wk0, Wv0, b0, W_emb, b_emb, g_norm, W_qkv, g_q, g_k, W_out,
                  mask_rows, parts0, parts1, pA, pB, pC, pD, xT, ident, condT)
        recurrence(nc, sem, sb, W_ih, W_hh, b_ih, b_hh, pA, pB, pC, pD, xT, ident, condT)
        block_attention(nc, sem, sb, cond, rms_w, Wk3, Wo3, gamma, beta, score_col, out,
                        pA, pB, pC, pD, xT, ident)


def attention(nc, sem, sb, x, cond, Wq0, Wk0, Wv0, b0, W_emb, b_emb, g_norm, W_qkv, g_q, g_k, W_out,
              mask_rows, parts0, parts1, pA, pB, pC, pD, xT, ident, condT):
    with ExitStack() as ctx:
        def t(name, shape, dt=F32):
            return sb(ctx, name, shape, dt)

        W0T = t("W0T", [P, 3, NC, N])
        wqkv = t("wqkv", [P, DC, 3 * D])
        wout = t("wout", [P, DC, D])
        film_scale = t("film_scale", [P, DC, B])
        film_shift = t("film_shift", [P, DC, B])
        head_ones = t("head_ones", [P, P])
        ones32 = t("ones32", [P, 32])
        row_const = t("row_const", [P, P], F16)
        gq = t("gq", [P, 1])
        gk = t("gk", [P, 1])
        xs = t("xs", [P, NC, D])
        mask_bc = t("mask_bc", [P, D])
        parts = t("parts", [P, 4, NC, D], F16)
        part = [parts[:, n, :, :] for n in range(4)]
        q_hi, q_lo, k_hi, k_lo = part
        y_pads = t("y_pads", [P, 2, D])
        y_pad = [y_pads[:, n, :] for n in range(2)]
        kf = y_pads
        q_rep = t("q_rep", [P, H, D], F16)
        k_rep = t("k_rep", [P, H, D], F16)
        v_aug = t("v_aug", [P, DC, H, 32])
        probs = [t(f"probs{n}", [P, 4, D]) for n in range(2)]
        head_max = t("head_max", [P, H * DC])
        max_row = t("max_row", [H * DC, P], F16)
        sums = t("sums", [P, D])
        y = t("y", [P, NC, D])
        x1 = t("x1", [P, NC, D])
        sq_sum = t("sq_sum", [P, NC])
        rstd = t("rstd", [P, NC])
        xn = t("xn", [P, NC, D])
        xnT = t("xnT", [P, DC, N])
        sq = [t(f"sq{n}", [P, N]) for n in range(2)]
        head_rstd = [t(f"head_rstd{n}", [P, N]) for n in range(2)]
        qn = [t(f"qn{n}", [P, N]) for n in range(2)]
        hi1 = parts[:, 0:2, :, :].rearrange("p a c (e n) -> p a (c e) n", e=2)
        lo1 = parts[:, 2:4, :, :].rearrange("p a c (e n) -> p a (c e) n", e=2)
        q1_rep = t("q1_rep", [P, H, N], F16)
        k1_rep = t("k1_rep", [P, H, N], F16)
        max1_rows = t("max1_rows", [P, H, N], F16)
        v1 = t("v1", [P, NC, D])
        head_max1 = t("head_max1", [P, H * NC])
        max1_row = t("max1_row", [H * NC, P], F16)
        inv_sum = t("inv_sum", [P, N])
        tick = t("tick", [P, 1])
        eps_d = t("eps_d", [P, 1])
        eps_h = t("eps_h", [P, 1])
        oT = t("oT", [P, DC, N])

        with ExitStack() as prep:
            w0 = [w[:, :].rearrange("p (c n) -> p c n", c=NC) for w in (y_pad[0], y_pad[1], sums)]
            cond_sb = mask_bc[0:B, :]
            rows = y[0:B, :, :].rearrange("p a b -> p (a b)").bitcast(F16)[:, 0:3 * D].rearrange("p (r d) -> p r d", r=3)
            wemb = [p[:, :, :] for p in probs]
            bemb_c = sb(prep, "bemb_c", [P, 2 * DC])
            gn_c = sb(prep, "gn_c", [P, DC])
            bcol = sb(prep, "bcol", [P, 1])
            bcol16 = sb(prep, "bcol16", [P, 1], F16)
            low_sel = sb(prep, "low_sel", [P, 1])
            brow = sb(prep, "brow", [P, 1])
            film = sb(prep, "film", [P, 2 * DC, B])

            c_cond, c_w0, c_emb, c_bias, c_vec, c_big = (sem(n) for n in ("c_cond", "c_w0", "c_emb", "c_bias", "c_vec", "c_big"))
            c_zero, c_fill, c_diag, c_rows, c_rows_out, c_gains = (sem(n) for n in ("c_zero", "c_fill", "c_diag", "c_rows", "c_rows_out", "c_gains"))
            c_w0t, c_w0t_out, c_condt, c_condt_out, c_film, c_film_out, c_b = (
                sem(n) for n in ("c_w0t", "c_w0t_out", "c_condt", "c_condt_out", "c_film", "c_film_out", "c_b"))
            block = prep.enter_context(nc.Block())

            @block.sync
            def _(sp):
                sp.dma_start(cond_sb, cond).then_inc(c_cond, 16)
                for n, w in enumerate((Wq0, Wk0, Wv0)):
                    sp.dma_start(w0[n], w.rearrange("(c p) n -> p c n", p=P)).then_inc(c_w0, 16)
                we = W_emb.rearrange("(c p) n -> p c n", p=P)
                for n in range(2):
                    sp.dma_start(wemb[n].rearrange("p a b -> p (a b)").rearrange("p (c n) -> p c n", c=2),
                                 we[:, 2 * n:2 * n + 2, :]).then_inc(c_emb, 16)
                sp.dma_start(wqkv[:, :, :], W_qkv.rearrange("(c p) n -> p c n", p=P)).then_inc(c_big, 16)
                sp.dma_start(wout[:, :, :], W_out.rearrange("(c p) n -> p c n", p=P)).then_inc(c_big, 16)
                sp.wait_ge(c_rows, 2)
                sp.dma_start(mask_rows, rows[:, :, :]).then_inc(c_rows_out, 16)
                sp.wait_ge(c_rows_out, 16)
                sp.wait_ge(c_big, 32)

            @block.scalar
            def _(act):
                nc.scalar.preload_act_table_set("natural_log_exp_and_others")

            @block.gpsimd
            def _(pool):
                pool.dma_start(bcol[65:66, :], b0.rearrange("(a n) -> a n", a=1)).then_inc(c_bias, 16)
                pool.dma_start(bcol[66:67, :], b0.rearrange("(a n) -> a n", a=1)).then_inc(c_bias, 16)
                pool.dma_start(bemb_c[:, :], b_emb.rearrange("(c p) -> p c", p=P), allow_slow_non_contiguous=True).then_inc(c_vec, 16)
                pool.dma_start(gn_c[:, :], g_norm.rearrange("(c p) -> p c", p=P), allow_slow_non_contiguous=True).then_inc(c_vec, 16)
                for j in range(4):
                    pool.dma_start(gq[32 * j:32 * j + 32, :], g_q.rearrange("(p a) -> p a", a=1)).then_inc(c_vec, 16)
                    pool.dma_start(gk[32 * j:32 * j + 32, :], g_k.rearrange("(p a) -> p a", a=1)).then_inc(c_vec, 16)
                pool.wait_ge(c_zero, 4)
                pool.affine_select(out=ident[:, :], in_=ident[:, :], compare_op=ALU.not_equal, fill=1.0,
                                   base=0, pattern=[[-1, P]], channel_multiplier=1).then_inc(c_diag, 1)
                pool.affine_select(out=low_sel[:, :], in_=low_sel[:, :], compare_op=ALU.not_equal, fill=1.0,
                                   base=-66, pattern=[[0, 1]], channel_multiplier=1).then_inc(c_diag, 1)
                pool.wait_ge(c_vec, 160)

            @block.vector
            def _(dve):
                for tile in (ident, head_ones, row_const, low_sel):
                    nc.vector.memset(tile[:, :], 0.0).then_inc(c_zero, 1)
                nc.vector.memset(q_rep[:, :, :].bitcast(F32), 0.0).then_inc(c_b, 1)
                nc.vector.memset(k_rep[:, :, :].bitcast(F32), 0.0).then_inc(c_b, 1)
                nc.vector.memset(max1_rows[:, :, :].bitcast(F32), 0.0).then_inc(c_fill, 1)
                nc.vector.memset(ones32[:, :], 1.0).then_inc(c_fill, 1)
                nc.vector.memset(eps_d[:, :], D * EPS).then_inc(c_fill, 1)
                nc.vector.memset(eps_h[:, :], DH1 * EPS).then_inc(c_fill, 1)
                nc.vector.memset(v_aug[:, :, :, :], 1.0).then_inc(c_fill, 1)
                dve.wait_ge(c_zero, 4)
                nc.vector.memset(row_const[0:1, :], ROW).then_inc(c_fill, 1)
                for j in range(4):
                    nc.vector.memset(head_ones[32 * j:32 * j + 32, 32 * j:32 * j + 32], 1.0).then_inc(c_fill, 1)
                dve.wait_ge(c_cond, 16)
                nc.vector.tensor_scalar(rows[:, 0, :], cond_sb[:, :], MASKED, -MASKED, ALU.mult, ALU.add).then_inc(c_rows, 1)
                nc.vector.tensor_copy(rows[:, 1:3, :], cond_sb[:, :].unsqueeze(1).broadcast_to([B, 2, D])).then_inc(c_rows, 1)
                dve.wait_ge(c_vec, 160)
                nc.vector.tensor_scalar(gq[:, :], gq[:, :], QS * DH1 ** 0.5, None, ALU.mult).then_inc(c_gains, 1)
                nc.vector.tensor_scalar(gk[:, :], gk[:, :], QS * DH1 ** 0.5, None, ALU.mult).then_inc(c_gains, 1)
                dve.wait_ge(c_b, 2)
                nc.vector.memset(k_rep[96:97, :, :], ROW).then_inc(c_b, 1)
                nc.vector.memset(bcol[64:65, :], ROW).then_inc(c_b, 1)
                dve.wait_ge(c_bias, 32)
                dve.wait_ge(c_b, 4)
                dve.wait_ge(c_diag, 2)
                nc.vector.tensor_copy(bcol16[64:67, :], bcol[64:67, :]).then_inc(c_b, 1)
                dve.wait_ge(c_b, 5)
                nc.vector.tensor_tensor(brow[64:67, :], bcol16[64:67, :], low_sel[64:67, :], ALU.mult).then_inc(c_b, 1)
                dve.wait_ge(c_b, 6)
                nc.vector.tensor_tensor(brow[64:67, :], bcol[64:67, :], brow[64:67, :], ALU.subtract).then_inc(c_b, 1)
                dve.wait_ge(c_b, 7)
                nc.vector.tensor_scalar(q_rep[64:67, :, :], q_rep[64:67, :, :], brow[64:67, 0:1], None, ALU.add).then_inc(c_b, 1)
                dve.wait_ge(c_w0t, 1)
                for n in range(3):
                    src = (pA, pA, pB)[n][:, n % 2, :].rearrange("p (c o) -> p c o", c=NC)
                    last = nc.vector.tensor_copy(W0T[:, n, :, :], src)
                last.then_inc(c_w0t_out, 1)
                dve.wait_ge(c_condt, 1)
                nc.vector.tensor_copy(condT[:, :, :], pC[:, 0, 0:DC * B].rearrange("p (c b) -> p c b", c=DC)).then_inc(c_condt_out, 1)
                dve.wait_ge(c_film, 1)
                nc.vector.tensor_tensor(film[:, :, :], pD[:, 0, 0:2 * DC * B].rearrange("p (c b) -> p c b", c=2 * DC),
                                        bemb_c[:, :].unsqueeze(2).broadcast_to([P, 2 * DC, B]), ALU.add).then_inc(c_film_out, 1)
                dve.wait_ge(c_film_out, 1)
                nc.vector.tensor_scalar(film_scale[:, :, :], film[:, 0:DC, :], 1.0, None, ALU.add).then_inc(c_film_out, 1)
                nc.vector.tensor_copy(film_shift[:, :, :], film[:, DC:, :]).then_inc(c_film_out, 1)
                dve.wait_ge(c_film_out, 3)
                nc.vector.tensor_tensor(film_scale[:, :, :], film_scale[:, :, :],
                                        gn_c[:, :].unsqueeze(2).broadcast_to([P, DC, B]), ALU.mult).then_inc(c_film_out, 1)

            @block.tensor
            def _(pe):
                pe.wait_ge(c_diag, 1)
                pe.wait_ge(c_w0, 48)
                for n in range(3):
                    for oc in range(NC):
                        for cc in range(NC):
                            last = nc.tensor.transpose((pA, pA, pB)[n][:, n % 2, cc * N + oc * P:cc * N + oc * P + P],
                                                       w0[n][:, oc, cc * P:cc * P + P], ident[:, :])
                last.then_inc(c_w0t, 1)
                pe.wait_ge(c_cond, 16)
                for c in range(DC):
                    last = nc.tensor.transpose(pC[:, 0, c * B:c * B + B], cond_sb[:, c * P:c * P + P], ident[0:B, 0:B])
                last.then_inc(c_condt, 1)
                pe.wait_ge(c_condt_out, 1)
                pe.wait_ge(c_emb, 32)
                for m in range(2 * DC):
                    for k in range(DC):
                        w = wemb[k // 2].rearrange("p a b -> p (a b)").rearrange("p (c n) -> p c n", c=2)
                        last = nc.tensor.matmul(pD[:, 0, m * B:m * B + B], w[:, k % 2, m * P:m * P + P], condT[:, k, :],
                                                start=(m == 0 and k == 0), stop=(k == DC - 1), skip_group_check=True)
                last.then_inc(c_film, 1)

        ld_x, ld_x1, ld_mask, ld_rows, st_parts, ld_rep, ld_max = (
            sem(n) for n in ("ld_x", "ld_x1", "ld_mask", "ld_rows", "st_parts", "ld_rep", "ld_max"))
        ld_y = [sem(f"ld_y{n}") for n in range(2)]
        q_ps, k_ps, v_ps, q_hi_ok, q_lo_ok, kf_ok, k_hi_ok, k_lo_ok, v_ok = (
            sem(n) for n in ("q_ps", "k_ps", "v_ps", "q_hi_ok", "q_lo_ok", "kf_ok", "k_hi_ok", "k_lo_ok", "v_ok"))
        s_ps, s_max, neg_max, max_ps, max_ok, st_ps, exp_ok, pv_ps, sums_ok, inv_ok, y_ok, x1_ok = (
            sem(n) for n in ("s_ps", "s_max", "neg_max", "max_ps", "max_ok", "st_ps", "exp_ok", "pv_ps", "sums_ok", "inv_ok", "y_ok", "x1_ok"))
        ss_ok, sse_ok, hln_ok, rstd_ok, xn_ok, xnT_ps, xnT_ok, qk_ps, sq_ok, hss_ps, hrs_ok, qn_ok, hi_ok, lo_ok, v1_ps, v1_ok = (
            sem(n) for n in ("ss_ok", "sse_ok", "hln_ok", "rstd_ok", "xn_ok", "xnT_ps", "xnT_ok", "qk_ps", "sq_ok", "hss_ps", "hrs_ok", "qn_ok",
                             "hi_ok", "lo_ok", "v1_ps", "v1_ok"))
        st_parts1, ld_rep1, s1_ps, s1_max, neg_max1, max1_ps, max1_ok, ld_max1, st1_ps, exp1_ok, pv1_ps, inv1_ok, log1_ok, oT_ok, res_ps, xT_ok = (
            sem(n) for n in ("st_parts1", "ld_rep1", "s1_ps", "s1_max", "neg_max1", "max1_ps", "max1_ok", "ld_max1", "st1_ps",
                             "exp1_ok", "pv1_ps", "inv1_ok", "log1_ok", "oT_ok", "res_ps", "xT_ok"))
        ticked = sem("ticked")
        block = ctx.enter_context(nc.Block())
        pair = [pA, pB]
        pair1 = [pC, pD]
        qk_bank = [pC[:, 0, :], pC[:, 1, :], pD[:, 1, :]]
        U0 = 2 * H
        U1 = H // 2
        M8 = 2 * DC

        def beside():
            free = iter(range(U0))
            for m in range(M8):
                yield "qk", m
                for _ in range(2 if m >= 4 else 0):
                    yield "max", next(free)
            yield "qk", M8
            for n in range(DC * NC):
                yield "v", n
                yield "max", next(free)
            for _ in range(6):
                yield "max", next(free)
            for u in range(U1):
                yield "max1", u
            yield "row1", 0
            for _ in range(4):
                yield "max", next(free)
            for h in range(H):
                yield "score1", h
                if h % 4 == 1:
                    yield "max", next(free)
                if h % 4 == 3 and h >= 7:
                    yield "weigh1", h // 4 - 1
                if h % 4 == 1 and h >= 9:
                    yield "out1", h // 4 - 2
            yield "weigh1", G - 1
            yield "out1", G - 2
            for u in free:
                yield "max", u
            yield "row", 0
            yield "out1", G - 1
        BESIDE = list(beside())
        ALONE0 = [("max", u) for u in range(U0)] + [("row", 0)]
        ALONE1 = [step for step in BESIDE if step[0] not in ("max", "row")]

        @block.sync
        def _(sp):
            def load_x(b, first=False):
                if not first:
                    sp.wait_ge(v_ps, b)
                sp.dma_start(xs[:, :, :], x[bass.ds(b, 1), :, :].rearrange("o (c p) d -> p (o c) d", p=P)).then_inc(ld_x, 16)
                if not first:
                    sp.wait_ge(kf_ok, b)
                sp.dma_start(mask_bc[:, :], cond[bass.ds(b, 1), :].broadcast_to([P, D])).then_inc(ld_mask, 16)

            def load_x1(b, first=False):
                if not first:
                    sp.wait_ge(res_ps, b)
                sp.dma_start(x1[:, :, :], x[bass.ds(b, 1), :, :].rearrange("o (c p) d -> p (o c) d", p=P)).then_inc(ld_x1, 16)

            def spread(b, first=False):
                if not first:
                    sp.wait_ge(st_ps, b * U0)
                sp.dma_start(k_rep[64:67, :, :], mask_rows[bass.ds(b, 1), :, :].rearrange("o r t -> (o r) t").unsqueeze(1)
                             .broadcast_to([3, H, D])).then_inc(ld_rows, 16)
                for n, ready in enumerate((q_hi_ok, q_lo_ok, k_hi_ok, k_lo_ok)):
                    sp.wait_ge(ready, b + 1)
                    sp.dma_start(parts0[n].rearrange("(c h) d t -> (h d) c t", c=2), part[n][:, :, :]).then_inc(st_parts, 16)
                sp.wait_ge(st_parts, b * 64 + 64)
                for n, row in ((0, 0), (0, 32), (1, 16), (1, 48)):
                    sp.dma_start(q_rep[row:row + DH0, :, :], parts0[n].rearrange("h d t -> d h t")).then_inc(ld_rep, 16)
                for n, row in ((2, 0), (2, 16), (3, 32), (3, 48)):
                    sp.dma_start(k_rep[row:row + DH0, :, :], parts0[n].rearrange("h d t -> d h t")).then_inc(ld_rep, 16)

            def place_max(b):
                sp.wait_ge(max_ok, b + 1)
                sp.dma_start(q_rep[96:97, :, :].rearrange("o h (c t) -> o (h c) t", c=DC), max_row[:, :]).then_inc(ld_max, 16)

            def move_y(b):
                for g in range(G):
                    sp.wait_ge(y_ok, b * G + g + 1)
                    for j in range(4):
                        r = (4 * g + j) * DH0
                        sp.dma_start(y[r % P:r % P + DH0, r // P, :], y_pad[g % 2][32 * j:32 * j + DH0, :]).then_inc(ld_y[g % 2], 16)

            def spread1(e):
                sp.wait_ge(hi_ok, e * M8 + M8)
                sp.wait_ge(lo_ok, e * M8 + M8)
                for n in range(2):
                    for m, tile in enumerate((hi1, lo1)):
                        sp.dma_start(parts1[2 * n + m].rearrange("(c h) d t -> (h d) c t", c=DC), tile[:, n, :, :]).then_inc(st_parts1, 16)
                sp.wait_ge(st_parts1, e * 64 + 64)
                for n, row in ((0, 0), (0, 64), (1, 32), (1, 96)):
                    sp.dma_start(q1_rep[row:row + DH1, :, :], parts1[n].rearrange("h d t -> d h t")).then_inc(ld_rep1, 16)
                for n, row in ((2, 0), (2, 32), (3, 64), (3, 96)):
                    sp.dma_start(k1_rep[row:row + DH1, :, :], parts1[n].rearrange("h d t -> d h t")).then_inc(ld_rep1, 16)
                sp.wait_ge(max1_ok, e + 1)
                sp.dma_start(max1_rows[0:1, :, :].rearrange("o h (c t) -> o (h c) t", c=NC), max1_row[:, :]).then_inc(ld_max1, 16)

            load_x(0, first=True)
            load_x1(0, first=True)
            spread(0, first=True)
            place_max(0)
            with sp.Fori(0, B - 1) as e:
                load_x(e + 1)
                move_y(e)
                spread(e + 1)
                spread1(e)
                place_max(e + 1)
                load_x1(e + 1)
            move_y(B - 1)
            spread1(B - 1)

        @block.tensor
        def _(pe):
            def project(b, first=False):
                pe.wait_ge(ld_x, b * 16 + 16)
                if not first:
                    pe.wait_ge(exp_ok, b * U0)
                for n, (bank, done) in enumerate(((pA, q_ps), (pB, k_ps))):
                    for oc in range(NC):
                        for c in range(NC):
                            last = nc.tensor.matmul(bank[:, oc, :], W0T[:, n, c, oc * P:oc * P + P], xs[:, c, :],
                                                    start=(c == 0), stop=(c == NC - 1))
                    last.then_inc(done, 1)
                if not first:
                    pe.wait_ge(y_ok, b * G)
                for tc in range(DC):
                    for c in range(NC):
                        last = nc.tensor.matmul(pC[:, tc // 2, (tc % 2) * N:(tc % 2) * N + N], xs[:, c, tc * P:tc * P + P],
                                                W0T[:, 2, c, :], start=(tc % 2 == 0 and c == 0), stop=(c == NC - 1),
                                                skip_group_check=True)
                last.then_inc(v_ps, 1)

            def max_scores(b, u):
                if u == 0:
                    pe.wait_ge(ld_rep, b * 128 + 128)
                    pe.wait_ge(ld_rows, b * 16 + 16)
                    pe.wait_ge(q_lo_ok, b + 1)
                if u == 1:
                    pe.wait_ge(kf_ok, b + 1)
                if u >= 2:
                    pe.wait_ge(s_max, b * U0 + (u - 1))
                for qc in range(2):
                    t0 = (2 * (u % 2) + qc) * P
                    last = nc.tensor.matmul(pair[u % 2][:, qc, :], q_rep[0:96, u // 2, t0:t0 + P], k_rep[0:96, u // 2, :],
                                            start=True, stop=True)
                last.then_inc(s_ps, 1)

            def max_to_row(b):
                pe.wait_ge(neg_max, b + 1)
                nc.tensor.matmul(pA[0:H * DC, 0, 0:P], head_max[:, :], ident[:, :], start=True, stop=True).then_inc(max_ps, 1)

            def attend(b, e=None):
                if e is not None:
                    residual(e, 0)
                    residual(e, 1)
                pe.wait_ge(ld_max, b * 16 + 16)
                pe.wait_ge(v_ok, b + 1)

                def weigh(n):
                    g, kc = n // DC, n % DC
                    pe.wait_ge(exp_ok, b * U0 + (2 * n + 2))
                    if kc == 0 and g >= 2:
                        pe.wait_ge(y_ok, b * G + (g - 1))
                    for j in range(4):
                        last = nc.tensor.matmul(pC[32 * j:32 * j + 32, g % 2, :], v_aug[:, kc, 4 * g + j, :], probs[n % 2][:, j, :],
                                                start=(kc == 0), stop=(kc == DC - 1), skip_group_check=True)
                    last.then_inc(pv_ps, 1)

                for n in range(G * DC):
                    g, kc = n // DC, n % DC
                    for hf in range(2):
                        u = 2 * n + hf
                        if u >= 2:
                            pe.wait_ge(exp_ok, b * U0 + (u - 1))
                        for j in range(2):
                            h = 4 * g + 2 * hf + j
                            last = nc.tensor.matmul(pair[u % 2][:, j, :], k_rep[:, h, kc * P:kc * P + P], q_rep[:, h, :],
                                                    start=True, stop=True)
                        last.then_inc(st_ps, 1)
                    if e is not None and n < 2:
                        residual(e, 2 + n)
                    if n >= 1:
                        weigh(n - 1)
                weigh(G * DC - 1)

            def tokens(e, last_one=False):
                pe.wait_ge(xn_ok, e * 2 + 2)
                for c in range(DC):
                    for tc in range(NC):
                        last = nc.tensor.transpose(pD[:, c // 2, (c % 2) * N + tc * P:(c % 2) * N + tc * P + P],
                                                   xn[:, tc, c * P:c * P + P], ident[:, :])
                last.then_inc(xnT_ps, 1)
                pe.wait_ge(xnT_ok, e * DC + DC)
                if last_one:
                    pe.wait_ge(y_ok, B * G)
                else:
                    pe.wait_ge(v_ok, e + 2)

            def qk_chunk(e, m):
                if m < M8:
                    if m >= 3:
                        pe.wait_ge(qn_ok, e * M8 + (m - 2))
                    for c in range(DC):
                        last = nc.tensor.matmul(qk_bank[m % 3][:, 0:N], wqkv[:, c, m * P:m * P + P], xnT[:, c, :],
                                                start=(c == 0), stop=(c == DC - 1))
                    last.then_inc(qk_ps, 1)
                if m >= 1:
                    pe.wait_ge(sq_ok, e * M8 + m)
                    if m >= 2:
                        pe.wait_ge(hln_ok, e * M8 + (m - 1))
                    nc.tensor.matmul(pD[:, 0, 0:N], head_ones[:, :], sq[(m - 1) % 2][:, :], start=True, stop=True).then_inc(hss_ps, 1)

            def v_tokens(e, n):
                tc, c = n // DC, n % DC
                if n == 0:
                    pe.wait_ge(hln_ok, e * M8 + M8)
                if c == 0 and tc == 1:
                    pe.wait_ge(qn_ok, e * M8 + M8)
                last = nc.tensor.matmul(pD[:, tc, :], xnT[:, c, tc * P:tc * P + P], wqkv[:, c, 2 * D:3 * D],
                                        start=(c == 0), stop=(c == DC - 1))
                if n == NC * DC - 1:
                    last.then_inc(v1_ps, 1)

            def max1_scores(e, u):
                if u == 0:
                    pe.wait_ge(ld_rep1, e * 128 + 128)
                    pe.wait_ge(qn_ok, e * M8 + M8)
                elif u == 1:
                    pe.wait_ge(v1_ok, e + 1)
                else:
                    pe.wait_ge(s1_max, e * U1 + (u - 1))
                for j in range(2):
                    for qc in range(NC):
                        last = nc.tensor.matmul(pair1[u % 2][:, j, qc * N:qc * N + N], q1_rep[:, 2 * u + j, qc * P:qc * P + P],
                                                k1_rep[:, 2 * u + j, :], start=(qc == 0), stop=(qc == NC - 1),
                                                skip_group_check=True)
                last.then_inc(s1_ps, 1)

            def max1_to_row(e):
                pe.wait_ge(neg_max1, e + 1)
                nc.tensor.matmul(pC[0:H * NC, 0, 0:P], head_max1[:, :], ident[:, :], start=True, stop=True).then_inc(max1_ps, 1)

            def scores1(e, h):
                if h == 0:
                    pe.wait_ge(ld_max1, e * 16 + 16)
                    pe.wait_ge(max1_ok, e + 1)
                if h >= 2:
                    pe.wait_ge(exp1_ok, e * H + (h - 1))
                for kc in range(NC):
                    o = pC[:, h % 2, kc * N:kc * N + N]
                    nc.tensor.matmul(o, k1_rep[:, h, kc * P:kc * P + P], q1_rep[:, h, :],
                                     start=(kc == 0), stop=False, skip_group_check=True)
                    last = nc.tensor.matmul(o, row_const[:, :], max1_rows[:, h, :], start=False, stop=True,
                                            skip_group_check=True)
                last.then_inc(st1_ps, 1)

            def weigh1(e, g):
                pe.wait_ge(exp1_ok, e * H + (4 * g + 4))
                if g >= 2:
                    pe.wait_ge(oT_ok, e * G + (g - 1))
                for side in range(2):
                    for kc in range(NC):
                        for j in range(4):
                            h = 4 * g + j
                            v = ones32[:, :] if side else v1[:, kc, h * DH1:h * DH1 + DH1]
                            last = nc.tensor.matmul(pD[32 * j:32 * j + 32, g % 2, side * N:side * N + N], v,
                                                    probs[g % 2][:, j, kc * N:kc * N + N],
                                                    start=(side == 0 and kc == 0), stop=(kc == NC - 1), skip_group_check=True)
                last.then_inc(pv1_ps, 1)

            def residual(e, oc):
                if oc == 0:
                    pe.wait_ge(oT_ok, e * G + G)
                o = pD[:, oc // 2, (oc % 2) * N:(oc % 2) * N + N]
                for tc in range(NC):
                    nc.tensor.matmul(o[:, tc * P:tc * P + P], x1[:, tc, oc * P:oc * P + P], ident[:, :],
                                     start=(oc % 2 == 0 and tc == 0), stop=False, skip_group_check=True)
                for c in range(DC):
                    last = nc.tensor.matmul(o, wout[:, c, oc * P:oc * P + P], oT[:, c, :], start=False, stop=(c == DC - 1),
                                            skip_group_check=True)
                if oc == DC - 1:
                    last.then_inc(res_ps, 1)

            def steps(order, e, b):
                for kind, n in order:
                    if kind == "max":
                        max_scores(b, n)
                    elif kind == "row":
                        max_to_row(b)
                    elif kind == "qk":
                        qk_chunk(e, n)
                    elif kind == "v":
                        v_tokens(e, n)
                    elif kind == "max1":
                        max1_scores(e, n)
                    elif kind == "row1":
                        max1_to_row(e)
                    elif kind == "score1":
                        scores1(e, n)
                    elif kind == "weigh1":
                        weigh1(e, n)

            project(0, first=True)
            steps(ALONE0, None, 0)
            attend(0)
            with pe.Fori(0, B - 1) as e:
                project(e + 1)
                tokens(e)
                steps(BESIDE, e, e + 1)
                attend(e + 1, e)
            tokens(B - 1, last_one=True)
            steps(ALONE1, B - 1, None)
            for oc in range(DC):
                residual(B - 1, oc)

        @block.scalar
        def _(act):
            def q_parts(b):
                act.wait_ge(q_ps, b + 1)
                nc.scalar.activation(q_hi[:, :, :], pA[:, :, :], ACT.Copy, scale=QS).then_inc(q_hi_ok, 1)

            def kv_parts(b):
                act.wait_ge(kf_ok, b + 1)
                nc.scalar.activation(k_hi[:, :, :], kf[:, :, :], ACT.Copy).then_inc(k_hi_ok, 1)
                act.wait_ge(v_ps, b + 1)
                nc.scalar.activation(v_aug[:, :, :, 0:DH0], pC[:, :, :].rearrange("p a (b h d) -> p (a b) h d", b=2, d=DH0),
                                     ACT.Copy).then_inc(v_ok, 1)

            def max_rows(b):
                act.wait_ge(max_ps, b + 1)
                nc.scalar.activation(max_row[:, :], pA[0:H * DC, 0, 0:P], ACT.Copy).then_inc(max_ok, 1)

            def attend(b):
                for n in range(G * DC):
                    for hf in range(2):
                        u = 2 * n + hf
                        act.wait_ge(st_ps, b * U0 + (u + 1))
                        if n >= 2 and hf == 0:
                            act.wait_ge(pv_ps, b * G * DC + (n - 1))
                        nc.scalar.activation(probs[n % 2][:, 2 * hf:2 * hf + 2, :], pair[u % 2][:, :, :], ACT.Exp,
                                             scale=LOGIT0).then_inc(exp_ok, 1)

            def token_rms(e):
                act.wait_ge(x1_ok, e + 1)
                for c in range(NC):
                    nc.scalar.activation(xn[:, c, :], x1[:, c, :], ACT.Square, accum_out=sq_sum[:, c:c + 1]).then_inc(ss_ok, 1)
                act.wait_ge(ss_ok, e * 2 + 2)
                nc.scalar.activation(rstd[:, :], sq_sum[:, :], ACT.Ln, bias=eps_d[:, 0:1]).then_inc(sse_ok, 1)
                act.wait_ge(sse_ok, e + 1)
                nc.scalar.activation(rstd[:, :], rstd[:, :], ACT.Exp, scale=-0.5).then_inc(rstd_ok, 1)

            def qk_chunk(e, m):
                def head_rms(m):
                    act.wait_ge(hss_ps, e * M8 + (m + 1))
                    if m >= 2:
                        act.wait_ge(qn_ok, e * M8 + (m - 1))
                    nc.scalar.activation(head_rstd[m % 2][:, :], pD[:, 0, 0:N], ACT.Ln, bias=eps_h[:, 0:1]).then_inc(hln_ok, 1)
                    act.wait_ge(hln_ok, e * M8 + (m + 1))
                    nc.scalar.activation(head_rstd[m % 2][:, :], head_rstd[m % 2][:, :], ACT.Exp, scale=-0.5).then_inc(hrs_ok, 1)

                def hi_part(m):
                    if m == 0 and not isinstance(e, int):
                        act.wait_ge(st_parts, e * 64 + 128)
                    act.wait_ge(qn_ok, e * M8 + (m + 1))
                    nc.scalar.activation(hi1[:, m // DC, m % DC, :], qn[m % 2][:, :], ACT.Copy).then_inc(hi_ok, 1)

                if m < M8:
                    act.wait_ge(qk_ps, e * M8 + (m + 1))
                    if m >= 2:
                        act.wait_ge(hss_ps, e * M8 + (m - 1))
                    nc.scalar.activation(sq[m % 2][:, :], qk_bank[m % 3][:, 0:N], ACT.Square).then_inc(sq_ok, 1)
                if m >= 1:
                    head_rms(m - 1)
                if m >= 2:
                    hi_part(m - 2)
                if m == M8:
                    hi_part(m - 1)

            def inverse1(e, g):
                act.wait_ge(pv1_ps, e * G + (g + 1))
                if g >= 1:
                    act.wait_ge(oT_ok, e * G + g)
                nc.scalar.activation(inv_sum[:, :], pD[:, g % 2, N:2 * N], ACT.Ln).then_inc(log1_ok, 1)
                act.wait_ge(log1_ok, e * G + (g + 1))
                nc.scalar.activation(inv_sum[:, :], inv_sum[:, :], ACT.Exp, scale=-1.0).then_inc(inv1_ok, 1)

            def steps(order, e, b):
                for kind, n in order:
                    if kind == "row":
                        max_rows(b)
                    elif kind == "qk":
                        qk_chunk(e, n)
                    elif kind == "v" and n == NC * DC - 1:
                        act.wait_ge(v1_ps, e + 1)
                        nc.scalar.activation(v1[:, :, :], pD[:, :, :], ACT.Copy).then_inc(v1_ok, 1)
                    elif kind == "row1":
                        act.wait_ge(max1_ps, e + 1)
                        nc.scalar.activation(max1_row[:, :], pC[0:H * NC, 0, 0:P], ACT.Copy).then_inc(max1_ok, 1)
                    elif kind == "score1":
                        act.wait_ge(st1_ps, e * H + (n + 1))
                        if n == 0:
                            act.wait_ge(pv_ps, e * G * DC + G * DC)
                        if n >= 8 and n % 4 == 0:
                            act.wait_ge(pv1_ps, e * G + (n // 4 - 1))
                        nc.scalar.activation(probs[(n // 4) % 2][:, n % 4, :], pC[:, n % 2, :], ACT.Exp, scale=LOGIT1).then_inc(exp1_ok, 1)
                    elif kind == "weigh1":
                        inverse1(e, n)

            q_parts(0)
            kv_parts(0)
            steps(ALONE0, None, 0)
            attend(0)
            with act.Fori(0, B - 1) as e:
                q_parts(e + 1)
                token_rms(e)
                kv_parts(e + 1)
                steps(BESIDE, e, e + 1)
                attend(e + 1)
            token_rms(B - 1)
            steps(ALONE1, B - 1, None)

        @block.vector
        def _(dve):
            def q_parts(b, first=False):
                dve.wait_ge(q_hi_ok, b + 1)
                nc.vector.scalar_tensor_tensor(out=q_lo[:, :, :], in0=pA[:, :, :], scalar=QS, in1=q_hi[:, :, :],
                                               op0=ALU.mult, op1=ALU.subtract).then_inc(q_lo_ok, 1)
                if not first:
                    for n in range(2):
                        dve.wait_ge(ld_y[n], b * 128)
                dve.wait_ge(ld_mask, b * 16 + 16)
                dve.wait_ge(k_ps, b + 1)
                for c in range(NC):
                    last = nc.vector.scalar_tensor_tensor(out=kf[:, c, :], in0=pB[:, c, :], scalar=QS, in1=mask_bc[:, :],
                                                          op0=ALU.mult, op1=ALU.mult)
                last.then_inc(kf_ok, 1)

            def k_part(b):
                dve.wait_ge(kf_ok, b + 1)
                dve.wait_ge(k_hi_ok, b + 1)
                nc.vector.tensor_tensor(k_lo[:, :, :], kf[:, :, :], k_hi[:, :, :], ALU.subtract).then_inc(k_lo_ok, 1)

            def attend(b):
                for g in range(G):
                    dve.wait_ge(pv_ps, b * G * DC + DC * (g + 1))
                    if g >= 1:
                        dve.wait_ge(y_ok, b * G + g)
                    nc.vector.memset(tick[:, :], 0.0).then_inc(ticked, 1)
                    nc.vector.stream_shuffle(sums[:, :], pC[:, g % 2, :], [16 + n % 16 for n in range(32)]).then_inc(sums_ok, 1)
                    dve.wait_ge(sums_ok, b * G + (g + 1))
                    nc.vector.reciprocal(sums[:, :], sums[:, :]).then_inc(inv_ok, 1)
                    dve.wait_ge(inv_ok, b * G + (g + 1))
                    if g >= 2:
                        dve.wait_ge(ld_y[g % 2], b * 128 + 64)
                    nc.vector.tensor_tensor(y_pad[g % 2], pC[:, g % 2, :], sums[:, :], ALU.mult).then_inc(y_ok, 1)

            def normalise(e):
                dve.wait_ge(rstd_ok, e + 1)
                for c in range(NC):
                    nc.vector.tensor_scalar(xn[:, c, :], x1[:, c, :], rstd[:, c:c + 1], D ** 0.5, ALU.mult, ALU.mult).then_inc(xn_ok, 1)

            def tokens(e):
                dve.wait_ge(xnT_ps, e + 1)
                for c in range(DC):
                    nc.vector.tensor_scalar(xnT[:, c, :], pD[:, c // 2, (c % 2) * N:(c % 2) * N + N],
                                            film_scale[:, c, bass.ds(e, 1)], film_shift[:, c, bass.ds(e, 1)],
                                            ALU.mult, ALU.add).then_inc(xnT_ok, 1)

            def qk_chunk(e, m):
                def lo_part(m):
                    dve.wait_ge(hi_ok, e * M8 + (m + 1))
                    nc.vector.tensor_tensor(lo1[:, m // DC, m % DC, :], qn[m % 2][:, :], hi1[:, m // DC, m % DC, :],
                                            ALU.subtract).then_inc(lo_ok, 1)

                dve.wait_ge(hrs_ok, e * M8 + (m + 1))
                if m >= 2:
                    dve.wait_ge(lo_ok, e * M8 + (m - 1))
                nc.vector.scalar_tensor_tensor(out=qn[m % 2][:, :], in0=qk_bank[m % 3][:, 0:N],
                                               scalar=(gq if m < DC else gk)[:, 0:1], in1=head_rstd[m % 2][:, :],
                                               op0=ALU.mult, op1=ALU.mult).then_inc(qn_ok, 1)
                if m >= 1:
                    lo_part(m - 1)
                if m == M8 - 1:
                    lo_part(m)

            def steps(order, e, b):
                for kind, n in order:
                    if kind == "max":
                        dve.wait_ge(s_ps, b * U0 + (n + 1))
                        nc.vector.tensor_reduce(head_max[:, 2 * n:2 * n + 2], pair[n % 2][:, :, :], AX.X, ALU.max).then_inc(s_max, 1)
                    elif kind == "qk" and n >= 1:
                        qk_chunk(e, n - 1)
                    elif kind == "row":
                        dve.wait_ge(s_max, b * U0 + U0)
                        nc.vector.tensor_scalar(head_max[:, :], head_max[:, :], -1.0 / ROW, None, ALU.mult).then_inc(neg_max, 1)
                    elif kind == "max1":
                        dve.wait_ge(s1_ps, e * U1 + (n + 1))
                        nc.vector.tensor_reduce(head_max1[:, 4 * n:4 * n + 4], pair1[n % 2][:, :, :].rearrange("p j (q k) -> p (j q) k", q=NC),
                                                AX.X, ALU.max).then_inc(s1_max, 1)
                    elif kind == "row1":
                        dve.wait_ge(s1_max, e * U1 + U1)
                        nc.vector.tensor_scalar(head_max1[:, :], head_max1[:, :], -1.0 / ROW, None, ALU.mult).then_inc(neg_max1, 1)
                    elif kind == "out1":
                        dve.wait_ge(inv1_ok, e * G + (n + 1))
                        nc.vector.tensor_tensor(oT[:, n, :], pD[:, n % 2, 0:N], inv_sum[:, :], ALU.mult).then_inc(oT_ok, 1)

            def residual(e):
                dve.wait_ge(res_ps, e + 1)
                dve.wait_ge(oT_ok, e * G + G)
                nc.vector.tensor_tensor(xT[:, :, bass.ds(e, 1), :].rearrange("p c o t -> p c (o t)"),
                                        pD[:, :, :].rearrange("p a (b t) -> p (a b) t", b=2), oT[:, :, :], ALU.add).then_inc(xT_ok, 1)

            q_parts(0, first=True)
            k_part(0)
            steps(ALONE0, None, 0)
            attend(0)
            with dve.Fori(0, B - 1) as e:
                q_parts(e + 1)
                normalise(e)
                k_part(e + 1)
                tokens(e)
                steps(BESIDE, e, e + 1)
                residual(e)
                attend(e + 1)
            normalise(B - 1)
            tokens(B - 1)
            steps(ALONE1, B - 1, None)
            residual(B - 1)

        @block.gpsimd
        def _(pool):
            with pool.Fori(0, B) as b:
                for n in range(2):
                    pool.wait_ge(ld_y[n], b * 128 + 128)
                pool.wait_ge(ld_x1, b * 16 + 16)
                nc.gpsimd.tensor_tensor(x1[:, :, :], x1[:, :, :], y[:, :, :], ALU.add).then_inc(x1_ok, 1)


def recurrence(nc, sem, sb, W_ih, W_hh, b_ih, b_hh, pA, pB, pC, pD, xT, ident, condT):
    with ExitStack() as ctx:
        def t(name, shape, dt=F32):
            return sb(ctx, name, shape, dt)

        w_in = [t(f"wih_{n}", [P, DC, 3 * D], F16) for n in ("hi", "lo")]
        w_part = [t(f"whh_{n}", [P, DC, 3 * D], F16) for n in ("hi", "lo")]
        gi_rz = t("gi_rz", [P, N, 2 * DC, 2, B], F16)
        gi_n = t("gi_n", [P, N + 1, DC, B])
        x_part = t("x_part", [P, 2, DC, B, TB], F16)
        gi_f32 = t("gi_f32", [P, B, TB])
        spread16 = t("spread16", [P, P], F16)
        bias_in = t("bias_in", [P, MC])
        bias_hn = t("bias_hn", [P, DC, 2, B], F16)
        bias_f32 = t("bias_f32", [P, DC, B])
        state = [t(f"state{n}", [P, DC, B]) for n in range(2)]
        moving = t("moving", [P, DC, 2, B], F16)
        r_pre = t("r_pre", [P, DC, B])
        r_gate = t("r_gate", [P, DC, B])
        z_pre = t("z_pre", [P, DC, B])
        z_gate = t("z_gate", [P, DC, B])
        n_terms = t("n_terms", [P, DC, 3, B])
        n_pre = t("n_pre", [P, DC, B])
        cand = t("cand", [P, DC, B])
        diff = t("diff", [P, DC, B])
        z_diff = t("z_diff", [P, DC, B])
        unscaled = t("unscaled", [P, DC, B])
        unit = t("unit", [P, DC, B])
        bih_c = t("bih_c", [P, MC])
        bhh_c = t("bhh_c", [P, MC])
        staged = gi_rz[:, TB:, :, :, :].rearrange("p t m s b -> p (t m s b)").bitcast(F32)
        staged = [staged[:, n * DC * 3 * D:(n + 1) * DC * 3 * D].rearrange("p (c n) -> p c n", c=DC) for n in range(2)]

        w_ld, w_ld2, b_ld, wi_hi, wi_lo, w_hi, w_lo, b_ok, h_ok, diag_ok = (
            sem(n) for n in ("w_ld", "w_ld2", "b_ld", "wi_hi", "wi_lo", "w_hi", "w_lo", "b_ok", "h_ok", "diag_ok"))
        x_hi, x_lo, gi_ps, gi_out, gi_hi, gi_lo = (
            sem("gru_" + n) for n in ("x_hi", "x_lo", "gi_ps", "gi_out", "gi_hi", "gi_lo"))
        r_ps, n_ps, z_ps, r_sum, z_sum, r_ok, z_ok, n_mul, n_sum, n_ok, d_ok, zd_ok, hi_done, st_ok, lo_done = (
            sem("gru_" + n) for n in ("r_ps", "n_ps", "z_ps", "r_sum", "z_sum", "r_ok", "z_ok", "n_mul", "n_sum", "n_ok", "d_ok", "zd_ok", "hi_done", "st_ok",
                      "lo_done"))
        n_in, h_un, x_add = (sem("gru_" + n) for n in ("n_in", "h_un", "x_add"))
        block = ctx.enter_context(nc.Block())
        CHUNKS = (range(0, 1), range(1, DC))
        SLICE = (slice(0, 1), slice(1, DC))
        pR = (pA[:, 0, 0:16], pA[:, 1, 0:48])
        pN = (pB[:, 0, 0:16], pB[:, 1, 0:48])
        pZ = (pC[:, 0, 0:16], pC[:, 1, 0:48])
        pG = [pD[:, 0, :], pD[:, 1, :]]
        BLOCKS = N // TB
        BODY = DC
        PLAIN = TB - MC * BODY
        RZ = 2 * DC

        def halves(ps):
            return ps.rearrange("p (c s b) -> p c b s", s=2, b=B)

        def blocks(eng, step, split, product):
            with eng.Fori(0, BLOCKS - 1) as blk:
                with eng.Fori(0, PLAIN // BODY) as k:
                    for j in range(BODY):
                        step(blk * TB + k * BODY + j, j, blk)
                        if j == 0:
                            split(blk + 1, k)
                with eng.Fori(0, RZ) as m:
                    for j in range(BODY):
                        step(blk * TB + m * BODY + (PLAIN + j), j)
                        product(blk + 1, m, j, False)
                with eng.Fori(RZ, MC) as m:
                    for j in range(BODY):
                        step(blk * TB + m * BODY + (PLAIN + j), j)
                        product(blk + 1, m, j, True)
            with eng.Fori(0, TB // BODY) as k:
                for j in range(BODY):
                    step(k * BODY + (N - TB + j), j, BLOCKS - 1)

        @block.sync
        def _(sp):
            sp.dma_start(bih_c[:, :], b_ih.rearrange("(c p) -> p c", p=P), allow_slow_non_contiguous=True).then_inc(b_ld, 16)
            sp.dma_start(bhh_c[:, :], b_hh.rearrange("(c p) -> p c", p=P), allow_slow_non_contiguous=True).then_inc(b_ld, 16)
            sp.dma_start(staged[0], W_ih.rearrange("(c p) n -> p c n", p=P)).then_inc(w_ld, 16)
            sp.dma_start(staged[1], W_hh.rearrange("(c p) n -> p c n", p=P)).then_inc(w_ld2, 16)

        @block.tensor
        def _(pe):
            def products(m, k, bank):
                for w in range(2):
                    for part in range(2):
                        last = nc.tensor.matmul(bank, w_in[w][:, k, bass.ts(m, P)], x_part[:, part, k, :, :].rearrange("p b t -> p (b t)"),
                                                start=(k == 0 and w == 0 and part == 0), stop=(k == DC - 1 and w == 1 and part == 1))
                return last

            def step(step, j, blk=None):
                if j == 0 and blk is not None:
                    pe.wait_ge(gi_lo, blk * RZ + RZ)
                pe.wait_ge(hi_done, step * 2 + 1)
                for part in range(2):
                    c0, c1 = SLICE[part].start, SLICE[part].stop
                    for ps, src in ((pR, gi_rz[:, bass.ds(step, 1), c0:c1, :, :].rearrange("p o c s b -> p (o c s b)")),
                                    (pN, bias_hn[:, c0:c1, :, :].rearrange("p c s b -> p (c s b)")),
                                    (pZ, gi_rz[:, bass.ds(step, 1), DC + c0:DC + c1, :, :].rearrange("p o c s b -> p (o c s b)"))):
                        nc.tensor.matmul(ps[part], spread16[:, :], src, start=True, stop=False, skip_group_check=True)

                def gate(ps, first, part, ks):
                    for c in CHUNKS[part]:
                        o = (c - CHUNKS[part][0]) * 2 * B
                        for k in ks:
                            for w in w_part:
                                last = nc.tensor.matmul(ps[part][:, o:o + 2 * B], w[:, k, (first + c) * P:(first + c) * P + P],
                                                        moving[:, k, :, :].rearrange("p s b -> p (s b)"), start=False,
                                                        stop=(k == DC - 1), skip_group_check=True)
                    return last

                pe.wait_ge(lo_done, step * 2 + 1)
                for ps, first in ((pR, 0), (pN, 2 * DC), (pZ, DC)):
                    for part in range(2):
                        gate(ps, first, part, CHUNKS[0])
                pe.wait_ge(lo_done, step * 2 + 2)
                for part in range(2):
                    for ps, first, done in ((pR, 0, r_ps), (pN, 2 * DC, n_ps), (pZ, DC, z_ps)):
                        gate(ps, first, part, CHUNKS[1]).then_inc(done, 1)

            def nothing(*_):
                pass

            def product(blk, m, j, is_n):
                if j == 0:
                    pe.wait_ge(x_lo, blk * DC + DC)
                    pe.wait_ge(gi_out, blk * MC + m)
                last = products(m, j, pG[0])
                if j == DC - 1:
                    last.then_inc(gi_ps, 1)

            pe.wait_ge(wi_lo, DC)
            pe.wait_ge(x_lo, DC)
            for m in range(MC):
                if m >= 2:
                    pe.wait_ge(gi_out, m - 1)
                for k in range(DC):
                    last = products(m, k, pG[m % 2])
                last.then_inc(gi_ps, 1)
            pe.wait_ge(w_lo, DC)
            pe.wait_ge(b_ok, 7)
            pe.wait_ge(gi_out, MC)
            pe.wait_ge(gi_lo, RZ)
            blocks(pe, step, nothing, product)

        @block.scalar
        def _(act):
            act.wait_ge(w_ld, 16)
            for k in range(DC):
                nc.scalar.activation(w_in[0][:, k, :], staged[0][:, k, :], ACT.Copy, scale=WS).then_inc(wi_hi, 1)
            act.wait_ge(w_ld2, 16)
            for k in range(DC):
                nc.scalar.activation(w_part[0][:, k, :], staged[1][:, k, :], ACT.Copy, scale=WS).then_inc(w_hi, 1)
            nc.scalar.preload_act_table_set("sigmoid_and_others")
            act.wait_ge(b_ok, 6)

            def step(step, j, blk=None):
                for kind, part in (("r", 0), ("z", 0), ("r", 1), ("n", 0), ("n", 1), ("z", 1)):
                    src, dst, ready, done = {"r": (r_pre, r_gate, r_sum, r_ok), "z": (z_pre, z_gate, z_sum, z_ok),
                                             "n": (n_pre, cand, n_sum, n_ok)}[kind]
                    act.wait_ge(ready, step * 2 + (part + 1))
                    nc.scalar.activation(dst[:, SLICE[part], :], src[:, SLICE[part], :], ACT.Tanh if kind == "n" else ACT.Sigmoid,
                                         scale=1.0 / GS).then_inc(done, 1)

            def nothing(*_):
                pass

            def evacuate(blk, m, bank, is_n, first=False):
                act.wait_ge(gi_ps, blk * MC + m + 1)
                src = bank.rearrange("p (b t) -> p b t", b=B)
                if is_n:
                    dst = gi_n[:, bass.ts(blk, TB), bass.ds(m - RZ, 1), :].rearrange("p t o b -> p b (t o)")
                    nc.scalar.activation(dst, src, ACT.Identity, bias=bias_in[:, bass.ds(m, 1)], scale=GS / WS).then_inc(gi_out, 1)
                else:
                    if not first:
                        act.wait_ge(gi_lo, blk * RZ + m)
                    dst = gi_rz[:, bass.ts(blk, TB), bass.ds(m, 1), 0, :].rearrange("p t o b -> p b (t o)")
                    nc.scalar.activation(dst, src, ACT.Identity, bias=bias_in[:, bass.ds(m, 1)], scale=IS / WS).then_inc(gi_hi, 1)
                    nc.scalar.activation(gi_f32[:, :, :], src, ACT.Identity, bias=bias_in[:, bass.ds(m, 1)], scale=IS / WS).then_inc(gi_out, 1)

            def product(blk, m, j, is_n):
                if j == BODY - 1:
                    evacuate(blk, m, pG[0], is_n)

            for m in range(MC):
                evacuate(0, m, pG[m % 2], m >= RZ, first=(m == 0))
            blocks(act, step, nothing, product)

        @block.vector
        def _(dve):
            dve.wait_ge(b_ld, 32)
            nc.vector.tensor_tensor(bias_in[:, 0:RZ], bih_c[:, 0:RZ], bhh_c[:, 0:RZ], ALU.add).then_inc(b_ok, 1)
            nc.vector.tensor_scalar(bias_in[:, RZ:], bih_c[:, RZ:], GS, None, ALU.mult).then_inc(b_ok, 1)
            nc.vector.tensor_scalar(bias_f32[:, :, :], bhh_c[:, RZ:].unsqueeze(2).broadcast_to([P, DC, B]), IS, None, ALU.mult).then_inc(b_ok, 1)
            nc.vector.tensor_scalar(spread16[:, :], ident[:, :], GS / IS, None, ALU.mult).then_inc(b_ok, 1)
            dve.wait_ge(b_ok, 3)
            nc.vector.tensor_scalar(bias_in[:, 0:RZ], bias_in[:, 0:RZ], IS, None, ALU.mult).then_inc(b_ok, 1)
            nc.vector.tensor_copy(bias_hn[:, :, 0, :], bias_f32[:, :, :]).then_inc(b_ok, 1)
            dve.wait_ge(b_ok, 6)
            nc.vector.tensor_tensor(bias_hn[:, :, 1, :], bias_f32[:, :, :], bias_hn[:, :, 0, :], ALU.subtract).then_inc(b_ok, 1)
            nc.vector.tensor_scalar(state[1][:, :, :], condT[:, :, :], HS, None, ALU.mult).then_inc(h_ok, 1)
            for part in range(2):
                nc.vector.tensor_scalar(moving[:, SLICE[part], 0, :], condT[:, SLICE[part], :], HS, None, ALU.mult).then_inc(hi_done, 1)
            dve.wait_ge(h_ok, 1)
            for part in range(2):
                dve.wait_ge(hi_done, part + 1)
                nc.vector.tensor_tensor(moving[:, SLICE[part], 1, :], state[1][:, SLICE[part], :], moving[:, SLICE[part], 0, :],
                                        ALU.subtract).then_inc(lo_done, 1)
            for n, (w, his, los) in enumerate(((w_in, wi_hi, wi_lo), (w_part, w_hi, w_lo))):
                for k in range(DC):
                    dve.wait_ge(his, k + 1)
                    nc.vector.scalar_tensor_tensor(out=w[1][:, k, :], in0=staged[n][:, k, :], scalar=WS, in1=w[0][:, k, :],
                                                   op0=ALU.mult, op1=ALU.subtract).then_inc(los, 1)

            def step(step, j, blk=None):
                old, new = state[1 - j % 2], state[j % 2]

                def sum_r(part):
                    dve.wait_ge(r_ps, step * 2 + (part + 1))
                    nc.vector.tensor_reduce(r_pre[:, SLICE[part], :], halves(pR[part]), AX.X, ALU.add).then_inc(r_sum, 1)

                def sum_z(part):
                    dve.wait_ge(z_ps, step * 2 + (part + 1))
                    nc.vector.tensor_reduce(z_pre[:, SLICE[part], :], halves(pZ[part]), AX.X, ALU.add).then_inc(z_sum, 1)

                def mul_n(part):
                    dve.wait_ge(n_ps, step * 2 + (part + 1))
                    dve.wait_ge(r_ok, step * 2 + (part + 1))
                    nc.vector.tensor_tensor(n_terms[:, SLICE[part], 0:2, :], pN[part].rearrange("p (c s b) -> p c s b", s=2, b=B),
                                            r_gate[:, SLICE[part], :].unsqueeze(2).broadcast_to([P, len(CHUNKS[part]), 2, B]),
                                            ALU.mult).then_inc(n_mul, 1)

                def sum_n(part):
                    if part == 0:
                        dve.wait_ge(n_in, step + 1)
                    dve.wait_ge(n_mul, step * 2 + (part + 1))
                    nc.vector.tensor_reduce(n_pre[:, SLICE[part], :], n_terms[:, SLICE[part], :, :].rearrange("p c s b -> p c b s"), AX.X,
                                            ALU.add).then_inc(n_sum, 1)

                def difference(part):
                    dve.wait_ge(n_ok, step * 2 + (part + 1))
                    nc.vector.scalar_tensor_tensor(out=diff[:, SLICE[part], :], in0=cand[:, SLICE[part], :], scalar=-HS,
                                                   in1=old[:, SLICE[part], :], op0=ALU.mult, op1=ALU.add).then_inc(d_ok, 1)

                def weigh(part):
                    dve.wait_ge(z_ok, step * 2 + (part + 1))
                    dve.wait_ge(d_ok, step * 2 + (part + 1))
                    nc.vector.tensor_tensor(z_diff[:, SLICE[part], :], z_gate[:, SLICE[part], :], diff[:, SLICE[part], :],
                                            ALU.mult).then_inc(zd_ok, 1)

                def new_state(part):
                    dve.wait_ge(zd_ok, step * 2 + (part + 1))
                    for out, done in ((moving[:, SLICE[part], 0, :], hi_done), (new[:, SLICE[part], :], st_ok)):
                        nc.vector.scalar_tensor_tensor(out=out, in0=cand[:, SLICE[part], :], scalar=HS, in1=z_diff[:, SLICE[part], :],
                                                       op0=ALU.mult, op1=ALU.add).then_inc(done, 1)

                def lo_part(part):
                    dve.wait_ge(st_ok, step * 2 + (part + 1))
                    nc.vector.tensor_tensor(moving[:, SLICE[part], 1, :], new[:, SLICE[part], :], moving[:, SLICE[part], 0, :],
                                            ALU.subtract).then_inc(lo_done, 1)

                sum_r(0)
                dve.wait_ge(x_add, step + 1)
                sum_z(0)
                mul_n(0)
                sum_r(1)
                sum_n(0)
                mul_n(1)
                difference(0)
                sum_n(1)
                weigh(0)
                sum_z(1)
                new_state(0)
                lo_part(0)
                difference(1)
                weigh(1)
                new_state(1)
                lo_part(1)

            def nothing(*_):
                pass

            blocks(dve, step, nothing, nothing)

        @block.gpsimd
        def _(pool):
            def split(blk, k):
                src = xT[:, bass.ds(k, 1), :, bass.ts(blk, TB)].rearrange("p o b t -> p (o b) t")
                hi, lo = (x_part[:, n, bass.ds(k, 1), :, :].rearrange("p o b t -> p (o b) t") for n in range(2))
                nc.gpsimd.tensor_copy(hi, src).then_inc(x_hi, 1)
                pool.wait_ge(x_hi, blk * DC + k + 1)
                nc.gpsimd.tensor_tensor(lo, src, hi, ALU.subtract).then_inc(x_lo, 1)

            def lo_tile(blk, m):
                pool.wait_ge(gi_out, blk * MC + m + 1)
                nc.gpsimd.tensor_tensor(gi_rz[:, bass.ts(blk, TB), bass.ds(m, 1), 1, :].rearrange("p t o b -> p (t o) b"),
                                        gi_f32[:, :, :].rearrange("p b t -> p t b"),
                                        gi_rz[:, bass.ts(blk, TB), bass.ds(m, 1), 0, :].rearrange("p t o b -> p (t o) b"),
                                        ALU.subtract).then_inc(gi_lo, 1)

            def input_n(step):
                nc.gpsimd.tensor_copy(n_terms[:, :, 2, :], gi_n[:, bass.ds(step, 1), :, :].rearrange("p o c b -> p (o c) b")).then_inc(n_in, 1)

            def step(step, j, blk=None):
                pool.wait_ge(lo_done, step * 2 + 4)
                input_n(step + 1)
                pool.wait_ge(x_add, step + 2)
                nc.gpsimd.tensor_tensor(unscaled[:, :, :], state[j % 2][:, :, :], unit[:, :, :], ALU.mult).then_inc(h_un, 1)
                pool.wait_ge(h_un, step + 1)
                xt = xT[:, :, :, bass.ds(step, 1)].rearrange("p c b o -> p c (b o)")
                nc.gpsimd.tensor_tensor(xt, xt, unscaled[:, :, :], ALU.add).then_inc(x_add, 1)

            def product(blk, m, j, is_n):
                if j == BODY - 1 and not is_n:
                    lo_tile(blk, m)
                if j == BODY - 2 and is_n:
                    pool.wait_ge(gi_out, blk * MC + m + 1)

            nc.gpsimd.memset(unit[:, :, :], 1.0 / HS).then_inc(x_add, 1)
            nc.gpsimd.memset(gi_n[:, N:, :, :], 0.0).then_inc(x_add, 1)
            for k in range(DC):
                split(0, k)
            for m in range(RZ):
                lo_tile(0, m)
            pool.wait_ge(gi_out, MC)
            input_n(0)
            blocks(pool, step, split, product)


def block_attention(nc, sem, sb, cond, rms_w, Wk3, Wo3, gamma, beta, score_col, out, pA, pB, pC, pD, xT, ident):
    NB = 8
    R = B * NB
    with ExitStack() as ctx:
        def t(name, shape, dt=F32):
            return sb(ctx, name, shape, dt)

        wk = t("wk", [P, DC, D])
        tick = t("tick3", [P, 1])
        wo = t("wo", [P, DC, D])
        wkT = t("wkT", [P, DC, D])
        woT = t("woT", [P, DC, D])
        gamma_bc = t("gamma_bc", [P, D])
        beta_bc = t("beta_bc", [P, D])
        query = t("query", [R, D])
        rms_bc = t("rms_bc", [R, D])
        ones_row = t("ones_row", [1, P])
        eps_d = t("eps_d3", [P, 1])
        eps_1 = t("eps_1", [P, 1])
        sumsT = t("sumsT", [P, DC, R])
        key_sq = t("key_sq", [R, D])
        key_q = t("key_q", [R, D])
        key_ss = t("key_ss", [R, 1])
        key_rstd = t("key_rstd", [R, 1])
        key_dot = t("key_dot", [R, 1])
        score = t("score", [R, 1])
        srow = t("srow", [1, B, NB])
        smax = t("smax", [1, B])
        sden = t("sden", [1, B])
        weighted = t("weighted", [P, DC, B, NB])
        attT = t("attT", [P, DC, B])
        projT = t("projT", [P, DC, B])
        xp = t("xp", [P, DC, B, N])
        stats = [t(f"stats{n}", [P, 6]) for n in range(2)]
        mv = [t(f"mv{n}", [P, 2]) for n in range(2)]
        ln_rstd = [t(f"ln_rstd{n}", [P, 1]) for n in range(2)]
        ln_shift = [t(f"ln_shift{n}", [P, 1]) for n in range(2)]
        ln = [t(f"ln{n}", [P, D]) for n in range(2)]
        ln_g = [t(f"ln_g{n}", [P, D]) for n in range(2)]
        ln_x = [t(f"ln_x{n}", [P, D]) for n in range(2)]
        res = [t(f"res{n}", [P, D]) for n in range(2)]

        ld, ones_ok, wT_ps, wT_ok, sums_ok, qw_ok, key_ps, sq_ok, dot_ok, rs_ok, sc_ok, sc_ps, sm, at_ps, wt_ok, att_ok, pj_ps, pj_ok, xp_ok = (
            sem("blk_" + n) for n in ("ld", "ones", "wT_ps", "wT_ok", "sums", "qw", "key_ps", "sq", "dot", "rs", "sc", "sc_ps", "sm", "at_ps",
                                    "wt", "att", "pj_ps", "pj", "xp"))
        y_ps, st_ok, mv_ok, rstd_ok, shift_ok, ln_ok, g_ok, x_ok, res_ok, stored = (
            sem("norm_" + n) for n in ("y_ps", "st", "mv", "rstd", "shift", "ln", "g", "x", "res", "stored"))
        ticked = sem("ticked3")
        block = ctx.enter_context(nc.Block())
        TILES = B * NC

        @block.sync
        def _(sp):
            sp.dma_start(wk[:, :, :], Wk3.rearrange("(c p) n -> p c n", p=P)).then_inc(ld, 16)
            sp.dma_start(wo[:, :, :], Wo3.rearrange("(c p) n -> p c n", p=P)).then_inc(ld, 16)
            sp.dma_start(query[:, :], cond[1:2, :].broadcast_to([R, D])).then_inc(ld, 16)
            sp.dma_start(rms_bc[:, :], rms_w.rearrange("(a n) -> a n", a=1).broadcast_to([R, D])).then_inc(ld, 16)
            sp.dma_start(gamma_bc[:, :], gamma.rearrange("(a n) -> a n", a=1).broadcast_to([P, D])).then_inc(ld, 16)
            sp.dma_start(beta_bc[:, :], beta.rearrange("(a n) -> a n", a=1).broadcast_to([P, D])).then_inc(ld, 16)
            with sp.Fori(0, B) as b:
                for c in range(NC):
                    sp.wait_ge(res_ok, NC * b + c + 1)
                    sp.dma_start(out[bass.ds(b, 1), c * P:c * P + P, :].rearrange("o p d -> (o p) d"), res[c][:, :]).then_inc(stored, 16)
            sp.wait_ge(stored, 16 * TILES)

        @block.tensor
        def _(pe):
            pe.wait_ge(ld, 96)
            for n, w in enumerate((wk, wo)):
                for kc in range(DC):
                    if n or kc >= 2:
                        pe.wait_ge(wT_ok, DC * n + kc - 1)
                    for hc in range(DC):
                        last = nc.tensor.transpose(pA[:, kc % 2, hc * P:hc * P + P], w[:, kc, hc * P:hc * P + P], ident[:, :])
                    last.then_inc(wT_ps, 1)
            pe.wait_ge(wT_ok, 2 * DC)
            pe.wait_ge(sums_ok, DC)
            for c in range(DC):
                last = nc.tensor.matmul(pB[0:R, 0, :], sumsT[:, c, :], wkT[:, c, :], start=(c == 0), stop=(c == DC - 1))
            last.then_inc(key_ps, 1)
            pe.wait_ge(sc_ok, 1)
            nc.tensor.transpose(pC[0:1, 0, 0:R], score[:, :], ident[0:R, 0:R]).then_inc(sc_ps, 1)
            pe.wait_ge(sm, 6)
            pe.wait_ge(ones_ok, 3)
            nc.tensor.matmul(pD[:, 0, 0:R], ones_row[:, :], srow[:, :, :].rearrange("o b n -> o (b n)"), start=True, stop=True).then_inc(at_ps, 1)
            pe.wait_ge(att_ok, 1)
            for kc in range(DC):
                for c in range(DC):
                    last = nc.tensor.matmul(pC[:, 1, kc * B:kc * B + B], woT[:, c, kc * P:kc * P + P], attT[:, c, :],
                                            start=(kc == 0 and c == 0), stop=(c == DC - 1), skip_group_check=True)
            last.then_inc(pj_ps, 1)
            pe.wait_ge(xp_ok, B * DC)
            for b in range(B):
                for tc in range(NC):
                    if b >= 1:
                        pe.wait_ge(x_ok, NC * (b - 1) + tc + 1)
                    for bank, src in ((pA, xp), (pB, xT)):
                        for c in range(DC):
                            last = nc.tensor.matmul(bank[:, tc, c * P:c * P + P], src[:, c, b, tc * P:tc * P + P], ident[:, :],
                                                    start=(c == 0), stop=(c == DC - 1), skip_group_check=True)
                    last.then_inc(y_ps, 1)

        @block.scalar
        def _(act):
            act.wait_ge(key_ps, 1)
            nc.scalar.activation(key_sq[:, :], pB[0:R, 0, :], ACT.Square, accum_out=key_ss[:, :]).then_inc(sq_ok, 1)
            act.wait_ge(sq_ok, 1)
            act.wait_ge(ones_ok, 3)
            nc.scalar.activation(key_rstd[:, :], key_ss[:, :], ACT.Ln, bias=eps_d[0:R, 0:1]).then_inc(rs_ok, 1)
            act.wait_ge(rs_ok, 1)
            nc.scalar.activation(key_rstd[:, :], key_rstd[:, :], ACT.Exp, scale=-0.5).then_inc(rs_ok, 1)
            act.wait_ge(sm, 2)
            nc.scalar.activation(srow[:, :, :], srow[:, :, :], ACT.Exp).then_inc(sm, 1)
            with act.Fori(0, B) as b:
                for tc in range(NC):
                    act.wait_ge(mv_ok, NC * b + tc + 1)
                    nc.scalar.activation(ln_rstd[tc][:, :], mv[tc][:, 1:2], ACT.Ln, bias=eps_1[:, 0:1]).then_inc(rstd_ok, 1)
                    act.wait_ge(rstd_ok, 2 * (NC * b + tc) + 1)
                    nc.scalar.activation(ln_rstd[tc][:, :], ln_rstd[tc][:, :], ACT.Exp, scale=-0.5).then_inc(rstd_ok, 1)
                    act.wait_ge(shift_ok, NC * b + tc + 1)
                    act.wait_ge(g_ok, NC * b)
                    nc.scalar.activation(ln[tc][:, :], pA[:, tc, :], ACT.Identity, bias=ln_shift[tc][:, 0:1],
                                         scale=ln_rstd[tc][:, 0:1]).then_inc(ln_ok, 1)

        @block.vector
        def _(dve):
            nc.vector.memset(ones_row[:, :], 1.0).then_inc(ones_ok, 1)
            nc.vector.memset(eps_d[:, :], D * EPS).then_inc(ones_ok, 1)
            nc.vector.memset(eps_1[:, :], EPS).then_inc(ones_ok, 1)
            for c in range(DC):
                nc.vector.tensor_reduce(sumsT[:, c, :].rearrange("p (b n) -> p b n", b=B),
                                        xT[:, c, :, :].rearrange("p b (n t) -> p b n t", n=NB), AX.X, ALU.add).then_inc(sums_ok, 1)
            dve.wait_ge(ld, 96)
            nc.vector.tensor_tensor(query[:, :], query[:, :], rms_bc[:, :], ALU.mult).then_inc(qw_ok, 1)
            for n, w in enumerate((wkT, woT)):
                for kc in range(DC):
                    dve.wait_ge(wT_ps, DC * n + kc + 1)
                    nc.vector.tensor_copy(w[:, :, kc * P:kc * P + P], pA[:, kc % 2, :].rearrange("p (h k) -> p h k", h=DC)).then_inc(wT_ok, 1)
            dve.wait_ge(sq_ok, 1)
            dve.wait_ge(qw_ok, 1)
            nc.vector.tensor_tensor(key_q[:, :], pB[0:R, 0, :], query[:, :], ALU.mult).then_inc(dot_ok, 1)
            dve.wait_ge(dot_ok, 1)
            nc.vector.tensor_reduce(key_dot[:, :], key_q[:, :], AX.X, ALU.add).then_inc(dot_ok, 1)
            dve.wait_ge(dot_ok, 2)
            dve.wait_ge(rs_ok, 2)
            nc.vector.tensor_scalar(score[:, :], key_dot[:, :], key_rstd[:, 0:1], D ** 0.5, ALU.mult, ALU.mult).then_inc(sc_ok, 1)
            dve.wait_ge(sc_ps, 1)
            nc.vector.tensor_reduce(smax[:, :], pC[0:1, 0, 0:R].rearrange("o (b n) -> o b n", b=B), AX.X, ALU.max).then_inc(sm, 1)
            dve.wait_ge(sm, 1)
            nc.vector.tensor_tensor(srow[:, :, :], pC[0:1, 0, 0:R].rearrange("o (b n) -> o b n", b=B),
                                    smax[:, :].unsqueeze(2).broadcast_to([1, B, NB]), ALU.subtract).then_inc(sm, 1)
            dve.wait_ge(sm, 3)
            nc.vector.tensor_reduce(sden[:, :], srow[:, :, :], AX.X, ALU.add).then_inc(sm, 1)
            dve.wait_ge(sm, 4)
            nc.vector.reciprocal(sden[:, :], sden[:, :]).then_inc(sm, 1)
            dve.wait_ge(sm, 5)
            nc.vector.tensor_tensor(srow[:, :, :], srow[:, :, :], sden[:, :].unsqueeze(2).broadcast_to([1, B, NB]), ALU.mult).then_inc(sm, 1)
            dve.wait_ge(at_ps, 1)
            dve.wait_ge(sums_ok, DC)
            for c in range(DC):
                nc.vector.tensor_tensor(weighted[:, c, :, :].rearrange("p b n -> p (b n)"), sumsT[:, c, :], pD[:, 0, 0:R], ALU.mult).then_inc(wt_ok, 1)
            dve.wait_ge(wt_ok, DC)
            nc.vector.tensor_reduce(attT[:, :, :], weighted[:, :, :, :], AX.X, ALU.add).then_inc(att_ok, 1)
            dve.wait_ge(pj_ps, 1)
            nc.vector.tensor_copy(projT[:, :, :], pC[:, 1, 0:DC * B].rearrange("p (c b) -> p c b", c=DC)).then_inc(pj_ok, 1)
            dve.wait_ge(pj_ok, 1)
            for c in range(DC):
                for b in range(B):
                    nc.vector.tensor_scalar(xp[:, c, b, :], xT[:, c, b, :], projT[:, c, b:b + 1], None, ALU.add).then_inc(xp_ok, 1)
            with dve.Fori(0, B) as b:
                for tc in range(NC):
                    n = NC * b + tc
                    dve.wait_ge(y_ps, n + 1)
                    nc.vector.bn_stats(stats[tc][:, :], pA[:, tc, :]).then_inc(st_ok, 1)
                    dve.wait_ge(st_ok, n + 1)
                    nc.vector.memset(tick[:, :], 0.0).then_inc(ticked, 1)
                    nc.vector.bn_aggr(mv[tc][:, :], stats[tc][:, :]).then_inc(mv_ok, 1)
                    dve.wait_ge(rstd_ok, 2 * n + 2)
                    nc.vector.scalar_tensor_tensor(out=ln_shift[tc][:, :], in0=mv[tc][:, 0:1], scalar=-1.0, in1=ln_rstd[tc][:, :],
                                                   op0=ALU.mult, op1=ALU.mult).then_inc(shift_ok, 1)
                    dve.wait_ge(g_ok, n + 1)
                    dve.wait_ge(res_ok, NC * b)
                    nc.vector.tensor_tensor(ln_x[tc][:, :], pB[:, tc, :], ln_g[tc][:, :], ALU.add).then_inc(x_ok, 1)

        @block.gpsimd
        def _(pool):
            with pool.Fori(0, B) as b:
                for tc in range(NC):
                    n = NC * b + tc
                    pool.wait_ge(ln_ok, n + 1)
                    pool.wait_ge(x_ok, NC * b)
                    pool.wait_ge(ld, 96)
                    nc.gpsimd.tensor_tensor(ln_g[tc][:, :], ln[tc][:, :], gamma_bc[:, :], ALU.mult).then_inc(g_ok, 1)
                    pool.wait_ge(x_ok, n + 1)
                    pool.wait_ge(stored, 16 * NC * b)
                    nc.gpsimd.tensor_tensor(res[tc][:, :], ln_x[tc][:, :], beta_bc[:, :], ALU.add).then_inc(res_ok, 1)


_INS = ['x', 'cond_2048', 'L0_cond_Wq', 'L0_cond_Wk', 'L0_cond_Wv', 'L0_cond_b', 'L1_cond_W_emb', 'L1_cond_b_emb', 'L1_cond_g_norm',
        'L1_cond_W_qkv', 'L1_cond_g_q', 'L1_cond_g_k', 'L1_cond_W_out', 'L2_cond_W_ih', 'L2_cond_W_hh', 'L2_cond_b_ih', 'L2_cond_b_hh',
        'L3_cond_rms_weight', 'L3_cond_Wk', 'L3_cond_Wo', 'L3_cond_ln_gamma', 'L3_cond_ln_beta']


def kernel(**inputs):
    import numpy as _np
    import concourse.bacc as _bacc
    from concourse import mybir as _mybir
    from concourse.bass_utils import run_bass_kernel_spmd as _run

    nc = _bacc.Bacc("TRN2", target_bir_lowering=False, num_devices=1)
    arrays, args = {}, []
    for name in _INS:
        a = _np.ascontiguousarray(inputs[name])
        arrays[f"in_{name}_dram"] = a
        args.append(nc.dram_tensor(f"in_{name}_dram", a.shape, _mybir.dt.from_np(a.dtype), kind="ExternalInput").ap())
    args.append(nc.dram_tensor("out_0_dram", (B, N, D), F32, kind="ExternalOutput").ap())
    build(nc, *args)
    r = _run(nc, [arrays], core_ids=[0])
    return r.results[0]["out_0_dram"]
```

```python
from contextlib import ExitStack

import numpy as np

import concourse.bass as bass
from concourse import mybir

F32 = mybir.dt.float32
F16 = mybir.dt.float16
ALU = mybir.AluOpType
ACT = mybir.ActivationFunctionType
AX = mybir.AxisListType

P = 128
B, N, D = 8, 256, 512
H = 16
DH0 = N // H
DH1 = D // H
NC, DC = N // P, D // P
G = H // 4
MC = 3 * DC
NB = 8
TB = N // NB
EPS = 1e-6

QS = 32.0
LOGIT0 = 1.0 / (QS * QS * DH0 ** 0.5)
LOGIT1 = 1.0 / (QS * QS * DH1 ** 0.5)
ROW = 4096.0
MASKED = 60000.0
HS = 2.0 ** 11
WS = 2.0 ** 10
GS = HS * WS
IS = 2.0 ** 6


def build(nc, x, cond, Wq0, Wk0, Wv0, b0, W_emb, b_emb, g_norm, W_qkv, g_q, g_k, W_out,
          W_ih, W_hh, b_ih, b_hh, rms_w, Wk3, Wo3, gamma, beta, out):
    top = ExitStack()
    with top:
        def sem(name):
            return top.enter_context(nc.semaphore(name))

        def sb(ctx, name, shape, dt=F32):
            return ctx.enter_context(nc.sbuf_tensor(name, shape, dt))

        def scratch(name, shape, dt):
            return nc.dram_tensor(name, shape, dt, kind="Internal").ap()

        mask_rows = scratch("mask_rows", (B, 3, D), F16)
        parts0 = scratch("parts0", (4, H, DH0, D), F16)
        parts1 = scratch("parts1", (4, H, DH1, N), F16)

        pA, pB, pC, pD = [top.enter_context(nc.psum_tensor(f"bank_pair_{n}", [P, 2, 512], F32)) for n in "ABCD"]

        xT = sb(top, "xT", [P, DC, B, N])
        ident = sb(top, "ident", [P, P])
        condT = sb(top, "condT", [P, DC, B])
        rep = sb(top, "rep", [P, 2, H, D], F16)
        w_in = sb(top, "w_in", [P, 2, DC, 3 * D], F16)
        w_ih = (w_in, sem("w_ih_ld"), sem("w_ih_hi"), sem("w_ih_lo"))

        attention(nc, sem, sb, x, cond, Wq0, Wk0, Wv0, b0, W_emb, b_emb, g_norm, W_qkv, g_q, g_k, W_out,
                  mask_rows, parts0, parts1, pA, pB, pC, pD, xT, ident, condT, rep, W_ih, w_ih)
        woT = sb(top, "woT", [P, DC, D])
        block_sums = sb(top, "block_sums", [P, DC, B, NB])
        query_c, rms_c, beta_c = (sb(top, n, [P, DC]) for n in ("query_c", "rms_c", "beta_c"))
        gamma_bc = sb(top, "gamma_bc", [P, D])
        norm = (query_c, rms_c, beta_c, gamma_bc, sem("norm_ld"))
        norm_from = (cond, rms_w, beta, gamma)
        recurrence(nc, sem, sb, W_ih, W_hh, b_ih, b_hh, Wk3, Wo3, pA, pB, pC, pD, xT, ident, condT, rep, w_ih, woT, block_sums,
                   norm, norm_from)
        block_attention(nc, sem, sb, out, pA, pB, pC, pD, xT, ident, key_weights(rep), woT, block_sums, norm, w_in)


def as_f32(rep):
    return rep[:, :, :, :].rearrange("p n h d -> p (n h d)").bitcast(F32)


def key_weights(rep):
    start = DC * 3 * D
    return as_f32(rep)[:, start:start + DC * D].rearrange("p (c n) -> p c n", c=DC)


def attention(nc, sem, sb, x, cond, Wq0, Wk0, Wv0, b0, W_emb, b_emb, g_norm, W_qkv, g_q, g_k, W_out,
              mask_rows, parts0, parts1, pA, pB, pC, pD, xT, ident, condT, rep, W_ih, w_ih):
    w_in, w_ih_ld, w_ih_hi, w_ih_lo = w_ih
    with ExitStack() as ctx:
        def t(name, shape, dt=F32):
            return sb(ctx, name, shape, dt)

        W0T = t("W0T", [P, 3, NC, N])
        wqkv = t("wqkv", [P, DC, 3 * D])
        wout = t("wout", [P, DC, D])
        film_scale = t("film_scale", [P, DC, B])
        film_shift = t("film_shift", [P, DC, B])
        head_ones = t("head_ones", [P, P])
        ones32 = t("ones32", [P, 32])
        row_const = t("row_const", [P, P], F16)
        gq = t("gq", [P, 1])
        gk = t("gk", [P, 1])
        words = w_in[:, :, :, :].rearrange("p s c n -> p (s c n)").bitcast(F32)
        ends = np.cumsum([NC * D, D, 2 * D, DC * H * 32, D, NC * D]).tolist()
        xs, mask_bc, y_pads, v_aug, sums, y = (words[:, start:end] for start, end in zip([0] + ends[:-1], ends))
        xs, y = (tile.rearrange("p (c d) -> p c d", c=NC) for tile in (xs, y))
        y_pads = y_pads.rearrange("p (n d) -> p n d", n=2)
        v_aug = v_aug.rearrange("p (c h d) -> p c h d", c=DC, h=H)
        parts = t("parts", [P, 4, NC, D], F16)
        part = [parts[:, n, :, :] for n in range(4)]
        q_hi, q_lo, k_hi, k_lo = part
        y_pad = [y_pads[:, n, :] for n in range(2)]
        kf = y_pads
        q_rep = rep[:, 0, :, :]
        k_rep = rep[:, 1, :, :]
        probs = [t(f"probs{n}", [P, 4, D]) for n in range(2)]
        head_max = t("head_max", [P, H * DC])
        max_row = t("max_row", [H * DC, P], F16)
        x1 = t("x1", [P, NC, D])
        sq_sum = t("sq_sum", [P, NC])
        rstd = t("rstd", [P, NC])
        xn = t("xn", [P, NC, D])
        xnT = t("xnT", [P, DC, N])
        sq = [t(f"sq{n}", [P, N]) for n in range(2)]
        head_rstd = [t(f"head_rstd{n}", [P, N]) for n in range(2)]
        qn = [t(f"qn{n}", [P, N]) for n in range(2)]
        hi1 = parts[:, 0:2, :, :].rearrange("p a c (e n) -> p a (c e) n", e=2)
        lo1 = parts[:, 2:4, :, :].rearrange("p a c (e n) -> p a (c e) n", e=2)
        q1_rep = t("q1_rep", [P, H, N], F16)
        k1_rep = t("k1_rep", [P, H, N], F16)
        max1_rows = t("max1_rows", [P, H, N], F16)
        v1 = t("v1", [P, NC, D])
        head_max1 = t("head_max1", [P, H * NC])
        max1_row = t("max1_row", [H * NC, P], F16)
        inv_sum = t("inv_sum", [P, N])
        tick = t("tick", [P, 1])
        eps_d = t("eps_d", [P, 1])
        eps_h = t("eps_h", [P, 1])
        oT = t("oT", [P, DC, N])

        wemb = [p[:, :, :].rearrange("p a b -> p (a b)").rearrange("p (c n) -> p c n", c=2) for p in probs]
        bemb_c = t("bemb_c", [P, 2 * DC])
        gn_c = t("gn_c", [P, DC])
        film = t("film", [P, 2 * DC, B])
        bcol = t("bcol", [P, 1])
        bcol16 = t("bcol16", [P, 1], F16)
        low_sel = t("low_sel", [P, 1])
        brow = t("brow", [P, 1])

        c_cond, c_w0, c_emb, c_bias, c_vec, c_big, ld_x = (sem(n) for n in ("c_cond", "c_w0", "c_emb", "c_bias", "c_vec", "c_big", "ld_x"))
        c_zero, c_fill, c_diag, c_rows, c_rows_out, c_gains = (sem(n) for n in ("c_zero", "c_fill", "c_diag", "c_rows", "c_rows_out", "c_gains"))
        c_w0t, c_condt, c_copied, c_film, c_film_out, c_b, c_later = (
            sem(n) for n in ("c_w0t", "c_condt", "c_copied", "c_film", "c_film_out", "c_b", "c_later"))

        with ExitStack() as prep:
            w0 = [w[:, :].rearrange("p (c n) -> p c n", c=NC) for w in (y_pad[0], y_pad[1], sums)]
            cond_sb = mask_bc[0:B, :]
            rows = y[0:B, :, :].rearrange("p a b -> p (a b)").bitcast(F16)[:, 0:3 * D].rearrange("p (r d) -> p r d", r=3)
            block = prep.enter_context(nc.Block())

            @block.sync
            def _(sp):
                for n, w in enumerate((Wq0, Wk0, Wv0)):
                    sp.dma_start(w0[n], w.rearrange("(c p) n -> p c n", p=P)).then_inc(c_w0, 16)
                sp.dma_start(cond_sb, cond).then_inc(c_cond, 16)
                sp.dma_start(xs[:, :, :], x[bass.ds(0, 1), :, :].rearrange("o (c p) d -> p (o c) d", p=P)).then_inc(ld_x, 16)
                we = W_emb.rearrange("(c p) n -> p c n", p=P)
                for n in range(2):
                    sp.dma_start(wemb[n], we[:, 2 * n:2 * n + 2, :]).then_inc(c_emb, 16)
                sp.wait_ge(c_rows, 2)
                sp.dma_start(mask_rows, rows[:, :, :]).then_inc(c_rows_out, 16)

            @block.scalar
            def _(act):
                nc.scalar.preload_act_table_set("natural_log_exp_and_others")

            @block.gpsimd
            def _(pool):
                pool.wait_ge(c_zero, 2)
                pool.affine_select(out=ident[:, :], in_=ident[:, :], compare_op=ALU.not_equal, fill=1.0,
                                   base=0, pattern=[[-1, P]], channel_multiplier=1).then_inc(c_diag, 1)
                pool.affine_select(out=low_sel[:, :], in_=low_sel[:, :], compare_op=ALU.not_equal, fill=1.0,
                                   base=-66, pattern=[[0, 1]], channel_multiplier=1).then_inc(c_diag, 1)
                for row in (65, 66):
                    pool.dma_start(bcol[row:row + 1, :], b0.rearrange("(a n) -> a n", a=1)).then_inc(c_bias, 16)
                pool.wait_ge(c_diag, 2)
                nc.gpsimd.memset(k_rep[:, :, :].bitcast(F32), 0.0).then_inc(c_fill, 1)

            @block.vector
            def _(dve):
                for tile in (ident, low_sel, head_ones, row_const):
                    nc.vector.memset(tile[:, :], 0.0).then_inc(c_zero, 1)
                nc.vector.memset(ones32[:, :], 1.0).then_inc(c_fill, 1)
                nc.vector.memset(eps_d[:, :], D * EPS).then_inc(c_fill, 1)
                nc.vector.memset(eps_h[:, :], DH1 * EPS).then_inc(c_fill, 1)
                nc.vector.memset(bcol[64:65, :], ROW).then_inc(c_fill, 1)
                dve.wait_ge(c_zero, 4)
                nc.vector.memset(row_const[0:1, :], ROW).then_inc(c_fill, 1)
                for j in range(4):
                    nc.vector.memset(head_ones[32 * j:32 * j + 32, 32 * j:32 * j + 32], 1.0).then_inc(c_fill, 1)
                nc.vector.memset(q_rep[:, :, :].bitcast(F32), 0.0).then_inc(c_fill, 1)
                dve.wait_ge(c_cond, 16)
                nc.vector.tensor_scalar(rows[:, 0, :], cond_sb[:, :], MASKED, -MASKED, ALU.mult, ALU.add).then_inc(c_rows, 1)
                nc.vector.tensor_copy(rows[:, 1:3, :], cond_sb[:, :].unsqueeze(1).broadcast_to([B, 2, D])).then_inc(c_rows, 1)
                dve.wait_ge(c_w0t, 1)
                for n in range(3):
                    src = (pA, pA, pB)[n][:, n % 2, :].rearrange("p (c o) -> p c o", c=NC)
                    nc.vector.tensor_copy(W0T[:, n, :, :], src).then_inc(c_copied, 1)
                dve.wait_ge(c_condt, 1)
                nc.vector.tensor_copy(condT[:, :, :], pC[:, 0, 0:DC * B].rearrange("p (c b) -> p c b", c=DC)).then_inc(c_copied, 1)

            @block.tensor
            def _(pe):
                pe.wait_ge(c_diag, 1)
                pe.wait_ge(c_w0, 48)
                for n in range(3):
                    for oc in range(NC):
                        for cc in range(NC):
                            last = nc.tensor.transpose((pA, pA, pB)[n][:, n % 2, cc * N + oc * P:cc * N + oc * P + P],
                                                       w0[n][:, oc, cc * P:cc * P + P], ident[:, :])
                last.then_inc(c_w0t, 1)
                pe.wait_ge(c_cond, 16)
                for c in range(DC):
                    last = nc.tensor.transpose(pC[:, 0, c * B:c * B + B], cond_sb[:, c * P:c * P + P], ident[0:B, 0:B])
                last.then_inc(c_condt, 1)

        ld_x1, ld_mask, ld_rows, st_parts, ld_rep, ld_max = (
            sem(n) for n in ("ld_x1", "ld_mask", "ld_rows", "st_parts", "ld_rep", "ld_max"))
        ld_y = [sem(f"ld_y{n}") for n in range(2)]
        q_ps, k_ps, v_ps, q_hi_ok, q_lo_ok, kf_ok, k_hi_ok, k_lo_ok, v_ok = (
            sem(n) for n in ("q_ps", "k_ps", "v_ps", "q_hi_ok", "q_lo_ok", "kf_ok", "k_hi_ok", "k_lo_ok", "v_ok"))
        s_ps, s_max, neg_max, max_ps, max_ok, st_ps, exp_ok, pv_ps, sums_ok, inv_ok, y_ok, x1_ok = (
            sem(n) for n in ("s_ps", "s_max", "neg_max", "max_ps", "max_ok", "st_ps", "exp_ok", "pv_ps", "sums_ok", "inv_ok", "y_ok", "x1_ok"))
        ss_ok, sse_ok, hln_ok, rstd_ok, xn_ok, xnT_ps, xnT_ok, qk_ps, sq_ok, hss_ps, hrs_ok, qn_ok, hi_ok, lo_ok, v1_ps, v1_ok = (
            sem(n) for n in ("ss_ok", "sse_ok", "hln_ok", "rstd_ok", "xn_ok", "xnT_ps", "xnT_ok", "qk_ps", "sq_ok", "hss_ps", "hrs_ok", "qn_ok",
                             "hi_ok", "lo_ok", "v1_ps", "v1_ok"))
        st_parts1, ld_rep1, s1_ps, s1_max, neg_max1, max1_ps, max1_ok, ld_max1, st1_ps, exp1_ok, pv1_ps, inv1_ok, log1_ok, oT_ok, res_ps, xT_ok = (
            sem(n) for n in ("st_parts1", "ld_rep1", "s1_ps", "s1_max", "neg_max1", "max1_ps", "max1_ok", "ld_max1", "st1_ps",
                             "exp1_ok", "pv1_ps", "inv1_ok", "log1_ok", "oT_ok", "res_ps", "xT_ok"))
        ticked, log0_ok, x1_last, ld_rep1_end = (sem(n) for n in ("ticked", "log0_ok", "x1_last", "ld_rep1_end"))
        block = ctx.enter_context(nc.Block())
        pair = [pA, pB]
        pair1 = [pC, pD]
        qk_bank = [pC[:, 0, :], pC[:, 1, :], pD[:, 1, :]]
        U0 = 2 * H
        U1 = H // 2
        M8 = 2 * DC

        def beside():
            free = iter(range(U0))
            for m in range(M8):
                yield "qk", m
                for _ in range({4: 2, 5: 2, 6: 2, 7: 2}.get(m, 0)):
                    yield "max", next(free)
            yield "qk", M8
            for n in range(DC * NC):
                yield "v", n
                if n in (0, 1, 2, 3, 4, 5, 6):
                    yield "max", next(free)
            for u in range(U1):
                yield "max1", u
                if u in ():
                    yield "max", next(free)
            yield "row1", 0
            for _ in range(4):
                yield "max", next(free)
            for h in range(H):
                yield "score1", h
                if h in (1, 2, 3, 5, 6, 7, 8, 9, 10, 11, 12, 13, 14):
                    yield "max", next(free)
                if h % 4 == 3 and h >= 7:
                    yield "weigh1", h // 4 - 1
                if h % 4 == 1 and h >= 9:
                    yield "inv1", h // 4 - 2
                if h % 4 == 2 and h >= 9:
                    yield "out1", h // 4 - 2
            yield "inv1", G - 2
            yield "weigh1", G - 1
            yield "out1", G - 2
            yield "inv1", G - 1
            for u in free:
                yield "max", u
            yield "row", 0
            yield "out1", G - 1
        BESIDE = list(beside())
        ALONE0 = [("max", u) for u in range(U0)] + [("row", 0)]
        ALONE1 = [step for step in BESIDE if step[0] not in ("max", "row")]
        ROW1 = ALONE1.index(("row1", 0))
        w_ih_f32 = as_f32(rep)[:, 0:DC * 3 * D].rearrange("p (c n) -> p c n", c=DC)

        @block.sync
        def _(sp):
            def load_x(b, first=False):
                if not first:
                    sp.wait_ge(v_ps, b)
                    sp.dma_start(xs[:, :, :], x[bass.ds(b, 1), :, :].rearrange("o (c p) d -> p (o c) d", p=P)).then_inc(ld_x, 16)
                    sp.wait_ge(kf_ok, b)
                sp.dma_start(mask_bc[:, :], cond[bass.ds(b, 1), :].broadcast_to([P, D])).then_inc(ld_mask, 16)

            def load_x1(b, first=False):
                if not first:
                    sp.wait_ge(res_ps, b)
                sp.dma_start(x1[:, :, :], x[bass.ds(b, 1), :, :].rearrange("o (c p) d -> p (o c) d", p=P)).then_inc(ld_x1, 16)

            def spread(b, first=False):
                if not first:
                    sp.wait_ge(st_ps, b * U0)
                sp.dma_start(k_rep[64:67, :, :], mask_rows[bass.ds(b, 1), :, :].rearrange("o r t -> (o r) t").unsqueeze(1)
                             .broadcast_to([3, H, D])).then_inc(ld_rows, 16)
                for i, (rep0, rows) in enumerate(((q_rep, ((0, 0), (0, 32), (1, 16), (1, 48))), (k_rep, ((2, 0), (2, 16), (3, 32), (3, 48))))):
                    for n, ready in ((0, q_hi_ok), (1, q_lo_ok)) if i == 0 else ((2, k_hi_ok), (3, k_lo_ok)):
                        sp.wait_ge(ready, b + 1)
                        sp.dma_start(parts0[n].rearrange("(c h) d t -> (h d) c t", c=2), part[n][:, :, :]).then_inc(st_parts, 16)
                    sp.wait_ge(st_parts, b * 64 + (i + 1) * 32)
                    for n, row in rows:
                        sp.dma_start(rep0[row:row + DH0, :, :], parts0[n].rearrange("h d t -> d h t")).then_inc(ld_rep, 16)

            def place_max(b):
                sp.wait_ge(max_ok, b + 1)
                sp.dma_start(q_rep[96:97, :, :].rearrange("o h (c t) -> o (h c) t", c=DC), max_row[:, :]).then_inc(ld_max, 16)

            def move_y(b):
                for g in range(G):
                    sp.wait_ge(y_ok, b * G + g + 1)
                    for j in range(4):
                        r = (4 * g + j) * DH0
                        sp.dma_start(y[r % P:r % P + DH0, r // P, :], y_pad[g % 2][32 * j:32 * j + DH0, :]).then_inc(ld_y[g % 2], 16)

            def spread1(e):
                Q, K = ((0, 0), (0, 64), (1, 32), (1, 96)), ((2, 0), (2, 32), (3, 64), (3, 96))
                pieces = ((0, range(0, DC), q1_rep, Q, ld_rep1), (1, range(0, DC // 2), k1_rep, K, ld_rep1), (1, range(DC // 2, DC), k1_rep, K, ld_rep1_end))
                stored = 0
                for n, chunks, rep1, rows, done in pieces:
                    c0, c1 = chunks[0], chunks[-1] + 1
                    sp.wait_ge(hi_ok, e * M8 + (n * DC + c1))
                    sp.wait_ge(lo_ok, e * M8 + (n * DC + c1))
                    for m, tile in enumerate((hi1, lo1)):
                        sp.dma_start(parts1[2 * n + m][4 * c0:4 * c1, :, :].rearrange("(c h) d t -> (h d) c t", h=4),
                                     tile[:, n, c0:c1, :]).then_inc(st_parts1, 16)
                    stored += 32
                    sp.wait_ge(st_parts1, e * 96 + stored)
                    for part1, row in rows:
                        sp.dma_start(rep1[row:row + DH1, 4 * c0:4 * c1, :], parts1[part1][4 * c0:4 * c1, :, :].rearrange("h d t -> d h t")).then_inc(done, 16)
                sp.wait_ge(max1_ok, e + 1)
                sp.dma_start(max1_rows[0:1, :, :].rearrange("o h (c t) -> o (h c) t", c=NC), max1_row[:, :]).then_inc(ld_max1, 16)

            load_x(0, first=True)
            sp.wait_ge(c_rows_out, 16)
            spread(0, first=True)
            load_x1(0, first=True)
            sp.dma_start(wqkv[:, :, :], W_qkv.rearrange("(c p) n -> p c n", p=P)).then_inc(c_big, 16)
            sp.dma_start(wout[:, :, :], W_out.rearrange("(c p) n -> p c n", p=P)).then_inc(c_big, 16)
            place_max(0)
            with sp.Fori(0, B - 1) as e:
                load_x(e + 1)
                move_y(e)
                spread(e + 1)
                spread1(e)
                place_max(e + 1)
                load_x1(e + 1)
            move_y(B - 1)
            sp.wait_ge(st_ps, B * U0)
            sp.dma_start(w_ih_f32, W_ih.rearrange("(c p) n -> p c n", p=P)).then_inc(w_ih_ld, 16)
            spread1(B - 1)

        @block.tensor
        def _(pe):
            def project(b, first=False):
                pe.wait_ge(ld_x, b * 16 + 16)
                if not first:
                    pe.wait_ge(exp_ok, b * U0)
                for n, (bank, done) in enumerate(((pA, q_ps), (pB, k_ps))):
                    for oc in range(NC):
                        for c in range(NC):
                            last = nc.tensor.matmul(bank[:, oc, :], W0T[:, n, c, oc * P:oc * P + P], xs[:, c, :],
                                                    start=(c == 0), stop=(c == NC - 1))
                    last.then_inc(done, 1)
                if not first:
                    pe.wait_ge(y_ok, b * G)
                project_v(0)

            def project_v(half):
                for tc in range(2 * half, 2 * half + 2):
                    for c in range(NC):
                        last = nc.tensor.matmul(pC[:, tc // 2, (tc % 2) * N:(tc % 2) * N + N], xs[:, c, tc * P:tc * P + P],
                                                W0T[:, 2, c, :], start=(tc % 2 == 0 and c == 0), stop=(c == NC - 1),
                                                skip_group_check=True)
                if half == 1:
                    last.then_inc(v_ps, 1)

            def max_scores(b, u):
                if u == 0:
                    pe.wait_ge(ld_rep, b * 128 + 128)
                    pe.wait_ge(ld_rows, b * 16 + 16)
                    pe.wait_ge(q_lo_ok, b + 1)
                if u == 1:
                    pe.wait_ge(kf_ok, b + 1)
                if u >= 2:
                    pe.wait_ge(s_max, b * U0 + (u - 1))
                for qc in range(2):
                    t0 = (2 * (u % 2) + qc) * P
                    last = nc.tensor.matmul(pair[u % 2][:, qc, :], q_rep[0:96, u // 2, t0:t0 + P], k_rep[0:96, u // 2, :],
                                            start=True, stop=True)
                last.then_inc(s_ps, 1)

            def max_to_row(b):
                pe.wait_ge(neg_max, b + 1)
                nc.tensor.matmul(pA[0:H * DC, 0, 0:P], head_max[:, :], ident[:, :], start=True, stop=True).then_inc(max_ps, 1)

            def attend(b, e=None):
                if e is not None:
                    residual(e, 0)
                    residual(e, 1)
                pe.wait_ge(ld_max, b * 16 + 16)
                pe.wait_ge(v_ok, b + 1)

                def unit(u):
                    return u // 2 // DC, u // 2 % DC, slice(u % 2 * N, u % 2 * N + N)

                def weigh(u):
                    g, kc, queries = unit(u)
                    pe.wait_ge(exp_ok, b * U0 + (u + 1))
                    if u % (2 * DC) == 0 and g >= 2:
                        pe.wait_ge(y_ok, b * G + (g - 1))
                    for j in range(4):
                        last = nc.tensor.matmul(pC[32 * j:32 * j + 32, g % 2, queries], v_aug[:, kc, 4 * g + j, :],
                                                probs[u // 2 % 2][:, j, queries],
                                                start=(u % (2 * DC) == 0), stop=(kc == DC - 1), skip_group_check=True)
                    last.then_inc(pv_ps, 1)

                for u in range(U0):
                    g, kc, queries = unit(u)
                    if u >= 2:
                        pe.wait_ge(exp_ok, b * U0 + (u - 1))
                    for j in range(4):
                        h = 4 * g + j
                        last = nc.tensor.matmul(pair[u % 2][:, j // 2, (j % 2) * N:(j % 2) * N + N], k_rep[:, h, kc * P:kc * P + P],
                                                q_rep[:, h, queries], start=(j % 2 == 0), stop=True, skip_group_check=True)
                    last.then_inc(st_ps, 1)
                    if e is not None and u in (1, 3):
                        residual(e, 2 + u // 2)
                    if u >= 2:
                        weigh(u - 2)
                weigh(U0 - 2)
                weigh(U0 - 1)

            def tokens(e, last_one=False):
                pe.wait_ge(xn_ok, e * 2 + 2)
                for c in range(DC):
                    for tc in range(NC):
                        last = nc.tensor.transpose(pD[:, c // 2, (c % 2) * N + tc * P:(c % 2) * N + tc * P + P],
                                                   xn[:, tc, c * P:c * P + P], ident[:, :])
                last.then_inc(xnT_ps, 1)
                if not last_one:
                    project_v(1)
                pe.wait_ge(xnT_ok, e * DC + DC)
                if last_one:
                    pe.wait_ge(y_ok, B * G)
                else:
                    pe.wait_ge(v_ok, e + 2)

            def qk_chunk(e, m):
                if m < M8:
                    if m >= 3:
                        pe.wait_ge(qn_ok, e * M8 + (m - 2))
                    for c in range(DC):
                        last = nc.tensor.matmul(qk_bank[m % 3][:, 0:N], wqkv[:, c, m * P:m * P + P], xnT[:, c, :],
                                                start=(c == 0), stop=(c == DC - 1))
                    last.then_inc(qk_ps, 1)
                if m >= 1:
                    pe.wait_ge(sq_ok, e * M8 + m)
                    if m >= 2:
                        pe.wait_ge(hln_ok, e * M8 + (m - 1))
                    nc.tensor.matmul(pD[:, 0, 0:N], head_ones[:, :], sq[(m - 1) % 2][:, :], start=True, stop=True).then_inc(hss_ps, 1)

            def v_tokens(e, n):
                tc, c = n // DC, n % DC
                if n == 0:
                    pe.wait_ge(hln_ok, e * M8 + M8)
                if c == 0 and tc == 1:
                    pe.wait_ge(qn_ok, e * M8 + M8)
                last = nc.tensor.matmul(pD[:, tc, :], xnT[:, c, tc * P:tc * P + P], wqkv[:, c, 2 * D:3 * D],
                                        start=(c == 0), stop=(c == DC - 1))
                if n == NC * DC - 1:
                    last.then_inc(v1_ps, 1)

            def max1_scores(e, u):
                if u == 0:
                    pe.wait_ge(ld_rep1, e * 128 + 128)
                    pe.wait_ge(qn_ok, e * M8 + M8)
                elif u == 1:
                    pe.wait_ge(v1_ok, e + 1)
                else:
                    if u == U1 // 2:
                        pe.wait_ge(ld_rep1_end, e * 64 + 64)
                    pe.wait_ge(s1_max, e * U1 + (u - 1))
                for j in range(2):
                    for qc in range(NC):
                        last = nc.tensor.matmul(pair1[u % 2][:, j, qc * N:qc * N + N], q1_rep[:, 2 * u + j, qc * P:qc * P + P],
                                                k1_rep[:, 2 * u + j, :], start=(qc == 0), stop=(qc == NC - 1),
                                                skip_group_check=True)
                last.then_inc(s1_ps, 1)

            def max1_to_row(e):
                pe.wait_ge(neg_max1, e + 1)
                nc.tensor.matmul(pC[0:H * NC, 0, 0:P], head_max1[:, :], ident[:, :], start=True, stop=True).then_inc(max1_ps, 1)

            def scores1(e, h):
                if h == 0:
                    pe.wait_ge(ld_max1, e * 16 + 16)
                    pe.wait_ge(max1_ok, e + 1)
                if h >= 2:
                    pe.wait_ge(exp1_ok, e * H + (h - 1))
                for kc in range(NC):
                    o = pC[:, h % 2, kc * N:kc * N + N]
                    nc.tensor.matmul(o, k1_rep[:, h, kc * P:kc * P + P], q1_rep[:, h, :],
                                     start=(kc == 0), stop=False, skip_group_check=True)
                    last = nc.tensor.matmul(o, row_const[:, :], max1_rows[:, h, :], start=False, stop=True,
                                            skip_group_check=True)
                last.then_inc(st1_ps, 1)

            def weigh1(e, g):
                pe.wait_ge(exp1_ok, e * H + (4 * g + 4))
                if g >= 2:
                    pe.wait_ge(oT_ok, e * G + (g - 1))
                for side in range(2):
                    for kc in range(NC):
                        for j in range(4):
                            h = 4 * g + j
                            v = ones32[:, :] if side else v1[:, kc, h * DH1:h * DH1 + DH1]
                            last = nc.tensor.matmul(pD[32 * j:32 * j + 32, g % 2, side * N:side * N + N], v,
                                                    probs[g % 2][:, j, kc * N:kc * N + N],
                                                    start=(side == 0 and kc == 0), stop=(kc == NC - 1), skip_group_check=True)
                last.then_inc(pv1_ps, 1)

            def residual(e, oc):
                if oc == 0:
                    pe.wait_ge(oT_ok, e * G + G)
                o = pD[:, oc // 2, (oc % 2) * N:(oc % 2) * N + N]
                for tc in range(NC):
                    nc.tensor.matmul(o[:, tc * P:tc * P + P], x1[:, tc, oc * P:oc * P + P], ident[:, :],
                                     start=(oc % 2 == 0 and tc == 0), stop=False, skip_group_check=True)
                for c in range(DC):
                    last = nc.tensor.matmul(o, wout[:, c, oc * P:oc * P + P], oT[:, c, :], start=False, stop=(c == DC - 1),
                                            skip_group_check=True)
                if oc == DC - 1:
                    last.then_inc(res_ps, 1)

            def steps(order, e, b):
                for kind, n in order:
                    if kind == "max":
                        max_scores(b, n)
                    elif kind == "row":
                        max_to_row(b)
                    elif kind == "qk":
                        qk_chunk(e, n)
                    elif kind == "v":
                        v_tokens(e, n)
                    elif kind == "max1":
                        max1_scores(e, n)
                    elif kind == "row1":
                        max1_to_row(e)
                    elif kind == "score1":
                        scores1(e, n)
                    elif kind == "weigh1":
                        weigh1(e, n)

            def film_chunk(m):
                for k in range(DC):
                    last = nc.tensor.matmul(pD[:, 0, m * B:m * B + B], wemb[k // 2][:, k % 2, m * P:m * P + P], condT[:, k, :],
                                            start=(m == 0 and k == 0), stop=(k == DC - 1), skip_group_check=True)
                last.then_inc(c_film, 1)

            project(0, first=True)
            project_v(1)
            pe.wait_ge(c_emb, 32)
            for m in range(2 * DC):
                film_chunk(m)
            pe.wait_ge(c_b, 4)
            steps(ALONE0, None, 0)
            pe.wait_ge(c_later, 3)
            pe.wait_ge(c_big, 32)
            attend(0)
            with pe.Fori(0, B - 1) as e:
                project(e + 1)
                tokens(e)
                steps(BESIDE, e, e + 1)
                attend(e + 1, e)
            tokens(B - 1, last_one=True)
            steps(ALONE1, B - 1, None)
            for oc in range(DC):
                residual(B - 1, oc)

        @block.scalar
        def _(act):
            def q_parts(b):
                act.wait_ge(q_ps, b + 1)
                nc.scalar.activation(q_hi[:, :, :], pA[:, :, :], ACT.Copy, scale=QS).then_inc(q_hi_ok, 1)

            def kv_parts(b):
                act.wait_ge(kf_ok, b + 1)
                nc.scalar.activation(k_hi[:, :, :], kf[:, :, :], ACT.Copy).then_inc(k_hi_ok, 1)
                act.wait_ge(v_ps, b + 1)
                nc.scalar.activation(v_aug[:, :, :, 0:DH0], pC[:, :, :].rearrange("p a (b h d) -> p (a b) h d", b=2, d=DH0),
                                     ACT.Copy).then_inc(v_ok, 1)

            def max_rows(b):
                act.wait_ge(max_ps, b + 1)
                nc.scalar.activation(max_row[:, :], pA[0:H * DC, 0, 0:P], ACT.Copy).then_inc(max_ok, 1)

            def attend(b):
                for u in range(U0):
                    act.wait_ge(st_ps, b * U0 + (u + 1))
                    if u >= 4:
                        act.wait_ge(pv_ps, b * U0 + (u - 3))
                    nc.scalar.activation(probs[u // 2 % 2][:, :, u % 2 * N:u % 2 * N + N],
                                         pair[u % 2][:, :, :].rearrange("p a (b t) -> p (a b) t", b=2), ACT.Exp, scale=LOGIT0).then_inc(exp_ok, 1)
                act.wait_ge(sums_ok, b * G + G)
                nc.scalar.activation(sums[:, :], sums[:, :], ACT.Ln).then_inc(log0_ok, 1)
                act.wait_ge(log0_ok, b + 1)
                nc.scalar.activation(sums[:, :], sums[:, :], ACT.Exp, scale=-1.0).then_inc(inv_ok, 1)

            def token_rms(e):
                for c in range(NC):
                    if c < NC - 1:
                        act.wait_ge(x1_ok, e * (NC - 1) + (c + 1))
                    else:
                        act.wait_ge(x1_last, e + 1)
                    nc.scalar.activation(xn[:, c, :], x1[:, c, :], ACT.Square, accum_out=sq_sum[:, c:c + 1]).then_inc(ss_ok, 1)
                act.wait_ge(ss_ok, e * 2 + 2)
                nc.scalar.activation(rstd[:, :], sq_sum[:, :], ACT.Ln, bias=eps_d[:, 0:1]).then_inc(sse_ok, 1)
                act.wait_ge(sse_ok, e + 1)
                nc.scalar.activation(rstd[:, :], rstd[:, :], ACT.Exp, scale=-0.5).then_inc(rstd_ok, 1)

            def qk_chunk(e, m):
                def head_rms(m):
                    act.wait_ge(hss_ps, e * M8 + (m + 1))
                    if m >= 2:
                        act.wait_ge(qn_ok, e * M8 + (m - 1))
                    nc.scalar.activation(head_rstd[m % 2][:, :], pD[:, 0, 0:N], ACT.Ln, bias=eps_h[:, 0:1]).then_inc(hln_ok, 1)
                    act.wait_ge(hln_ok, e * M8 + (m + 1))
                    nc.scalar.activation(head_rstd[m % 2][:, :], head_rstd[m % 2][:, :], ACT.Exp, scale=-0.5).then_inc(hrs_ok, 1)

                def hi_part(m):
                    if m == 0 and not isinstance(e, int):
                        act.wait_ge(st_parts, e * 64 + 128)
                    act.wait_ge(qn_ok, e * M8 + (m + 1))
                    nc.scalar.activation(hi1[:, m // DC, m % DC, :], qn[m % 2][:, :], ACT.Copy).then_inc(hi_ok, 1)

                if m < M8:
                    act.wait_ge(qk_ps, e * M8 + (m + 1))
                    if m >= 2:
                        act.wait_ge(hss_ps, e * M8 + (m - 1))
                    nc.scalar.activation(sq[m % 2][:, :], qk_bank[m % 3][:, 0:N], ACT.Square).then_inc(sq_ok, 1)
                if m >= 1:
                    head_rms(m - 1)
                if m >= 2:
                    hi_part(m - 2)
                if m == M8:
                    hi_part(m - 1)

            def inverse1(e, g):
                act.wait_ge(pv1_ps, e * G + (g + 1))
                if g >= 1:
                    act.wait_ge(oT_ok, e * G + g)
                nc.scalar.activation(inv_sum[:, :], pD[:, g % 2, N:2 * N], ACT.Ln).then_inc(log1_ok, 1)
                act.wait_ge(log1_ok, e * G + (g + 1))
                nc.scalar.activation(inv_sum[:, :], inv_sum[:, :], ACT.Exp, scale=-1.0).then_inc(inv1_ok, 1)

            def steps(order, e, b):
                for kind, n in order:
                    if kind == "row":
                        max_rows(b)
                    elif kind == "qk":
                        qk_chunk(e, n)
                    elif kind == "v" and n == NC * DC - 1:
                        act.wait_ge(v1_ps, e + 1)
                        nc.scalar.activation(v1[:, :, :], pD[:, :, :], ACT.Copy).then_inc(v1_ok, 1)
                    elif kind == "row1":
                        act.wait_ge(max1_ps, e + 1)
                        nc.scalar.activation(max1_row[:, :], pC[0:H * NC, 0, 0:P], ACT.Copy).then_inc(max1_ok, 1)
                    elif kind == "score1":
                        act.wait_ge(st1_ps, e * H + (n + 1))
                        if n == 0:
                            act.wait_ge(pv_ps, e * U0 + U0)
                        if n >= 8 and n % 4 == 0:
                            act.wait_ge(pv1_ps, e * G + (n // 4 - 1))
                        nc.scalar.activation(probs[(n // 4) % 2][:, n % 4, :], pC[:, n % 2, :], ACT.Exp, scale=LOGIT1).then_inc(exp1_ok, 1)
                    elif kind == "inv1":
                        inverse1(e, n)

            q_parts(0)
            kv_parts(0)
            steps(ALONE0, None, 0)
            attend(0)
            with act.Fori(0, B - 1) as e:
                q_parts(e + 1)
                token_rms(e)
                kv_parts(e + 1)
                steps(BESIDE, e, e + 1)
                attend(e + 1)
            token_rms(B - 1)
            steps(ALONE1[:ROW1], B - 1, None)
            act.wait_ge(w_ih_ld, 16)
            act.wait_ge(pv_ps, B * U0)
            for k in range(DC):
                nc.scalar.activation(w_in[:, 0, k, :], w_ih_f32[:, k, :], ACT.Copy, scale=WS).then_inc(w_ih_hi, 1)
            steps(ALONE1[ROW1:], B - 1, None)

        @block.vector
        def _(dve):
            def q_parts(b, first=False):
                dve.wait_ge(q_hi_ok, b + 1)
                nc.vector.scalar_tensor_tensor(out=q_lo[:, :, :], in0=pA[:, :, :], scalar=QS, in1=q_hi[:, :, :],
                                               op0=ALU.mult, op1=ALU.subtract).then_inc(q_lo_ok, 1)
                if not first:
                    add_last(b - 1)
                dve.wait_ge(ld_mask, b * 16 + 16)
                dve.wait_ge(k_ps, b + 1)
                for c in range(NC):
                    last = nc.vector.scalar_tensor_tensor(out=kf[:, c, :], in0=pB[:, c, :], scalar=QS, in1=mask_bc[:, :],
                                                          op0=ALU.mult, op1=ALU.mult)
                last.then_inc(kf_ok, 1)

            def k_part(b):
                dve.wait_ge(kf_ok, b + 1)
                dve.wait_ge(k_hi_ok, b + 1)
                nc.vector.tensor_tensor(k_lo[:, :, :], kf[:, :, :], k_hi[:, :, :], ALU.subtract).then_inc(k_lo_ok, 1)

            def attend(b):
                for g in range(G):
                    dve.wait_ge(pv_ps, b * U0 + 2 * DC * (g + 1))
                    if g >= 1:
                        dve.wait_ge(y_ok, b * G + g)
                    nc.vector.memset(tick[:, :], 0.0).then_inc(ticked, 1)
                    nc.vector.stream_shuffle(sums[:, :], pC[:, g % 2, :], [16 + n % 16 for n in range(32)]).then_inc(sums_ok, 1)
                    if g < G - 1:
                        dve.wait_ge(sums_ok, b * G + (g + 1))
                        nc.vector.reciprocal(sums[:, :], sums[:, :]).then_inc(inv_ok, 1)
                    dve.wait_ge(inv_ok, b * G + (g + 1))
                    if g >= 2:
                        dve.wait_ge(ld_y[g % 2], b * 128 + 64)
                    nc.vector.tensor_tensor(y_pad[g % 2], pC[:, g % 2, :], sums[:, :], ALU.mult).then_inc(y_ok, 1)

            def add_last(e):
                for n in range(2):
                    dve.wait_ge(ld_y[n], e * 128 + 128)
                dve.wait_ge(ld_x1, e * 16 + 16)
                nc.vector.tensor_tensor(x1[:, NC - 1, :], x1[:, NC - 1, :], y[:, NC - 1, :], ALU.add).then_inc(x1_last, 1)

            def normalise(e):
                dve.wait_ge(rstd_ok, e + 1)
                for c in range(NC):
                    nc.vector.tensor_scalar(xn[:, c, :], x1[:, c, :], rstd[:, c:c + 1], D ** 0.5, ALU.mult, ALU.mult).then_inc(xn_ok, 1)

            def tokens(e):
                dve.wait_ge(xnT_ps, e + 1)
                for c in range(DC):
                    nc.vector.tensor_scalar(xnT[:, c, :], pD[:, c // 2, (c % 2) * N:(c % 2) * N + N],
                                            film_scale[:, c, bass.ds(e, 1)], film_shift[:, c, bass.ds(e, 1)],
                                            ALU.mult, ALU.add).then_inc(xnT_ok, 1)

            def qk_chunk(e, m):
                def lo_part(m):
                    dve.wait_ge(hi_ok, e * M8 + (m + 1))
                    nc.vector.tensor_tensor(lo1[:, m // DC, m % DC, :], qn[m % 2][:, :], hi1[:, m // DC, m % DC, :],
                                            ALU.subtract).then_inc(lo_ok, 1)

                dve.wait_ge(hrs_ok, e * M8 + (m + 1))
                if m >= 2:
                    dve.wait_ge(lo_ok, e * M8 + (m - 1))
                nc.vector.scalar_tensor_tensor(out=qn[m % 2][:, :], in0=qk_bank[m % 3][:, 0:N],
                                               scalar=(gq if m < DC else gk)[:, 0:1], in1=head_rstd[m % 2][:, :],
                                               op0=ALU.mult, op1=ALU.mult).then_inc(qn_ok, 1)
                if m >= 1:
                    lo_part(m - 1)
                if m == M8 - 1:
                    lo_part(m)

            def steps(order, e, b):
                for kind, n in order:
                    if kind == "max":
                        dve.wait_ge(s_ps, b * U0 + (n + 1))
                        nc.vector.tensor_reduce(head_max[:, 2 * n:2 * n + 2], pair[n % 2][:, :, :], AX.X, ALU.max).then_inc(s_max, 1)
                    elif kind == "qk" and n >= 1:
                        qk_chunk(e, n - 1)
                    elif kind == "row":
                        dve.wait_ge(s_max, b * U0 + U0)
                        nc.vector.tensor_scalar(head_max[:, :], head_max[:, :], -1.0 / ROW, None, ALU.mult).then_inc(neg_max, 1)
                    elif kind == "max1":
                        dve.wait_ge(s1_ps, e * U1 + (n + 1))
                        nc.vector.tensor_reduce(head_max1[:, 4 * n:4 * n + 4], pair1[n % 2][:, :, :].rearrange("p j (q k) -> p (j q) k", q=NC),
                                                AX.X, ALU.max).then_inc(s1_max, 1)
                    elif kind == "row1":
                        dve.wait_ge(s1_max, e * U1 + U1)
                        nc.vector.tensor_scalar(head_max1[:, :], head_max1[:, :], -1.0 / ROW, None, ALU.mult).then_inc(neg_max1, 1)
                    elif kind == "out1":
                        dve.wait_ge(inv1_ok, e * G + (n + 1))
                        nc.vector.tensor_tensor(oT[:, n, :], pD[:, n % 2, 0:N], inv_sum[:, :], ALU.mult).then_inc(oT_ok, 1)

            def residual(e):
                dve.wait_ge(res_ps, e + 1)
                dve.wait_ge(oT_ok, e * G + G)
                nc.vector.tensor_tensor(xT[:, :, bass.ds(e, 1), :].rearrange("p c o t -> p c (o t)"),
                                        pD[:, :, :].rearrange("p a (b t) -> p (a b) t", b=2), oT[:, :, :], ALU.add).then_inc(xT_ok, 1)

            dve.wait_ge(c_bias, 32)
            nc.vector.tensor_copy(bcol16[64:67, :], bcol[64:67, :]).then_inc(c_b, 1)
            dve.wait_ge(c_b, 1)
            nc.vector.tensor_tensor(brow[64:67, :], bcol16[64:67, :], low_sel[64:67, :], ALU.mult).then_inc(c_b, 1)
            dve.wait_ge(c_b, 2)
            nc.vector.tensor_tensor(brow[64:67, :], bcol[64:67, :], brow[64:67, :], ALU.subtract).then_inc(c_b, 1)
            dve.wait_ge(c_b, 3)
            nc.vector.tensor_scalar(q_rep[64:67, :, :], q_rep[64:67, :, :], brow[64:67, 0:1], None, ALU.add).then_inc(c_b, 1)
            q_parts(0, first=True)
            k_part(0)
            steps(ALONE0, None, 0)
            dve.wait_ge(c_vec, 160)
            dve.wait_ge(c_film, 2 * DC)
            nc.vector.tensor_tensor(film[:, :, :], pD[:, 0, 0:2 * DC * B].rearrange("p (c b) -> p c b", c=2 * DC),
                                    bemb_c[:, :].unsqueeze(2).broadcast_to([P, 2 * DC, B]), ALU.add).then_inc(c_film_out, 1)
            dve.wait_ge(c_film_out, 1)
            nc.vector.tensor_scalar(film_scale[:, :, :], film[:, 0:DC, :], 1.0, None, ALU.add).then_inc(c_film_out, 1)
            nc.vector.tensor_copy(film_shift[:, :, :], film[:, DC:, :]).then_inc(c_film_out, 1)
            dve.wait_ge(c_film_out, 3)
            nc.vector.tensor_tensor(film_scale[:, :, :], film_scale[:, :, :],
                                    gn_c[:, :].unsqueeze(2).broadcast_to([P, DC, B]), ALU.mult).then_inc(c_film_out, 1)
            nc.vector.tensor_scalar(gq[:, :], gq[:, :], QS * DH1 ** 0.5, None, ALU.mult).then_inc(c_gains, 1)
            nc.vector.tensor_scalar(gk[:, :], gk[:, :], QS * DH1 ** 0.5, None, ALU.mult).then_inc(c_gains, 1)
            attend(0)
            with dve.Fori(0, B - 1) as e:
                q_parts(e + 1)
                normalise(e)
                k_part(e + 1)
                tokens(e)
                steps(BESIDE, e, e + 1)
                residual(e)
                attend(e + 1)
            add_last(B - 1)
            normalise(B - 1)
            tokens(B - 1)
            steps(ALONE1[:ROW1 + 1], B - 1, None)
            for k in range(DC):
                dve.wait_ge(w_ih_hi, k + 1)
                nc.vector.scalar_tensor_tensor(out=w_in[:, 1, k, :], in0=w_ih_f32[:, k, :], scalar=WS, in1=w_in[:, 0, k, :],
                                               op0=ALU.mult, op1=ALU.subtract).then_inc(w_ih_lo, 1)
            steps(ALONE1[ROW1 + 1:], B - 1, None)
            residual(B - 1)

        @block.gpsimd
        def _(pool):
            pair_of_rows = float(np.array([ROW, ROW], np.float16).view(np.float32)[0])
            nc.gpsimd.memset(v_aug[:, :, :, DH0:], 1.0).then_inc(c_later, 1)
            for tile, v in ((bemb_c, b_emb), (gn_c, g_norm)):
                pool.dma_start(tile[:, :], v.rearrange("(c p) -> p c", p=P), allow_slow_non_contiguous=True).then_inc(c_vec, 16)
            pool.wait_ge(c_later, 1)
            nc.gpsimd.memset(k_rep[96:97, :, :].bitcast(F32), pair_of_rows).then_inc(c_later, 1)
            pool.wait_ge(c_later, 2)
            nc.gpsimd.memset(max1_rows[:, :, :].bitcast(F32), 0.0).then_inc(c_later, 1)
            for j in range(4):
                for tile, v in ((gq, g_q), (gk, g_k)):
                    pool.dma_start(tile[32 * j:32 * j + 32, :], v.rearrange("(p a) -> p a", a=1)).then_inc(c_vec, 16)
            with pool.Fori(0, B) as b:
                pool.wait_ge(ld_x1, b * 16 + 16)
                for c in range(NC - 1):
                    for n in range(2):
                        pool.wait_ge(ld_y[n], b * 128 + 64 * (c + 1))
                    nc.gpsimd.tensor_tensor(x1[:, c, :], x1[:, c, :], y[:, c, :], ALU.add).then_inc(x1_ok, 1)


def recurrence(nc, sem, sb, W_ih, W_hh, b_ih, b_hh, Wk3, Wo3, pA, pB, pC, pD, xT, ident, condT, rep, w_ih, woT, block_sums,
               norm, norm_from):
    with ExitStack() as ctx:
        def t(name, shape, dt=F32):
            return sb(ctx, name, shape, dt)

        w_in, wi_lo = [w_ih[0][:, n, :, :] for n in range(2)], w_ih[3]
        w_part = rep[:, :, :, :].rearrange("p n h d -> p (n h d)")[:, 0:2 * DC * 3 * D].rearrange("p (s c n) -> p s c n", s=2, c=DC)
        w_part = [w_part[:, n, :, :] for n in range(2)]
        wkT = key_weights(rep)
        gi_rz = t("gi_rz", [P, N + 1, 2 * DC, B])
        gi_n = t("gi_n", [P, N + 1, DC, B])
        x_part = t("x_part", [P, 2, DC, B, TB], F16)
        bias_in = t("bias_in", [P, MC])
        bias_hn = t("bias_hn", [P, DC, B])
        state = [t(f"state{n}", [P, DC, B]) for n in range(2)]
        moving = t("moving", [P, DC, 2, B], F16)
        r_pre = t("r_pre", [P, DC, B])
        r_gate = t("r_gate", [P, DC, B])
        z_pre = t("z_pre", [P, DC, B])
        z_gate = t("z_gate", [P, DC, B])
        n_terms = t("n_terms", [P, DC, 3, B])
        n_pre = t("n_pre", [P, DC, B])
        cand = t("cand", [P, DC, B])
        z_old = t("z_old", [P, DC, B])
        z_new = t("z_new", [P, DC, B])
        unscaled = t("unscaled", [P, DC, B])
        unit = t("unit", [P, DC, B])
        bih_c = t("bih_c", [P, MC])
        tick = t("tick2", [P, 1])
        bhh_c = t("bhh_c", [P, MC])
        later = gi_rz[:, TB:N, :, :].rearrange("p t m b -> p (t m b)")
        staged = later[:, 0:DC * 3 * D].rearrange("p (c n) -> p c n", c=DC)
        wk, wo = (later[:, DC * (3 + n) * D:DC * (4 + n) * D].rearrange("p (c n) -> p c n", c=DC) for n in range(2))

        w_ld, b_ld, w_hi, w_lo, b_ok, h_ok, wko_ld, wT_ps, wT_ok, summed = (
            sem(n) for n in ("w_ld", "b_ld", "w_hi", "w_lo", "b_ok", "h_ok", "wko_ld", "wT_ps", "wT_ok", "summed"))
        x_hi, x_lo, gi_ps, gi_out, begun, seeded, zeros = (
            sem("gru_" + n) for n in ("x_hi", "x_lo", "gi_ps", "gi_out", "begun", "seeded", "zeros"))
        r_ps, n_ps, z_ps, r_sum, z_sum, r_ok, z_ok, n_mul, n_sum, n_ok, zh_ok, zn_ok, hi_done, st_ok, lo_done = (
            sem("gru_" + n) for n in ("r_ps", "n_ps", "z_ps", "r_sum", "z_sum", "r_ok", "z_ok", "n_mul", "n_sum", "n_ok", "zh_ok", "zn_ok", "hi_done", "st_ok",
                      "lo_done"))
        n_in, h_un, x_add, ticked = (sem("gru_" + n) for n in ("n_in", "h_un", "x_add", "ticked"))
        block = ctx.enter_context(nc.Block())
        CHUNKS = (range(0, 1), range(1, DC))
        SLICE = (slice(0, 1), slice(1, DC))
        pR = (pA[:, 0, 0:16], pA[:, 1, 0:48])
        pN = (pB[:, 0, 0:16], pB[:, 1, 0:48])
        pZ = (pC[:, 0, 0:16], pC[:, 1, 0:48])
        pG = [pD[:, 0, 0:B * TB], pD[:, 1, 0:B * TB]]
        BLOCKS = N // TB
        BODY = 2
        PLAIN = TB - MC * BODY
        RZ = 2 * DC
        W_HH_FROM = 3

        def halves(ps):
            return ps.rearrange("p (c s b) -> p c b s", s=2, b=B)

        def blocks(eng, step, split, product):
            with eng.Fori(0, BLOCKS - 1) as blk:
                with eng.Fori(0, PLAIN // BODY) as k:
                    for j in range(BODY):
                        step(blk * TB + k * BODY + j, j, blk, True)
                        if j == 0:
                            split(blk + 1, k)
                with eng.Fori(0, RZ) as m:
                    for j in range(BODY):
                        step(blk * TB + m * BODY + (PLAIN + j), j, blk)
                        product(blk + 1, m, j, False)
                with eng.Fori(RZ, MC) as m:
                    for j in range(BODY):
                        step(blk * TB + m * BODY + (PLAIN + j), j, blk)
                        product(blk + 1, m, j, True)
            with eng.Fori(0, TB // BODY) as k:
                for j in range(BODY):
                    step(k * BODY + (N - TB + j), j, BLOCKS - 1, True)

        @block.sync
        def _(sp):
            sp.dma_start(bih_c[:, :], b_ih.rearrange("(c p) -> p c", p=P), allow_slow_non_contiguous=True).then_inc(b_ld, 16)
            sp.dma_start(bhh_c[:, :], b_hh.rearrange("(c p) -> p c", p=P), allow_slow_non_contiguous=True).then_inc(b_ld, 16)
            sp.dma_start(staged, W_hh.rearrange("(c p) n -> p c n", p=P)).then_inc(w_ld, 16)
            for tile, w in ((wk, Wk3), (wo, Wo3)):
                sp.dma_start(tile, w.rearrange("(c p) n -> p c n", p=P)).then_inc(wko_ld, 16)
            *columns, gamma_bc, norm_ld = norm
            cond, rms_w, beta, gamma = norm_from
            for tile, row in zip(columns, (cond[1:2, :].rearrange("a n -> (a n)"), rms_w, beta)):
                sp.dma_start(tile[:, :], row.rearrange("(c p) -> p c", p=P), allow_slow_non_contiguous=True).then_inc(norm_ld, 16)
            sp.dma_start(gamma_bc[:, :], gamma.rearrange("(a n) -> a n", a=1).broadcast_to([P, D])).then_inc(norm_ld, 16)

        @block.tensor
        def _(pe):
            def products(m, k, bank):
                for w in range(2):
                    for part in range(2):
                        last = nc.tensor.matmul(bank, w_in[w][:, k, bass.ts(m, P)], x_part[:, part, k, :, :].rearrange("p b t -> p (b t)"),
                                                start=(k == 0 and w == 0 and part == 0), stop=(k == DC - 1 and w == 1 and part == 1))
                return last

            def step(step, j, blk, begins=False):
                pe.wait_ge(seeded, step * 6 + 5)

                def gate(ps, first, part, ks):
                    for c in CHUNKS[part]:
                        o = (c - CHUNKS[part][0]) * 2 * B
                        for k in ks:
                            for w in w_part:
                                last = nc.tensor.matmul(ps[part][:, o:o + 2 * B], w[:, k, (first + c) * P:(first + c) * P + P],
                                                        moving[:, k, :, :].rearrange("p s b -> p (s b)"), start=False,
                                                        stop=(k == DC - 1), skip_group_check=True)
                    return last

                pe.wait_ge(lo_done, step * 2 + 1)
                for ps, first in ((pR, 0), (pN, 2 * DC), (pZ, DC)):
                    for part in range(2):
                        if ps is pZ and part == 1:
                            pe.wait_ge(seeded, step * 6 + 6)
                        gate(ps, first, part, CHUNKS[0])
                pe.wait_ge(lo_done, step * 2 + 2)
                for part in range(2):
                    for ps, first, done in ((pR, 0, r_ps), (pN, 2 * DC, n_ps), (pZ, DC, z_ps)):
                        gate(ps, first, part, CHUNKS[1]).then_inc(done, 1)

            def nothing(*_):
                pass

            def product(blk, m, j, is_n):
                if j == 0:
                    pe.wait_ge(x_lo, blk * DC + DC)
                    pe.wait_ge(gi_out, blk * MC + m)
                for k in range(j * DC // BODY, (j + 1) * DC // BODY):
                    last = products(m, k, pG[0])
                if j == BODY - 1:
                    last.then_inc(gi_ps, 1)

            def first_products(m):
                if m >= 2:
                    pe.wait_ge(gi_out, m - 1)
                for k in range(DC):
                    if m == 0:
                        pe.wait_ge(x_lo, k + 1)
                    last = products(m, k, pG[m % 2])
                last.then_inc(gi_ps, 1)

            def transpose(n):
                w, bank = ((wk, pA), (wk, pB), (wo, pC), (wo, pA))[n]
                if n == 3:
                    pe.wait_ge(wT_ok, 1)
                for hf in range(2):
                    kc = 2 * (n % 2) + hf
                    for hc in range(DC):
                        last = nc.tensor.transpose(bank[:, hf, hc * P:hc * P + P], w[:, kc, hc * P:hc * P + P], ident[:, :])
                last.then_inc(wT_ps, 1)

            pe.wait_ge(wi_lo, DC)
            for m in range(RZ):
                first_products(m)
            pe.wait_ge(wko_ld, 32)
            for n in range(MC - RZ):
                transpose(n)
                first_products(RZ + n)
            pe.wait_ge(wT_ok, 4)
            pe.wait_ge(w_lo, DC)
            pe.wait_ge(lo_done, 2)
            for ps in (pR, pN, pZ):
                for part in range(2):
                    last = nc.tensor.matmul(ps[part], w_part[0][:, 0, 0:P], moving[:, SLICE[part], :, :].rearrange("p c s b -> p (c s b)"),
                                            start=True, stop=True)
            last.then_inc(begun, 1)
            blocks(pe, step, nothing, product)

        @block.scalar
        def _(act):
            for k in range(DC):
                nc.scalar.activation(x_part[:, 0, k, :, :], xT[:, k, :, 0:TB], ACT.Copy).then_inc(x_hi, 1)
            nc.scalar.preload_act_table_set("sigmoid_and_others")

            def seed(step, kind, part):
                c0, c1 = SLICE[part].start, SLICE[part].stop
                if kind == "n":
                    ps, src = pN, bias_hn[:, c0:c1, :]
                else:
                    first = DC if kind == "z" else 0
                    ps, src = pZ if kind == "z" else pR, gi_rz[:, bass.ds(step, 1), first + c0:first + c1, :].rearrange("p o c b -> p (o c) b")
                nc.scalar.activation(ps[part].rearrange("p (c s b) -> p c s b", s=2, b=B),
                                     src.unsqueeze(2).broadcast_to([P, c1 - c0, 2, B]), ACT.Copy).then_inc(seeded, 1)

            def step(step, j, blk, begins=False):
                def gate(kind, part):
                    src, dst, ready, done, func = {
                        "r": (r_pre, r_gate, r_sum, r_ok, ACT.Sigmoid), "z": (z_pre, z_gate, z_sum, z_ok, ACT.Sigmoid),
                        "n": (n_pre, cand, n_sum, n_ok, ACT.Tanh)}[kind]
                    act.wait_ge(ready, step * 2 + (part + 1))
                    nc.scalar.activation(dst[:, SLICE[part], :], src[:, SLICE[part], :], func, scale=1.0 / GS).then_inc(done, 1)

                gate("r", 0)
                gate("z", 0)
                seed(step + 1, "r", 0)
                gate("r", 1)
                gate("n", 0)
                seed(step + 1, "z", 0)
                seed(step + 1, "r", 1)
                seed(step + 1, "n", 0)
                act.wait_ge(n_mul, step * 2 + 2)
                seed(step + 1, "n", 1)
                gate("n", 1)
                gate("z", 1)
                seed(step + 1, "z", 1)

            def nothing(*_):
                pass

            def evacuate(blk, m, bank, is_n):
                act.wait_ge(gi_ps, blk * MC + m + 1)
                src = bank.rearrange("p (b t) -> p b t", b=B)
                if is_n:
                    dst, scale = gi_n[:, bass.ts(blk, TB), bass.ds(m - RZ, 1), :], GS / WS
                else:
                    dst, scale = gi_rz[:, bass.ts(blk, TB), bass.ds(m, 1), :], GS / 2 / WS
                nc.scalar.activation(dst.rearrange("p t o b -> p b (t o)"), src, ACT.Identity, bias=bias_in[:, bass.ds(m, 1)],
                                     scale=scale).then_inc(gi_out, 1)

            def product(blk, m, j, is_n):
                if j == BODY - 1:
                    if is_n:
                        act.wait_ge(gi_out, blk * MC + m)
                    evacuate(blk, m, pG[0], is_n)

            act.wait_ge(b_ok, 4)
            for m in range(MC):
                if W_HH_FROM <= m < W_HH_FROM + DC:
                    k = m - W_HH_FROM
                    if k == 0:
                        act.wait_ge(w_ld, 16)
                    nc.scalar.activation(w_part[0][:, k, :], staged[:, k, :], ACT.Copy, scale=WS).then_inc(w_hi, 1)
                evacuate(0, m, pG[m % 2], m >= RZ)
            act.wait_ge(begun, 1)
            act.wait_ge(gi_out, MC)
            act.wait_ge(zeros, 1)
            for kind in "rnz":
                for part in range(2):
                    seed(0, kind, part)
            blocks(act, step, nothing, product)

        @block.vector
        def _(dve):
            for k in range(DC):
                dve.wait_ge(x_hi, k + 1)
                nc.vector.tensor_tensor(x_part[:, 1, k, :, :], xT[:, k, :, 0:TB], x_part[:, 0, k, :, :], ALU.subtract).then_inc(x_lo, 1)
            dve.wait_ge(b_ld, 32)
            nc.vector.tensor_tensor(bias_in[:, 0:RZ], bih_c[:, 0:RZ], bhh_c[:, 0:RZ], ALU.add).then_inc(b_ok, 1)
            nc.vector.tensor_scalar(bias_in[:, RZ:], bih_c[:, RZ:], GS, None, ALU.mult).then_inc(b_ok, 1)
            nc.vector.tensor_scalar(bias_hn[:, :, :], bhh_c[:, RZ:].unsqueeze(2).broadcast_to([P, DC, B]), GS / 2, None, ALU.mult).then_inc(b_ok, 1)
            dve.wait_ge(b_ok, 3)
            nc.vector.tensor_scalar(bias_in[:, 0:RZ], bias_in[:, 0:RZ], GS / 2, None, ALU.mult).then_inc(b_ok, 1)
            nc.vector.tensor_scalar(state[1][:, :, :], condT[:, :, :], HS, None, ALU.mult).then_inc(h_ok, 1)
            for part in range(2):
                nc.vector.tensor_scalar(moving[:, SLICE[part], 0, :], condT[:, SLICE[part], :], HS, None, ALU.mult).then_inc(hi_done, 1)
            dve.wait_ge(h_ok, 1)
            for part in range(2):
                dve.wait_ge(hi_done, part + 1)
                nc.vector.tensor_tensor(moving[:, SLICE[part], 1, :], state[1][:, SLICE[part], :], moving[:, SLICE[part], 0, :],
                                        ALU.subtract).then_inc(lo_done, 1)
            for k in range(DC):
                dve.wait_ge(w_hi, k + 1)
                nc.vector.scalar_tensor_tensor(out=w_part[1][:, k, :], in0=staged[:, k, :], scalar=WS, in1=w_part[0][:, k, :],
                                               op0=ALU.mult, op1=ALU.subtract).then_inc(w_lo, 1)

            for n, (w, bank) in enumerate(((wkT, pA), (wkT, pB), (woT, pC), (woT, pA))):
                dve.wait_ge(wT_ps, n + 1)
                kc = 2 * (n % 2)
                nc.vector.tensor_copy(w[:, :, kc * P:kc * P + 2 * P].rearrange("p h (f k) -> p f h k", f=2),
                                      bank[:, :, :].rearrange("p f (h k) -> p f h k", h=DC)).then_inc(wT_ok, 1)

            def step(step, j, blk, begins=False):
                old, new = state[1 - j % 2], state[j % 2]

                def sum_r(part):
                    dve.wait_ge(r_ps, step * 2 + (part + 1))
                    nc.vector.tensor_reduce(r_pre[:, SLICE[part], :], halves(pR[part]), AX.X, ALU.add).then_inc(r_sum, 1)

                def sum_z(part):
                    dve.wait_ge(z_ps, step * 2 + (part + 1))
                    nc.vector.tensor_reduce(z_pre[:, SLICE[part], :], halves(pZ[part]), AX.X, ALU.add).then_inc(z_sum, 1)

                def mul_n(part):
                    dve.wait_ge(n_ps, step * 2 + (part + 1))
                    dve.wait_ge(r_ok, step * 2 + (part + 1))
                    nc.vector.tensor_tensor(n_terms[:, SLICE[part], 0:2, :], pN[part].rearrange("p (c s b) -> p c s b", s=2, b=B),
                                            r_gate[:, SLICE[part], :].unsqueeze(2).broadcast_to([P, len(CHUNKS[part]), 2, B]),
                                            ALU.mult).then_inc(n_mul, 1)

                def sum_n(part):
                    if part == 0:
                        dve.wait_ge(n_in, step + 1)
                    dve.wait_ge(n_mul, step * 2 + (part + 1))
                    nc.vector.tensor_reduce(n_pre[:, SLICE[part], :], n_terms[:, SLICE[part], :, :].rearrange("p c s b -> p c b s"), AX.X,
                                            ALU.add).then_inc(n_sum, 1)

                def kept(part):
                    dve.wait_ge(z_ok, step * 2 + (part + 1))
                    nc.vector.tensor_tensor(z_old[:, SLICE[part], :], z_gate[:, SLICE[part], :], old[:, SLICE[part], :], ALU.mult).then_inc(zh_ok, 1)

                def taken(part):
                    if part == 0:
                        dve.wait_ge(n_ok, step * 2 + 1)
                    nc.vector.scalar_tensor_tensor(out=z_new[:, SLICE[part], :], in0=z_gate[:, SLICE[part], :], scalar=1.0,
                                                   in1=cand[:, SLICE[part], :], op0=ALU.subtract, op1=ALU.mult).then_inc(zn_ok, 1)

                def new_state(part):
                    dve.wait_ge(zn_ok, step * 2 + (part + 1))
                    for out, done in ((moving[:, SLICE[part], 0, :], hi_done), (new[:, SLICE[part], :], st_ok)):
                        nc.vector.scalar_tensor_tensor(out=out, in0=z_new[:, SLICE[part], :], scalar=-HS, in1=z_old[:, SLICE[part], :],
                                                       op0=ALU.mult, op1=ALU.add).then_inc(done, 1)

                def lo_part(part):
                    dve.wait_ge(st_ok, step * 2 + (part + 1))
                    nc.vector.tensor_tensor(moving[:, SLICE[part], 1, :], new[:, SLICE[part], :], moving[:, SLICE[part], 0, :],
                                            ALU.subtract).then_inc(lo_done, 1)

                sum_r(0)
                dve.wait_ge(x_add, step + 1)
                sum_z(0)
                mul_n(0)
                sum_r(1)
                sum_n(0)
                kept(0)
                mul_n(1)
                taken(0)
                sum_n(1)
                sum_z(1)
                new_state(0)
                lo_part(0)
                kept(1)
                taken(1)
                new_state(1)
                lo_part(1)

            def nothing(*_):
                pass

            blocks(dve, step, nothing, nothing)

        @block.gpsimd
        def _(pool):
            def split(blk, k):
                src = xT[:, bass.ds(k, 1), :, bass.ts(blk, TB)].rearrange("p o b t -> p (o b) t")
                hi, lo = (x_part[:, n, bass.ds(k, 1), :, :].rearrange("p o b t -> p (o b) t") for n in range(2))
                nc.gpsimd.tensor_copy(hi, src).then_inc(x_hi, 1)
                pool.wait_ge(x_hi, blk * DC + k + 1)
                nc.gpsimd.tensor_tensor(lo, src, hi, ALU.subtract).then_inc(x_lo, 1)

            def input_n(step):
                nc.gpsimd.tensor_copy(n_terms[:, :, 2, :], gi_n[:, bass.ds(step, 1), :, :].rearrange("p o c b -> p (o c) b")).then_inc(n_in, 1)

            def step(step, j, blk, begins=False):
                pool.wait_ge(lo_done, step * 2 + 4)
                input_n(step + 1)
                pool.wait_ge(x_add, step + 2)
                nc.gpsimd.tensor_tensor(unscaled[:, :, :], state[j % 2][:, :, :], unit[:, :, :], ALU.mult).then_inc(h_un, 1)
                pool.wait_ge(h_un, step + 1)
                xt = xT[:, :, :, bass.ds(step, 1)].rearrange("p c b o -> p c (b o)")
                nc.gpsimd.tensor_tensor(xt, xt, unscaled[:, :, :], ALU.add).then_inc(x_add, 1)
                pool.wait_ge(x_add, step + 3)
                pool.wait_ge(summed, step + 1)
                nc.gpsimd.tensor_tensor(tick[:, :], unit[:, 0, 0:1], unit[:, 0, 0:1], ALU.mult).then_inc(ticked, 1)
                total = block_sums[:, :, :, bass.ds(blk, 1)].rearrange("p c b o -> p c (b o)")
                nc.gpsimd.tensor_tensor(total, total, xt, ALU.add).then_inc(summed, 1)

            def product(blk, m, j, is_n):
                if j == BODY - 2 and is_n:
                    pool.wait_ge(gi_out, blk * MC + m + 1)

            nc.gpsimd.memset(block_sums[:, :, :, :], 0.0).then_inc(summed, 1)
            nc.gpsimd.memset(unit[:, :, :], 1.0 / HS).then_inc(x_add, 1)
            nc.gpsimd.memset(gi_n[:, N:, :, :], 0.0).then_inc(x_add, 1)
            nc.gpsimd.memset(gi_rz[:, N:, :, :], 0.0).then_inc(zeros, 1)
            pool.wait_ge(gi_out, MC)
            input_n(0)
            blocks(pool, step, split, product)


def block_attention(nc, sem, sb, out, pA, pB, pC, pD, xT, ident, wkT, woT, block_sums, norm, w_in):
    R = B * NB
    query_c, rms_c, beta_c, gamma_bc, norm_ld = norm
    with ExitStack() as ctx:
        def t(name, shape, dt=F32):
            return sb(ctx, name, shape, dt)

        query = t("query", [P, DC])
        ones = t("ones", [P, P])
        eps_d = t("eps_d3", [P, 1])
        eps_1 = t("eps_1", [P, 1])
        tick = t("tick3", [P, 2 * NC])
        key_sq = t("key_sq", [P, DC, 2, R])
        key_rstd = t("key_rstd", [P, R])
        score = t("score", [P, B, NB])
        smax = t("smax", [P, B])
        sden = t("sden", [P, B])
        block_proj = t("block_proj", [P, DC, R])
        weighted = t("weighted", [P, DC, B, NB])
        projT = t("projT", [P, DC, B])
        xp = t("xp", [P, DC, B, N])
        xb = t("xb", [P, DC, B, N])
        stats = [t(f"stats{n}", [P, NC, 6]) for n in range(2)]
        mv = [t(f"mv{n}", [P, NC, 2]) for n in range(2)]
        ln_rstd = [t(f"ln_rstd{n}", [P, NC]) for n in range(2)]
        ln_shift = [t(f"ln_shift{n}", [P, NC]) for n in range(2)]
        places = w_in[:, :, :, :].rearrange("p s c n -> p (s c n)").bitcast(F32)
        places = [places[:, n * NC * D:(n + 1) * NC * D].rearrange("p (c d) -> p c d", c=NC) for n in range(4)]
        ln, ln_g = places[0:2], places[2:4]
        res = t("res", [P, B, NC, D])

        ones_ok, qw_ok, key_ps, sq_ok, dot_ok, sum_ps, rs_ok, sm, bp_ps, bp_ok, wt_ok, pj_ok, xb_act, xb_dve, xp_dve, xp_act, xp_pool = (
            sem("blk_" + n) for n in ("ones", "qw", "key_ps", "sq", "dot", "sum_ps", "rs", "sm", "bp_ps", "bp", "wt", "pj",
                                      "xb_act", "xb_dve", "xp_dve", "xp_act", "xp_pool"))
        y_ps, xb_ps, st_ok, mv_ok, log_ok, rstd_ok, shift_ok, ln_ok, g_ok, res_ok, stored, ticked = (
            sem("norm_" + n) for n in ("y_ps", "xb_ps", "st", "mv", "log", "rstd", "shift", "ln", "g", "res", "stored", "ticked"))
        block = ctx.enter_context(nc.Block())
        banks = ((pA, pB), (pC, pD))
        XP = ((range(0, 2), xp_dve), (range(2, 5), xp_act), (range(5, B), xp_pool))
        XB_ACT = DC // 2
        LAST = B // 2 - 1

        @block.sync
        def _(sp):
            with sp.Fori(0, B) as b:
                for tc in range(NC):
                    sp.wait_ge(res_ok, b * NC + (tc + 1))
                    sp.dma_start(out[bass.ds(b, 1), tc * P:tc * P + P, :].rearrange("o p d -> p (o d)"),
                                 res[:, bass.ds(b, 1), tc, :].rearrange("p o d -> p (o d)")).then_inc(stored, 16)
            sp.wait_ge(stored, 16 * B * NC)

        @block.tensor
        def _(pe):
            sumsT = [block_sums[:, c, :, :].rearrange("p b n -> p (b n)") for c in range(DC)]
            for kc in range(DC):
                for c in range(DC):
                    last = nc.tensor.matmul(pB[:, kc // 2, (kc % 2) * R:(kc % 2) * R + R], wkT[:, c, kc * P:kc * P + P], sumsT[c],
                                            start=(kc % 2 == 0 and c == 0), stop=(c == DC - 1), skip_group_check=True)
                if kc % 2 == 1:
                    last.then_inc(key_ps, 1)
            def project_sums(kc):
                for c in range(DC):
                    last = nc.tensor.matmul(pC[:, 0, kc * R:kc * R + R], woT[:, c, kc * P:kc * P + P], sumsT[c],
                                            start=(kc == 0 and c == 0), stop=(c == DC - 1), skip_group_check=True)
                return last

            project_sums(0)
            pe.wait_ge(sq_ok, 2)
            pe.wait_ge(dot_ok, 2)
            pe.wait_ge(ones_ok, 3)
            for c in range(DC):
                last = nc.tensor.matmul(pA[:, 0, 0:2 * R], ones[:, :], key_sq[:, c, :, :].rearrange("p s r -> p (s r)"),
                                        start=(c == 0), stop=(c == DC - 1))
            last.then_inc(sum_ps, 1)
            for kc in range(1, DC):
                last = project_sums(kc)
            last.then_inc(bp_ps, 1)

            def tile_of(src, bank, b, tc):
                for c in range(DC):
                    last = nc.tensor.transpose(bank[:, tc, c * P:c * P + P], src[:, c, b, tc * P:tc * P + P], ident[:, :])
                return last

            def projected(b):
                for elements, done in XP:
                    if b in elements:
                        pe.wait_ge(done, (b + 1 - elements[0]) * DC)

            pe.wait_ge(xb_act, XB_ACT)
            pe.wait_ge(xb_dve, DC - XB_ACT)
            def with_beta(b):
                for tc in range(NC):
                    if b >= 2:
                        pe.wait_ge(res_ok, b * NC + tc - 3)
                    tile_of(xb, banks[b % 2][1], b, tc).then_inc(xb_ps, 1)

            for b in range(2):
                with_beta(b)
            pe.wait_ge(sm, 2)
            pe.wait_ge(bp_ok, 1)
            def with_projection(b):
                projected(b)
                for tc in range(NC):
                    if b >= 2:
                        pe.wait_ge(ln_ok, b * NC + tc - 3)
                    tile_of(xp, banks[b % 2][0], b, tc).then_inc(y_ps, 1)

            for b in range(B):
                with_projection(b)
                if b >= 3:
                    with_beta(b - 1)
            with_beta(B - 1)

        @block.scalar
        def _(act):
            nc.scalar.preload_act_table_set("natural_log_exp_and_others")
            for n in range(2):
                act.wait_ge(key_ps, n + 1)
                nc.scalar.activation(key_sq[:, 2 * n:2 * n + 2, 0, :], pB[:, n, 0:2 * R].rearrange("p (c r) -> p c r", c=2), ACT.Square).then_inc(sq_ok, 1)
            act.wait_ge(norm_ld, 64)
            for c in range(XB_ACT):
                if c == 1:
                    act.wait_ge(sum_ps, 1)
                    nc.scalar.activation(key_rstd[:, :], pA[:, 0, 0:R], ACT.Ln, bias=eps_d[:, 0:1]).then_inc(rs_ok, 1)
                    act.wait_ge(rs_ok, 1)
                    nc.scalar.activation(key_rstd[:, :], key_rstd[:, :], ACT.Exp, scale=-0.5).then_inc(rs_ok, 1)
                    act.wait_ge(bp_ps, 1)
                    nc.scalar.activation(block_proj[:, :, :], pC[:, 0, 0:DC * R].rearrange("p (c r) -> p c r", c=DC), ACT.Copy).then_inc(bp_ok, 1)
                    act.wait_ge(sm, 3)
                    nc.scalar.activation(score[:, :, :], score[:, :, :], ACT.Exp).then_inc(sm, 1)
                nc.scalar.activation(xb[:, c, :, :], xT[:, c, :, :], ACT.Identity, bias=beta_c[:, c:c + 1]).then_inc(xb_act, 1)
            act.wait_ge(pj_ok, 1)
            for b in XP[1][0]:
                for c in range(DC):
                    nc.scalar.activation(xp[:, c, b, :], xT[:, c, b, :], ACT.Identity, bias=projT[:, c, b:b + 1]).then_inc(xp_act, 1)
            with act.Fori(0, B // 2) as i:
                for n in range(2):
                    act.wait_ge(mv_ok, i * 2 * NC + (n + 1) * NC)
                    nc.scalar.activation(ln_rstd[n][:, :], mv[n][:, :, 1:2].rearrange("p c o -> p (c o)"), ACT.Ln, bias=eps_1[:, 0:1]).then_inc(log_ok, 1)
                    act.wait_ge(log_ok, i * 2 + (n + 1))
                    nc.scalar.activation(ln_rstd[n][:, :], ln_rstd[n][:, :], ACT.Exp, scale=-0.5).then_inc(rstd_ok, 1)
                    act.wait_ge(shift_ok, i * 2 + (n + 1))
                    for tc in range(NC):
                        nc.scalar.activation(ln[n][:, tc, :], banks[n][0][:, tc, :], ACT.Identity, bias=ln_shift[n][:, tc:tc + 1],
                                             scale=ln_rstd[n][:, tc:tc + 1]).then_inc(ln_ok, 1)

        @block.vector
        def _(dve):
            nc.vector.memset(ones[:, :], 1.0).then_inc(ones_ok, 1)
            nc.vector.memset(eps_d[:, :], D * EPS).then_inc(ones_ok, 1)
            nc.vector.memset(eps_1[:, :], EPS).then_inc(ones_ok, 1)
            dve.wait_ge(norm_ld, 64)
            nc.vector.tensor_tensor(query[:, :], query_c[:, :], rms_c[:, :], ALU.mult).then_inc(qw_ok, 1)
            dve.wait_ge(qw_ok, 1)
            for n in range(2):
                dve.wait_ge(sq_ok, n + 1)
                nc.vector.tensor_tensor(key_sq[:, 2 * n:2 * n + 2, 1, :], pB[:, n, 0:2 * R].rearrange("p (c r) -> p c r", c=2),
                                        query[:, 2 * n:2 * n + 2].unsqueeze(2).broadcast_to([P, 2, R]), ALU.mult).then_inc(dot_ok, 1)
            for c in range(XB_ACT, DC):
                if c == DC - 1:
                    dve.wait_ge(rs_ok, 2)
                    nc.vector.scalar_tensor_tensor(out=score[:, :, :], in0=pA[:, 0, R:2 * R].rearrange("p (b n) -> p b n", b=B), scalar=D ** 0.5,
                                                   in1=key_rstd[:, :].rearrange("p (b n) -> p b n", b=B), op0=ALU.mult, op1=ALU.mult).then_inc(sm, 1)
                    dve.wait_ge(sm, 1)
                    nc.vector.tensor_reduce(smax[:, :], score[:, :, :], AX.X, ALU.max).then_inc(sm, 1)
                    dve.wait_ge(sm, 2)
                    nc.vector.tensor_tensor(score[:, :, :], score[:, :, :], smax[:, :].unsqueeze(2).broadcast_to([P, B, NB]), ALU.subtract).then_inc(sm, 1)
                nc.vector.tensor_scalar(xb[:, c, :, :], xT[:, c, :, :], beta_c[:, c:c + 1], None, ALU.add).then_inc(xb_dve, 1)
            dve.wait_ge(sm, 4)
            nc.vector.tensor_reduce(sden[:, :], score[:, :, :], AX.X, ALU.add).then_inc(sm, 1)
            dve.wait_ge(sm, 5)
            nc.vector.reciprocal(sden[:, :], sden[:, :]).then_inc(sm, 1)
            dve.wait_ge(sm, 6)
            nc.vector.tensor_tensor(score[:, :, :], score[:, :, :], sden[:, :].unsqueeze(2).broadcast_to([P, B, NB]), ALU.mult).then_inc(sm, 1)
            dve.wait_ge(bp_ok, 1)
            dve.wait_ge(sm, 7)
            nc.vector.tensor_tensor(weighted[:, :, :, :].rearrange("p c b n -> p c (b n)"), block_proj[:, :, :],
                                    score[:, :, :].rearrange("p b n -> p (b n)").unsqueeze(1).broadcast_to([P, DC, R]), ALU.mult).then_inc(wt_ok, 1)
            dve.wait_ge(wt_ok, 1)
            nc.vector.tensor_reduce(projT[:, :, :], weighted[:, :, :, :], AX.X, ALU.add).then_inc(pj_ok, 1)
            dve.wait_ge(pj_ok, 1)
            for b in XP[0][0]:
                for c in range(DC):
                    nc.vector.tensor_scalar(xp[:, c, b, :], xT[:, c, b, :], projT[:, c, b:b + 1], None, ALU.add).then_inc(xp_dve, 1)

            def statistics(i, n):
                for tc in range(NC):
                    dve.wait_ge(y_ps, i * 2 * NC + (n * NC + tc + 1))
                    nc.vector.bn_stats(stats[n][:, tc, :], banks[n][0][:, tc, :]).then_inc(st_ok, 1)
                for tc in range(NC):
                    dve.wait_ge(st_ok, i * 2 * NC + (n * NC + tc + 1))
                    nc.vector.memset(tick[:, n * NC + tc:n * NC + tc + 1], 0.0).then_inc(ticked, 1)
                    nc.vector.bn_aggr(mv[n][:, tc, :], stats[n][:, tc, :]).then_inc(mv_ok, 1)

            def shift(i, n):
                dve.wait_ge(rstd_ok, i * 2 + (n + 1))
                nc.vector.scalar_tensor_tensor(out=ln_shift[n][:, :], in0=mv[n][:, :, 0:1].rearrange("p c o -> p (c o)"), scalar=-1.0,
                                               in1=ln_rstd[n][:, :], op0=ALU.mult, op1=ALU.mult).then_inc(shift_ok, 1)

            def result(i, n):
                for tc in range(NC):
                    if tc == 0:
                        dve.wait_ge(xb_ps, i * 2 * NC + (n * NC + NC))
                    dve.wait_ge(g_ok, i * 2 * NC + (n * NC + tc + 1))
                    nc.vector.tensor_tensor(res[:, bass.ds(i * 2 + n, 1), tc, :].rearrange("p o d -> p (o d)"), banks[n][1][:, tc, :],
                                            ln_g[n][:, tc, :], ALU.add).then_inc(res_ok, 1)

            for n in range(2):
                statistics(0, n)
                shift(0, n)
            with dve.Fori(0, LAST) as i:
                for n in range(2):
                    statistics(i + 1, n)
                    result(i, n)
                    shift(i + 1, n)
            for n in range(2):
                result(LAST, n)

        @block.gpsimd
        def _(pool):
            pool.wait_ge(pj_ok, 1)
            for b in XP[2][0]:
                for c in range(DC):
                    nc.gpsimd.tensor_tensor(xp[:, c, b, :], xT[:, c, b, :], projT[:, c, b:b + 1].broadcast_to([P, N]), ALU.add).then_inc(xp_pool, 1)
            with pool.Fori(0, B // 2) as i:
                for n in range(2):
                    for tc in range(NC):
                        pool.wait_ge(ln_ok, i * 2 * NC + (n * NC + tc + 1))
                        nc.gpsimd.tensor_tensor(ln_g[n][:, tc, :], ln[n][:, tc, :], gamma_bc[:, :], ALU.mult).then_inc(g_ok, 1)


_INS = ['x', 'cond_2048', 'L0_cond_Wq', 'L0_cond_Wk', 'L0_cond_Wv', 'L0_cond_b', 'L1_cond_W_emb', 'L1_cond_b_emb', 'L1_cond_g_norm',
        'L1_cond_W_qkv', 'L1_cond_g_q', 'L1_cond_g_k', 'L1_cond_W_out', 'L2_cond_W_ih', 'L2_cond_W_hh', 'L2_cond_b_ih', 'L2_cond_b_hh',
        'L3_cond_rms_weight', 'L3_cond_Wk', 'L3_cond_Wo', 'L3_cond_ln_gamma', 'L3_cond_ln_beta']


def kernel(**inputs):
    import numpy as _np
    import concourse.bacc as _bacc
    from concourse import mybir as _mybir
    from concourse.bass_utils import run_bass_kernel_spmd as _run

    nc = _bacc.Bacc("TRN2", target_bir_lowering=False, num_devices=1)
    arrays, args = {}, []
    for name in _INS:
        a = _np.ascontiguousarray(inputs[name])
        arrays[f"in_{name}_dram"] = a
        args.append(nc.dram_tensor(f"in_{name}_dram", a.shape, _mybir.dt.from_np(a.dtype), kind="ExternalInput").ap())
    args.append(nc.dram_tensor("out_0_dram", (B, N, D), F32, kind="ExternalOutput").ap())
    build(nc, *args)
    r = _run(nc, [arrays], core_ids=[0])
    return r.results[0]["out_0_dram"]
```
